# Optimizing a Trainium2 kernel written in Bass

```python
import numpy as np
import jax
import jax.numpy as jnp

def _softmax(x, axis=-1):
    return jax.nn.softmax(x, axis=axis)

def _gelu(x):
    return jax.nn.gelu(x, approximate=True)

def _silu(x):
    return jax.nn.silu(x)

def _sigmoid(x):
    return jax.nn.sigmoid(x)

def _layernorm(x, axis=-1, eps=1e-05):
    m = jnp.mean(x, axis=axis, keepdims=True)
    v = jnp.var(x, axis=axis, keepdims=True)
    return (x - m) / jnp.sqrt(v + eps)

def _scatter_add(tgt, idx, src, axis=0):
    return tgt.at[idx].add(src)

def _segment_sum(src, seg, n):
    return jax.ops.segment_sum(src, seg, n)
kernel_name = 'mk_gnn_preln_d4_gnn_r64_dad785'

def setup_inputs(seed: int=0):
    np.random.seed(seed)
    _w = jnp.asarray

    def _rec_inputs():
        import jax
        import jax.numpy as jnp
        _gk = jax.random.key(seed)
        x = -0.0005121 + 1.001 * jax.random.normal(jax.random.fold_in(_gk, 1), (100000, 32), jnp.float32)
        src = jax.random.randint(jax.random.fold_in(_gk, 2), (50000,), 0, 100000, jnp.int32)
        dst = jnp.minimum((100000 * jax.random.uniform(jax.random.fold_in(_gk, 3), (50000,)) ** 2.0).astype(jnp.int32), 99999)
        _o = jnp.argsort(dst, stable=True)
        src = src[_o]
        dst = dst[_o]
        edge_attr3_2x32 = -8.16379e-05 + 0.999858 * jax.random.normal(jax.random.fold_in(_gk, 12), (50000, 2, 32), jnp.float32)
        return (x, src, dst, edge_attr3_2x32)
    x, src, dst, edge_attr3_2x32 = _rec_inputs()

    def _L0_gnn_setup():
        import jax, jax.numpy as jnp
        import numpy as np
        import math
        N_NODES = 100000
        N_EDGES = 25000
        IN_DIM = 32
        OUT_DIM = 32
        key = jax.random.key(seed)
        k1, k2, k3, k4 = jax.random.split(key, 4)
        X = jax.random.normal(k1, (N_NODES, IN_DIM), dtype=jnp.float32)
        src_idx = jax.random.randint(k2, (N_EDGES,), 0, N_NODES, dtype=jnp.int64)
        dst_idx = jax.random.randint(k3, (N_EDGES,), 0, N_NODES, dtype=jnp.int64)
        stdv = 1.0 / math.sqrt(OUT_DIM)
        W = jax.random.uniform(k4, (IN_DIM, OUT_DIM), dtype=jnp.float32, minval=-stdv, maxval=stdv)
        return {'X': X, 'W': W, 'src_idx': src_idx, 'dst_idx': dst_idx}
    _L0_gnn_all = _L0_gnn_setup()
    _L0_gnn_in = {k: v for k, v in _L0_gnn_all.items() if k in ('W',)}
    del _L0_gnn_all

    def _L1_gnn_setup():
        import jax, jax.numpy as jnp
        import numpy as np
        N = 50000
        E = 25000
        H = 2
        F = 32
        IN = 32
        OUT = 32
        NEG_SLOPE = 0.2
        key = jax.random.key(seed)
        ks = jax.random.split(key, 11)
        s = 0.1
        return {'feat': jax.random.normal(ks[0], (N, IN), jnp.float32), 'r_feat': jax.random.normal(ks[1], (E, H, F), jnp.float32), 'src': jax.random.randint(ks[2], (E,), 0, N), 'dst': jax.random.randint(ks[3], (E,), 0, N), 'W1': jax.random.normal(ks[4], (IN, OUT), jnp.float32) * s, 'b1': jnp.zeros((OUT,), jnp.float32), 'W2s': jax.random.normal(ks[5], (IN, H * F), jnp.float32) * s, 'b2s': jnp.zeros((H * F,), jnp.float32), 'W2d': jax.random.normal(ks[6], (IN, H * F), jnp.float32) * s, 'b2d': jnp.zeros((H * F,), jnp.float32), 'attn': jax.random.normal(ks[7], (1, H, F), jnp.float32) * s}
    _L1_gnn_all = _L1_gnn_setup()
    _L1_gnn_in = {k: v for k, v in _L1_gnn_all.items() if k in ('W1', 'b1', 'W2s', 'b2s', 'W2d', 'b2d', 'attn')}
    del _L1_gnn_all

    def _L2_gnn_setup():
        import jax, jax.numpy as jnp
        import numpy as np
        N = 100000
        E = 25000
        IN_C, HID, OUT_C = (32, 64, 32)

        def _mean_aggregate(x, src, dst, num_nodes):
            summed = jax.ops.segment_sum(x[src], dst, num_segments=num_nodes)
            deg = jax.ops.segment_sum(jnp.ones((src.shape[0],), x.dtype), dst, num_segments=num_nodes)
            return summed / jnp.maximum(deg, 1.0)[:, None]

        def _sage_conv(x, src, dst, W_l, b, W_r):
            agg = _mean_aggregate(x, src, dst, x.shape[0])
            return agg @ W_l + b + x @ W_r
        key = jax.random.key(seed)
        ks = jax.random.split(key, 8)
        x = jax.random.normal(ks[0], (N, IN_C), dtype=jnp.float32)
        edge_index = jax.random.randint(ks[1], (2, E), 0, N, dtype=jnp.int64)
        s1 = 1.0 / np.sqrt(IN_C)
        s2 = 1.0 / np.sqrt(HID)
        W1_l = jax.random.uniform(ks[2], (IN_C, HID), jnp.float32, -s1, s1)
        b1 = jnp.zeros((HID,), jnp.float32)
        W1_r = jax.random.uniform(ks[3], (IN_C, HID), jnp.float32, -s1, s1)
        W2_l = jax.random.uniform(ks[4], (HID, OUT_C), jnp.float32, -s2, s2)
        b2 = jnp.zeros((OUT_C,), jnp.float32)
        W2_r = jax.random.uniform(ks[5], (HID, OUT_C), jnp.float32, -s2, s2)
        return {'x': x, 'edge_index': edge_index, 'W1_l': W1_l, 'b1': b1, 'W1_r': W1_r, 'W2_l': W2_l, 'b2': b2, 'W2_r': W2_r}
    _L2_gnn_all = _L2_gnn_setup()
    _L2_gnn_in = {k: v for k, v in _L2_gnn_all.items() if k in ('W1_l', 'b1', 'W1_r', 'W2_l', 'b2', 'W2_r')}
    del _L2_gnn_all

    def _L3_gnn_setup():
        import jax, jax.numpy as jnp
        import numpy as np
        N_NODES = 100000
        N_EDGES = 25000
        IN_FEATS = 32
        OUT_FEATS = 32
        key = jax.random.key(seed)
        k1, k2, k3, k4, k5 = jax.random.split(key, 5)
        feature = jax.random.normal(k1, (N_NODES, IN_FEATS), dtype=jnp.float32)
        src = jax.random.randint(k2, (N_EDGES,), 0, N_NODES, dtype=jnp.int64)
        dst = jax.random.randint(k3, (N_EDGES,), 0, N_NODES, dtype=jnp.int64)
        dst = jnp.where(dst == src, (dst + 1) % N_NODES, dst)
        W = jax.random.normal(k4, (OUT_FEATS, IN_FEATS), dtype=jnp.float32) / np.sqrt(IN_FEATS)
        bias = jnp.zeros((OUT_FEATS,), dtype=jnp.float32)
        return {'feature': feature, 'src': src, 'dst': dst, 'W': W, 'bias': bias}
    _L3_gnn_all = _L3_gnn_setup()
    _L3_gnn_in = {k: v for k, v in _L3_gnn_all.items() if k in ('W', 'bias')}
    del _L3_gnn_all
    return {'x': x, 'src': src, 'dst': dst, 'edge_attr3_2x32': edge_attr3_2x32, 'L0_gnn_W': _L0_gnn_in['W'], 'L1_gnn_W1': _L1_gnn_in['W1'], 'L1_gnn_b1': _L1_gnn_in['b1'], 'L1_gnn_W2s': _L1_gnn_in['W2s'], 'L1_gnn_b2s': _L1_gnn_in['b2s'], 'L1_gnn_W2d': _L1_gnn_in['W2d'], 'L1_gnn_b2d': _L1_gnn_in['b2d'], 'L1_gnn_attn': _L1_gnn_in['attn'], 'L2_gnn_W1_l': _L2_gnn_in['W1_l'], 'L2_gnn_b1': _L2_gnn_in['b1'], 'L2_gnn_W1_r': _L2_gnn_in['W1_r'], 'L2_gnn_W2_l': _L2_gnn_in['W2_l'], 'L2_gnn_b2': _L2_gnn_in['b2'], 'L2_gnn_W2_r': _L2_gnn_in['W2_r'], 'L3_gnn_W': _L3_gnn_in['W'], 'L3_gnn_bias': _L3_gnn_in['bias']}

def reference(x, src, dst, edge_attr3_2x32, L0_gnn_W, L1_gnn_W1, L1_gnn_b1, L1_gnn_W2s, L1_gnn_b2s, L1_gnn_W2d, L1_gnn_b2d, L1_gnn_attn, L2_gnn_W1_l, L2_gnn_b1, L2_gnn_W1_r, L2_gnn_W2_l, L2_gnn_b2, L2_gnn_W2_r, L3_gnn_W, L3_gnn_bias):
    import jax
    import jax.numpy as jnp

    def _L0_gnn_ref(X, W, src_idx, dst_idx):
        import jax, jax.numpy as jnp
        import numpy as np
        import math
        N_NODES = 100000
        N_EDGES = 25000
        IN_DIM = 32
        OUT_DIM = 32
        agg = jax.ops.segment_sum(X[src_idx], dst_idx, num_segments=N_NODES)
        return agg @ W

    def _L1_gnn_ref(feat, r_feat, src, dst, W1, b1, W2s, b2s, W2d, b2d, attn):
        import jax, jax.numpy as jnp
        import numpy as np
        N = 50000
        E = 25000
        H = 2
        F = 32
        IN = 32
        OUT = 32
        NEG_SLOPE = 0.2
        n = feat.shape[0]
        feat_src = (feat @ W2s + b2s).reshape(n, H, F)
        feat_dst = (feat @ W2d + b2d).reshape(n, H, F)
        en = feat_src[src]
        ev = feat_dst[dst]
        e = jax.nn.leaky_relu(en + ev, negative_slope=NEG_SLOPE)
        e = jnp.sum(e * attn, axis=-1, keepdims=True)
        m = jax.ops.segment_max(e, dst, num_segments=n)
        m = jnp.where(jnp.isfinite(m), m, 0.0)
        ee = jnp.exp(e - m[dst])
        denom = jax.ops.segment_sum(ee, dst, num_segments=n)
        alpha = ee / jnp.maximum(denom[dst], 1e-09)
        msg = jax.nn.softmax(en * r_feat * alpha, axis=-1)
        g_agg = jax.ops.segment_sum(msg, dst, num_segments=n)
        g_sum = jnp.sum(g_agg, axis=1)
        rst = (feat + g_sum) @ W1 + b1
        return rst

    def _L2_gnn_ref(x, edge_index, W1_l, b1, W1_r, W2_l, b2, W2_r):
        import jax, jax.numpy as jnp
        import numpy as np
        N = 100000
        E = 25000
        IN_C, HID, OUT_C = (32, 64, 32)

        def _mean_aggregate(x, src, dst, num_nodes):
            summed = jax.ops.segment_sum(x[src], dst, num_segments=num_nodes)
            deg = jax.ops.segment_sum(jnp.ones((src.shape[0],), x.dtype), dst, num_segments=num_nodes)
            return summed / jnp.maximum(deg, 1.0)[:, None]

        def _sage_conv(x, src, dst, W_l, b, W_r):
            agg = _mean_aggregate(x, src, dst, x.shape[0])
            return agg @ W_l + b + x @ W_r
        src, dst = (edge_index[0], edge_index[1])
        h = jax.nn.relu(_sage_conv(x, src, dst, W1_l, b1, W1_r))
        return _sage_conv(h, src, dst, W2_l, b2, W2_r)

    def _L3_gnn_ref(feature, src, dst, W, bias):
        import jax, jax.numpy as jnp
        import numpy as np
        N_NODES = 100000
        N_EDGES = 25000
        IN_FEATS = 32
        OUT_FEATS = 32
        n = feature.shape[0]
        loops = jnp.arange(n, dtype=src.dtype)
        src_all = jnp.concatenate([src, loops])
        dst_all = jnp.concatenate([dst, loops])
        deg = jax.ops.segment_sum(jnp.ones_like(dst_all, dtype=feature.dtype), dst_all, num_segments=n)
        deg = jnp.maximum(deg, 1.0)[:, None]
        inv_sqrt_deg = jax.lax.rsqrt(deg)
        h = jnp.einsum('ni,oi->no', feature * inv_sqrt_deg, W)
        agg = jax.ops.segment_sum(h[src_all], dst_all, num_segments=n)
        out = jax.nn.relu(agg * inv_sqrt_deg + bias)
        return out
    edge_index = jnp.stack([src, dst])
    h = jnp.maximum(_layernorm(x, axis=-1), 0.0)
    x = x + _L0_gnn_ref(h, L0_gnn_W, src, dst)
    h = jnp.maximum(_layernorm(x, axis=-1), 0.0)
    x = x + _L1_gnn_ref(h, edge_attr3_2x32, src, dst, L1_gnn_W1, L1_gnn_b1, L1_gnn_W2s, L1_gnn_b2s, L1_gnn_W2d, L1_gnn_b2d, L1_gnn_attn)
    h = jnp.maximum(_layernorm(x, axis=-1), 0.0)
    x = x + _L2_gnn_ref(h, edge_index, L2_gnn_W1_l, L2_gnn_b1, L2_gnn_W1_r, L2_gnn_W2_l, L2_gnn_b2, L2_gnn_W2_r)
    h = jnp.maximum(_layernorm(x, axis=-1), 0.0)
    x = x + _L3_gnn_ref(h, src, dst, L3_gnn_W, L3_gnn_bias)
    return x

_drawn_inputs = setup_inputs


def setup_inputs(seed=0):
    import zlib

    import numpy as np

    out = dict(_drawn_inputs(seed))
    spreads = {'L1_gnn_b1': (0.0, 0.1),
     'L1_gnn_b2s': (0.0, 0.8),
     'L1_gnn_b2d': (0.0, 0.8),
     'L2_gnn_b1': (0.0, 0.1),
     'L2_gnn_b2': (0.0, 0.1),
     'L3_gnn_bias': (0.0, 0.1)}
    factors = {'edge_attr3_2x32': 8.0, 'L1_gnn_W2s': 8.0, 'L1_gnn_W2d': 8.0, 'L1_gnn_attn': 8.0}
    for name, (base, spread) in spreads.items():
        noise = np.random.default_rng([zlib.crc32(name.encode()), seed]).standard_normal(out[name].shape)
        drawn = base * np.exp(spread * noise) if base else spread * noise
        out[name] = jnp.asarray(drawn.astype(out[name].dtype))
    for name, factor in factors.items():
        out[name] = (out[name] * factor).astype(out[name].dtype)
    return out
```

```python
import numpy as np
from contextlib import ExitStack

import concourse.bass as bass
from concourse import mybir

F32 = mybir.dt.float32
BF16 = mybir.dt.bfloat16
I32 = mybir.dt.int32
U32 = mybir.dt.uint32
ALU = mybir.AluOpType
ACT = mybir.ActivationFunctionType
AX = mybir.AxisListType.X

P = 128
F = 32
GROUPS = 4
HALVES = 2
Q = GROUPS * HALVES
SPAN = HALVES * P
CHUNK = GROUPS * SPAN
LINE = 512
NODE_COLS = 16
RING = 2
FAR = 1.0e30
EPS = 1e-5
SLOPE = 0.2


class Kernel:
    pass


class NormSignals:

    def __init__(self, signal, name):
        self.centred, self.squared = signal(name + "_centred"), signal(name + "_squared")
        self.varied, self.rooted = signal(name + "_varied"), signal(name + "_rooted")


class NormTiles:
    def __init__(self, sb, name, n):
        self.total, self.centred = sb(name + "_total", [P, n])[:], sb(name + "_centred", [P, n, F])[:]
        self.squares, self.var = sb(name + "_squares", [P, n, F])[:], sb(name + "_var", [P, n])[:]
        self.dev, self.inv = sb(name + "_dev", [P, n])[:], sb(name + "_inv", [P, n])[:]


class SumTiles:
    def __init__(self, sb):
        self.carry, self.alone, self.sums = sb("carry", [P, 2, P]), sb("alone", [P, SPAN]), sb("sums", [P, SPAN])


class NodeTiles:
    def __init__(self, sb):
        self.rows, self.kept = sb("n_rows", [P, NODE_COLS, F]), sb("n_kept", [P, 4 * P])
        self.x, self.out = sb("n_x", [P, RING, NODE_COLS * F]), sb("n_out", [P, RING, NODE_COLS, F])
        self.ln = NormTiles(sb, "lnn", NODE_COLS)


class SortSemaphores:
    def __init__(self, sem):
        self.loaded, self.flags, self.counted = sem("sort_loaded"), sem("sort_flags"), sem("sort_counted")
        self.known, self.piece, self.piece_used = sem("sort_known"), sem("sort_piece"), sem("sort_piece_used")
        self.rows, self.set, self.free = sem("sort_rows"), sem("sort_set"), sem("sort_free")
        self.stored, self.ends = sem("sort_stored"), sem("sort_ends")


class Signal:

    def __init__(self, sem, unit=1):
        self.sem, self.unit, self.before = sem, unit, 0

    def at(self, n):
        return self.sem, self.before + n * self.unit

    def close(self, n):
        self.before += n * self.unit


class Order:

    def __init__(self, sem):
        self.sem, self.before, self.base, self.k = sem, 0, 0, 0

    def enter(self, eng, turn=0, per_turn=None):
        self.eng, self.k, self.per_turn = eng, 0, per_turn
        self.base = self.before + turn * (per_turn or 0)

    def settle(self, instruction):
        instruction.then_inc(self.sem, 1)
        self.k += 1
        self.eng.wait_ge(self.sem, self.base + self.k)

    def note(self, instruction):
        instruction.then_inc(self.sem, 1)
        self.k += 1

    def leave(self):
        assert self.per_turn is None or self.k == self.per_turn, f"a turn has {self.k} steps"

    def close(self, turns=1):
        self.before += self.k * turns


def chunks(eng, n, start=0):
    turns = (n - start) // RING
    if turns:
        with eng.Fori(0, turns) as i:
            for place in range(RING):
                yield i * RING + place + start, place, i
    for rest in range(turns * RING, n - start):
        yield rest + start, rest % RING, turns


def chunks_ahead(eng, n):
    for c, place, i in chunks(eng, n - RING):
        yield c, place, i, True
    for c in range(n - RING, n):
        yield c, c % RING, c // RING, False


def close_ring(signals, n, more=0):
    for place, s in enumerate(signals):
        s.close(len(range(place, n, RING)) + more)


def wait_ring(eng, signals, n, more=0):
    for place, s in enumerate(signals):
        eng.wait_ge(*s.at(len(range(place, n, RING)) + more))


def spread(ap, n, width):
    return ap.unsqueeze(2).to_broadcast([ap.shape[0], n, width])


def build(nc, d, NC):
    k = Kernel()
    k.nc, k.d, k.NC = nc, d, NC
    k.NP, k.EP, k.JN, k.SP = NC * NODE_COLS * P, NC * CHUNK, NC * NODE_COLS, NC * CHUNK // LINE
    with ExitStack() as ctx:
        def sb(name, shape, dt=F32):
            return ctx.enter_context(nc.sbuf_tensor(name, shape, dt))

        k.bank = [ctx.enter_context(nc.psum_tensor(f"bank{n}", [P, 512], F32)) for n in range(8)]

        k.ident = sb("ident", [P, P])
        k.ones_row = sb("ones_row", [1, P])
        k.carry_base = sb("carry_base", [P, 4, P])
        k.eps = sb("eps", [P, 1])
        k.w0 = sb("w0", [P, P])
        k.w1 = sb("w1", [P, P])
        k.w2s = sb("w2s", [P, 256])
        k.w2d = sb("w2d", [P, 256])
        k.w1l = sb("w1l", [P, 256])
        k.w1r = sb("w1r", [P, 256])
        k.w2lr = sb("w2lr", [P, P])
        k.w3 = sb("w3", [P, P])
        k.attn = sb("attn", [P, 4])
        k.attn_parts = sb("attn_parts", [P, 2, 4])
        k.bz = sb("bz", [P, 2])
        k.b1_col = sb("b1_col", [P, 1])
        k.b1_row = sb("b1_row", [1, 512])
        k.b2s_row = sb("b2s_row", [1, 512])
        k.b2 = sb("b2", [P, F])
        k.b3 = sb("b3", [P, F])
        k.dst_rows = sb("dst_rows", [P, NC, Q])
        k.dst_index = sb("dst_index", [P, NC * Q], U32)
        k.src_index = sb("src_index", [P, NC * Q], U32)
        k.table_index = sb("table_index", [P, NC * Q], U32)
        k.store_rows = sb("store_rows", [P, NC, Q])
        k.inv_deg = sb("inv_deg", [P, NC, Q])
        k.inv_sqrt_deg = sb("inv_sqrt_deg", [P, NC, Q])
        k.same = sb("same", [P, NC, SPAN + 1], BF16)
        k.first_col = sb("first_col", [P, NC + 1])
        k.last_col = sb("last_col", [P, NC + 1])
        k.first_all = sb("first_all", [P, NC, GROUPS])
        k.last_all = sb("last_all", [P, NC, GROUPS])
        k.line_same = sb("line_same", [k.SP, LINE + 1])
        k.line_far = sb("line_far", [k.SP, LINE + 1])
        k.line_fwd = sb("line_fwd", [k.SP, k.SP])
        k.line_bwd = sb("line_bwd", [k.SP, k.SP])
        k.line_far_fwd = sb("line_far_fwd", [k.SP, k.SP])
        k.line_far_bwd = sb("line_far_bwd", [k.SP, k.SP])
        k.line_ones = sb("line_ones", [k.SP, k.SP])
        k.carry_col = sb("carry_col", [k.SP, 1])
        k.line_a = sb("line_a", [k.SP, LINE])
        k.line_f = sb("line_f", [k.SP, LINE])
        k.line_b = sb("line_b", [k.SP, LINE])
        k.line_diag = sb("line_diag", [k.SP, k.SP])
        k.logits = sb("logits", [P, 8, NC * 2])
        k.alpha = sb("alpha", [P, NC, 2 * Q])

        def sem(name):
            return ctx.enter_context(nc.semaphore(name))

        k.dve, k.act, k.pool = Order(sem("dve_done")), Order(sem("act_done")), Order(sem("pool_done"))

        def signal(name, unit=1):
            return Signal(sem(name), unit)

        k.loaded = signal("loaded", 16)
        k.prepared = signal("prepared")
        k.line_carried = signal("line_carried")
        k.line_scanned = signal("line_scanned")
        k.turned = signal("turned")
        k.turned_used = signal("turned_used")
        k.gathered = [signal(f"gathered{n}", 16 * Q) for n in range(RING)]
        k.attr_ready = signal("attr_ready", 16)
        k.index_set = signal("index_set")
        k.gather_started = signal("gather_started")
        k.ring_free = [signal(f"ring_free{n}") for n in range(RING)]
        k.rows_ready = signal("rows_ready")
        k.columns_ready = signal("columns_ready")
        k.scanned_alone = signal("scanned_alone")
        k.carried = signal("carried")
        k.scanned = signal("scanned")
        k.projected = signal("projected")
        k.projected_used = signal("projected_used")
        k.e_ln, k.n_ln = NormSignals(signal, "e"), NormSignals(signal, "n")
        k.e_out = signal("e_out")
        k.e_stored = [signal(f"e_stored{n}", 16) for n in range(RING)]
        k.e_loaded = [signal(f"e_loaded{n}", 16) for n in range(RING)]
        k.e_load_used = signal("e_load_used")
        k.n_loaded = [signal(f"n_loaded{n}", 16) for n in range(RING)]
        k.n_load_used = signal("n_load_used")
        k.n_out = signal("n_out")
        k.n_out2 = signal("n_out2")
        k.n_stored = [signal(f"n_stored{n}", 16) for n in range(RING)]
        k.n_rows = signal("n_rows")
        k.n_columns = signal("n_columns")
        k.n_columns_kept = signal("n_columns_kept")
        k.n_hidden = signal("n_hidden")
        k.n_hidden_kept = signal("n_hidden_kept")
        k.n_projected = signal("n_projected")
        k.e_columns = signal("e_columns")
        k.e_columns_kept = signal("e_columns_kept")
        k.e_hidden = signal("e_hidden")
        k.e_hidden_kept = signal("e_hidden_kept")
        k.e_projected = signal("e_projected")
        k.e_gap = signal("e_gap")
        k.e_en = signal("e_en")
        k.e_state = signal("e_state")
        k.e_logits = signal("e_logits")
        k.weighted = signal("weighted")
        k.raised = signal("raised")
        k.summed = signal("summed")
        k.counted = signal("counted")
        k.onehot = signal("onehot")
        k.scattered = [signal(f"scattered{n}", 16 * Q) for n in range(RING)]

        k.sort_dve = Order(sem("sort_dve_done"))
        k.sort = SortSemaphores(sem)
        k.dst_sorted = nc.dram_tensor("dst_sorted", (k.EP + 2,), I32).ap()
        k.src_sorted = nc.dram_tensor("src_sorted", (k.EP,), I32).ap()
        k.attr_sorted = nc.dram_tensor("attr_sorted", (k.EP, 2 * F), F32).ap()
        k.t01 = nc.dram_tensor("table01", (k.NP + k.EP, F + 1), F32).ap()
        k.t2 = nc.dram_tensor("table2", (k.NP + k.EP, F), F32).ap()
        k.t2b = nc.dram_tensor("table2b", (k.NP + k.EP, F), F32).ap()
        k.t3 = nc.dram_tensor("table3", (k.NP + k.EP, F), F32).ap()
        k.xa = nc.dram_tensor("nodes_after1", (k.NP, F), F32).ap()
        k.xb = nc.dram_tensor("nodes_after2", (k.NP, F), F32).ap()
        k.gap_rows = nc.dram_tensor("edge_gaps", (k.EP, 2 * F), F32).ap()

        load_constants(k)
        sort_edges(k)
        k.state = sb("state", [P, NC, Q * F])
        prepare_edges(k)
        gather_destinations(k)
        with ExitStack() as inner:
            k.sums0 = inner.enter_context(nc.sbuf_tensor("sums0", [P, NC * SPAN], F32))
            layer0(k)
            layer1_logits(k)
        layer1_softmax(k)
        layer1_sums(k)
        layer2_first(k)
        layer2_second(k)
        layer3(k)



def allocator(k, ctx, phase):
    def sb(name, shape, dt=F32):
        return ctx.enter_context(k.nc.sbuf_tensor(f"{phase}_{name}", shape, dt))
    return sb


def edge_rows(table, base, c):
    width = table.shape[1]
    return table[bass.ds(base + c * CHUNK, CHUNK), :].rearrange("(p q) f -> p (q f)", p=P)


def node_rows(table, c, nodes):
    whole = table[0:nodes, :].rearrange("(p j) f -> p (j f)", p=P)
    width = NODE_COLS * table.shape[1]
    return whole[:, bass.ds(c * width, width)]


def gather(pool, k, table, ring, index_ring, place):
    pool.sem_inc(k.gather_started.sem, 1)
    for q in range(Q):
        pool.indirect_dma_start(out=ring[:, place, q, :], out_offset=None, in_=table,
                                in_offset=bass.IndirectOffsetOnAxis(ap=index_ring[:, place, q:q + 1], axis=0)
                                ).then_inc(k.gathered[place].sem, 16)


def ln_centre(dve, k, ln, x, n, s):
    k.dve.settle(dve.tensor_reduce(s.total, x, AX, ALU.add))
    dve.scalar_tensor_tensor(s.centred, spread(s.total, n, F), -1.0 / F, x, ALU.mult, ALU.add
                             ).then_inc(ln.centred.sem, 1)


def ln_square(act, k, ln, c, s):
    act.wait_ge(*ln.centred.at(c + 1))
    act.activation(s.squares, s.centred, ACT.Square).then_inc(ln.squared.sem, 1)


def ln_variance(dve, k, ln, c, s):
    dve.wait_ge(*ln.squared.at(c + 1))
    dve.tensor_reduce(s.var, s.squares, AX, ALU.add).then_inc(ln.varied.sem, 1)


def ln_root(act, k, ln, c, s):
    act.wait_ge(*ln.varied.at(c + 1))
    act.activation(s.dev, s.var, ACT.Sqrt, bias=k.eps[:], scale=1.0 / F).then_inc(ln.rooted.sem, 1)


def ln_scale(dve, k, ln, c, n, s, out):
    dve.wait_ge(*ln.rooted.at(c + 1))
    k.dve.settle(dve.reciprocal(s.inv, s.dev))
    return dve.scalar_tensor_tensor(out, s.centred, 0.0, spread(s.inv, n, F), ALU.max, ALU.mult)


def ln_close(ln, n):
    for s in (ln.centred, ln.squared, ln.varied, ln.rooted):
        s.close(n)


FORWARD, FORWARD_BEFORE, BACKWARD, BACKWARD_AFTER = range(4)


def pe_turn(pe, k, rows, columns):
    for h in range(HALVES):
        last = pe.transpose(columns[:, h * P:(h + 1) * P], rows[:, h * P:(h + 1) * P], k.ident[:])
    return last


def dve_scan_alone(dve, k, t, c, columns):
    dve.scalar_tensor_tensor(t.carry[:, 0, :].rearrange("p (g f) -> p g f", g=GROUPS),
                             spread(k.first_all[:, bass.ds(c, 1), :].rearrange("p o g -> p (o g)"), GROUPS, F),
                             k.last_col[:, bass.ds(c + 1, 1)],
                             k.carry_base[:, FORWARD, :].rearrange("p (g f) -> p g f", g=GROUPS),
                             ALU.is_equal, ALU.mult)
    dve.scalar_tensor_tensor(t.carry[:, 1, :].rearrange("p (g f) -> p g f", g=GROUPS),
                             spread(k.first_all[:, bass.ds(c, 1), :].rearrange("p o g -> p (o g)"), GROUPS, F),
                             k.last_col[:, bass.ds(c, 1)],
                             k.carry_base[:, FORWARD_BEFORE, :].rearrange("p (g f) -> p g f", g=GROUPS),
                             ALU.is_equal, ALU.mult)
    dve.wait_ge(*k.columns_ready.at(c + 1))
    dve.tensor_tensor_scan(t.alone[:], flat(k.same[:, bass.ds(c, 1), 0:SPAN]), columns, 0.0, ALU.mult, ALU.add
                           ).then_inc(k.scanned_alone.sem, 1)


def flat(ap):
    return ap.rearrange("p o n -> p (o n)")


def pe_carry(pe, k, t, c, before, out):
    pe.wait_ge(*k.scanned_alone.at(c + 1))
    pe.matmul(out, t.carry[:, 0, :], t.alone[:, SPAN - 1:SPAN], start=True, stop=False)
    pe.matmul(out, t.carry[:, 1, :], before, start=False, stop=True).then_inc(k.carried.sem, 1)


def dve_scan(dve, k, c, columns, carry, sums):
    dve.wait_ge(*k.carried.at(c + 1))
    dve.tensor_tensor_scan(sums, flat(k.same[:, bass.ds(c, 1), 0:SPAN]), columns, carry, ALU.mult, ALU.add
                           ).then_inc(k.scanned.sem, 1)


def act_index(act, k, index, index_ring, c, place, reverse=None):
    col = c * Q if reverse is None else (reverse - c) * Q
    return act.activation(index_ring[:, place, :], index[:, bass.ds(col, Q)], ACT.Copy)


def start_ring(act, k, index, index_ring, reverse=None):
    for place in range(RING):
        act_index(act, k, index, index_ring, place, place, reverse).then_inc(k.index_set.sem, 1)



def load_constants(k):
    nc, d = k.nc, k.d
    k.n_loads = 3 + 6 + 2 + 28 + 4 + 4 + 1
    squares = [(k.w0, d["L0_gnn_W"], F), (k.w1, d["L1_gnn_W1"], F), (k.w3, d["L3_gnn_W_turned"], F),
               (k.w2s, d["L1_gnn_W2s"], 2 * F), (k.w2d, d["L1_gnn_W2d"], 2 * F),
               (k.w1l, d["L2_gnn_W1_l"], 2 * F), (k.w1r, d["L2_gnn_W1_r"], 2 * F)]
    zeroed = [w for w, _, _ in squares] + [k.w2lr, k.attn]
    with nc.Block() as block:
        @block.vector
        def _(dve):
            dve.memset(k.ones_row[:], 1.0)
            dve.memset(k.eps[:], EPS)
            dve.memset(k.line_ones[:], 1.0)
            for w in zeroed:
                last = dve.memset(w[:], 0.0)
            last.then_inc(k.prepared.sem, 1)
            dve.wait_ge(*k.loaded.at(k.n_loads))
            dve.tensor_scalar(k.attn_parts[:, 0, :], k.attn[:], SLOPE, None, ALU.mult)
            dve.tensor_scalar(k.attn_parts[:, 1, :], k.attn[:], 1.0 - SLOPE, None, ALU.mult)
            dve.tensor_tensor(k.bz[:, 0:1], k.bz[:, 0:1], k.bz[:, 1:2], ALU.add).then_inc(k.prepared.sem, 1)
            dve.wait_ge(*k.prepared.at(2))

        @block.sync
        def _(sp):
            n = 0

            def load(out, in_):
                sp.dma_start(out, in_).then_inc(k.loaded.sem, 16)
                return 1

            n += load(k.ident[:], d["identity"])
            n += load(k.carry_base[:], d["carry_patterns"])
            n += load(k.b3[:], d["L3_gnn_bias"].partition_broadcast(P))
            n += load(k.b2[:], d["L2_gnn_b2"].partition_broadcast(P))
            for gl in range(2):
                n += load(k.b1_col[64 * gl:64 * gl + 64, :], d["L2_gnn_b1"].unsqueeze(1))
                n += load(k.bz[64 * gl:64 * gl + 64, 0:1], d["L1_gnn_b2s"].unsqueeze(1))
                n += load(k.bz[64 * gl:64 * gl + 64, 1:2], d["L1_gnn_b2d"].unsqueeze(1))
            n += load(k.b1_row[:].rearrange("o (n f) -> o n f", f=F),
                      d["L1_gnn_b1"].unsqueeze(0).unsqueeze(1).to_broadcast([1, 16, F]))
            n += load(k.b2s_row[:].rearrange("o (n f) -> o n f", f=2 * F),
                      d["L1_gnn_b2s"].unsqueeze(0).unsqueeze(1).to_broadcast([1, 8, 2 * F]))
            sp.wait_ge(*k.prepared.at(1))
            for w, src, width in squares:
                for g in range(GROUPS):
                    n += load(w[F * g:F * g + F, width * g:width * g + width], src)
            for gl in range(2):
                n += load(k.w2lr[64 * gl:64 * gl + 64, 64 * gl:64 * gl + 32], d["L2_gnn_W2_l"])
                n += load(k.w2lr[64 * gl:64 * gl + 64, 64 * gl + 32:64 * gl + 64], d["L2_gnn_W2_r"])
                for h in range(2):
                    at = 64 * gl + 32 * h
                    n += load(k.attn[at:at + 32, 2 * gl + h:2 * gl + h + 1], d["L1_gnn_attn"][0, h, :].unsqueeze(1))
            assert n == k.n_loads, n
            sp.wait_ge(*k.loaded.at(n))
    k.loaded.close(k.n_loads)
    k.prepared.close(2)


def sort_edges(k):
    nc, d, NC, SP, EP = k.nc, k.d, k.NC, k.SP, k.EP
    pieces = next(n for n in range(1, NC + 1) if NC % n == 0 and EP // n <= 8 * CHUNK)
    width = EP // pieces
    s, order = k.sort, k.sort_dve
    with ExitStack() as ctx:
        sb = allocator(k, ctx, "sort")
        line = sb("line", [SP, LINE + 2], I32)
        falls = sb("falls", [SP, LINE])
        fall_count = sb("fall_count", [SP, 1])
        unsorted = sb("unsorted", [1, 1], I32)
        dst_all = sb("dst_all", [P, width], I32)
        number_all = sb("number_all", [P, width])
        ahead = sb("ahead", [P, width])
        dst_own = sb("dst_own", [P, NC, Q], I32)
        src_own = sb("src_own", [P, NC, Q], I32)
        dst_f = sb("dst_f", [P, NC * Q])
        number_own = sb("number_own", [P, NC * Q])
        found = sb("found", [P, 1])
        rank = sb("rank", [P, NC * Q])
        row = sb("row", [P, 4, NC * Q], I32)
        targets = sb("targets", [P, 3, Q], U32)
        own = sb("own", [P, 2, Q], I32)
        attr = sb("attr", [P, Q, 2 * F])
        count = k.bank[0][0:1, 0:1]

        with nc.Block() as block:
            @block.sync
            def _(sp):
                sp.dma_start(line[:], bass.AP(tensor=d["dst_line"].tensor, offset=0, ap=[[LINE, SP], [1, LINE + 2]])
                             ).then_inc(s.loaded, 16)
                sp.wait_ge(s.known, 1)
                falling = sp.value_load(unsorted[0:1, 0:1])
                with sp.If(falling == 0):
                    sp.dma_start(k.dst_sorted, d["dst_line"]).then_inc(s.ends, 16)
                    sp.dma_start(k.src_sorted, d["src_line"]).then_inc(s.ends, 16)
                    sp.dma_start(k.attr_sorted, d["edge_attr"]).then_inc(k.attr_ready.sem, 16)
                    sp.wait_ge(s.ends, 32)
                with sp.Else():
                    for b in range(HALVES):
                        for c in range(NC):
                            at = c * CHUNK + b * P
                            with nc.allow_non_contiguous_dma("the edges of a lane lie apart"):
                                sp.dma_start(dst_own[:, c, b * GROUPS:(b + 1) * GROUPS],
                                             bass.AP(tensor=d["dst_line"].tensor, offset=1 + at, ap=[[1, P], [SPAN, GROUPS]])
                                             ).then_inc(s.rows, 16)
                                sp.dma_start(src_own[:, c, b * GROUPS:(b + 1) * GROUPS],
                                             bass.AP(tensor=d["src_line"].tensor, offset=at, ap=[[1, P], [SPAN, GROUPS]])
                                             ).then_inc(s.rows, 16)
                    sp.dma_start(number_own[:], d["edge_number_rows"]).then_inc(s.rows, 16)
                    for n in range(pieces):
                        if n:
                            sp.wait_ge(s.piece_used, n)
                        at = slice(n * width, (n + 1) * width)
                        sp.dma_start(dst_all[:], d["dst_line"][1 + n * width:1 + (n + 1) * width].partition_broadcast(P)
                                     ).then_inc(s.piece, 16)
                        sp.dma_start(number_all[:], d["edge_number"][at].partition_broadcast(P)).then_inc(s.piece, 16)
                    for at in (0, EP + 1):
                        sp.dma_start(k.dst_sorted[at:at + 1], d["dst_line"][at:at + 1]).then_inc(s.ends, 16)
                    with sp.Fori(0, NC) as c:
                        sp.wait_ge(s.free, c + 1)
                        sp.dma_start(attr[:].rearrange("p q f -> p (q f)"), edge_rows(d["edge_attr"], 0, c)).then_inc(s.loaded, 16)
                    sp.wait_ge(s.ends, 32)
                    sp.wait_ge(s.free, NC + 1)
                    sp.sem_inc(k.attr_ready.sem, 16)

            @block.tensor
            def _(pe):
                pe.wait_ge(s.flags, 1)
                pe.matmul(count, fall_count[:], k.line_ones[:, 0:1], start=True, stop=True).then_inc(s.counted, 1)

            @block.vector
            def _(dve):
                order.enter(dve)
                dve.wait_ge(s.loaded, 16)
                order.settle(dve.tensor_tensor(falls[:], line[:, 0:LINE], line[:, 1:LINE + 1], ALU.is_gt))
                dve.tensor_reduce(fall_count[:], falls[:], AX, ALU.add).then_inc(s.flags, 1)
                dve.wait_ge(s.counted, 1)
                dve.tensor_copy(unsorted[:], count).then_inc(s.known, 1)
                dve.wait_ge(s.known, 1)
                falling = dve.value_load(unsorted[0:1, 0:1])
                with dve.If(falling == 0):
                    dve.sem_inc(s.flags, 1)
                with dve.Else():
                    dve.wait_ge(s.rows, 16 * (4 * NC + 1))
                    order.settle(dve.tensor_copy(dst_f[:], dst_own[:].rearrange("p c q -> p (c q)")))
                    order.settle(dve.memset(rank[:], 0.0))
                    order.close()
                    for n in range(pieces):
                        dve.wait_ge(s.piece, 32 * (n + 1))
                        with dve.Fori(0, NC * Q) as t:
                            order.enter(dve, t, 5)
                            order.settle(dve.tensor_scalar(ahead[:], number_all[:], number_own[:, bass.ds(t, 1)], None, ALU.is_lt))
                            order.settle(dve.scalar_tensor_tensor(ahead[:], dst_all[:], dst_f[:, bass.ds(t, 1)], ahead[:],
                                                                  ALU.is_equal, ALU.mult))
                            order.settle(dve.scalar_tensor_tensor(ahead[:], dst_all[:], dst_f[:, bass.ds(t, 1)], ahead[:],
                                                                  ALU.is_lt, ALU.add))
                            order.settle(dve.tensor_reduce(found[:], ahead[:], AX, ALU.add))
                            order.note(dve.tensor_tensor(rank[:, bass.ds(t, 1)], rank[:, bass.ds(t, 1)], found[:], ALU.add))
                            order.leave()
                        order.close(NC * Q)
                        order.enter(dve)
                        dve.wait_ge(order.sem, order.base)
                        dve.sem_inc(s.piece_used, 1)
                    order.enter(dve)
                    order.settle(dve.tensor_copy(row[:, 0, :], rank[:]))
                    row_of_edge(dve, order, row)
                    order.close()
                    with dve.Fori(0, NC) as c:
                        order.enter(dve, c, 4)
                        dve.wait_ge(s.free, c + 1)
                        order.note(dve.tensor_scalar(targets[:, 0, :], rank[:, bass.ds(c * Q, Q)], 1.0, None, ALU.add))
                        order.note(dve.tensor_copy(targets[:, 1, :], rank[:, bass.ds(c * Q, Q)]))
                        order.note(dve.tensor_copy(targets[:, 2, :], row[:, 0, bass.ds(c * Q, Q)]))
                        order.note(dve.tensor_copy(own[:, 0, :], flat(dst_own[:, bass.ds(c, 1), :])))
                        dve.tensor_copy(own[:, 1, :], flat(src_own[:, bass.ds(c, 1), :])).then_inc(s.set, 1)
                        order.leave()
                    order.close(NC)

            @block.gpsimd
            def _(pool):
                pool.wait_ge(s.known, 1)
                falling = pool.value_load(unsorted[0:1, 0:1])
                with pool.If(falling == 0):
                    pool.sem_inc(s.flags, 1)
                with pool.Else():
                    pool.sem_inc(s.free, 1)
                    with pool.Fori(0, NC) as c:
                        pool.wait_ge(s.set, c + 1)
                        pool.wait_ge(s.loaded, 16 * (c + 2))
                        pool.sem_inc(s.flags, 1)
                        for q in range(Q):
                            for n, (out, data) in enumerate(((k.dst_sorted, own[:, 0, q:q + 1]), (k.src_sorted, own[:, 1, q:q + 1]),
                                                             (k.attr_sorted, attr[:, q, :]))):
                                pool.indirect_dma_start(
                                    out=out.unsqueeze(1) if n < 2 else out,
                                    out_offset=bass.IndirectOffsetOnAxis(ap=targets[:, n, q:q + 1], axis=0),
                                    in_=data, in_offset=None).then_inc(s.stored, 16)
                        pool.wait_ge(s.stored, (c + 1) * (16 * 3 * Q))
                        pool.sem_inc(s.free, 1)


def line_carry(k):
    return k.bank[0][0:k.SP, 0:1], k.bank[0][0:k.SP, 0:k.SP]


def dve_line_total(dve, k, values, op, out, turn):
    same, op0, start = (k.line_same, ALU.mult, 0.0) if op == ALU.add else (k.line_far, ALU.add, -FAR)
    carry, everyone = line_carry(k)
    for way in range(2):
        if way == 0:
            flags, data, result = same[:, 0:LINE], values, k.line_f[:]
            alone, tail, far = k.line_a[:], k.line_a[:, LINE - 1:LINE], k.line_far_fwd
        else:
            flags, data, result = same[:, 1:LINE + 1][:, ::-1], values[:, ::-1], k.line_b[:, ::-1]
            alone, tail, far = k.line_a[:, ::-1], k.line_a[:, 0:1], k.line_far_bwd
        if op == ALU.add:
            dve.tensor_tensor_scan(alone, flags, data, start, op0, op).then_inc(k.line_scanned.sem, 1)
            dve.wait_ge(*k.line_carried.at(turn + way + 1))
            k.dve.settle(dve.tensor_tensor_scan(result, flags, data, carry, op0, op))
        else:
            k.dve.settle(dve.tensor_tensor_scan(alone, flags, data, start, op0, op))
            dve.tensor_scalar(k.line_diag[:], k.ident[0:k.SP, 0:k.SP], tail, None, ALU.mult
                              ).then_inc(k.line_scanned.sem, 1)
            dve.wait_ge(*k.line_carried.at(turn + way + 1))
            k.dve.settle(dve.tensor_tensor(k.line_diag[:], everyone, far[:], ALU.add))
            k.dve.settle(dve.tensor_reduce(k.carry_col[:], k.line_diag[:], AX, ALU.max))
            k.dve.settle(dve.tensor_tensor_scan(result, flags, data, k.carry_col[:], op0, op))
    if op == ALU.add:
        k.dve.settle(dve.tensor_tensor(out, k.line_f[:], k.line_b[:], ALU.add))
        k.dve.settle(dve.tensor_tensor(out, out, values, ALU.subtract))
    else:
        k.dve.settle(dve.tensor_tensor(out, k.line_f[:], k.line_b[:], ALU.max))


def pe_line_total(pe, k, op, turn):
    carry, everyone = line_carry(k)
    for way in range(2):
        pe.wait_ge(*k.line_scanned.at(turn + way + 1))
        if op == ALU.add:
            reach, tail = ((k.line_fwd, k.line_a[:, LINE - 1:LINE]), (k.line_bwd, k.line_a[:, 0:1]))[way]
            pe.matmul(carry, reach[:], tail, start=True, stop=True).then_inc(k.line_carried.sem, 1)
        else:
            pe.matmul(everyone, k.line_ones[:], k.line_diag[:], start=True, stop=True).then_inc(k.line_carried.sem, 1)


def prepare_edges(k):
    nc, d, NC, SP = k.nc, k.d, k.NC, k.SP
    dst, src = k.dst_sorted, k.src_sorted
    with ExitStack() as ctx:
        sb = allocator(k, ctx, "prep")
        dst_int = sb("dst_int", [SP, LINE + 2], I32)
        src_int = sb("src_int", [SP, LINE], I32)
        dstf = sb("dstf", [SP, LINE + 2])
        srcf = sb("srcf", [SP, LINE])
        tmp = sb("tmp", [SP, LINE])
        ones = sb("ones", [SP, LINE])
        deg = sb("deg", [SP, LINE])
        inv = sb("inv", [SP, LINE])
        isd = sb("isd", [SP, LINE])
        store = sb("store", [SP, LINE])
        lt = sb("lt", [P, P])
        gt = sb("gt", [P, P])
        dcols = sb("dcols", [P, NC, SPAN + 2], I32)
        pick = sb("pick", [P, GROUPS, P])

        with nc.Block() as block:
            @block.sync
            def _(sp):
                sp.dma_start(dst_int[:], bass.AP(tensor=dst.tensor, offset=0, ap=[[LINE, SP], [1, LINE + 2]])
                             ).then_inc(k.loaded.sem, 16)
                sp.dma_start(src_int[:], src.rearrange("(p n) -> p n", n=LINE)).then_inc(k.loaded.sem, 16)
                sp.dma_start(lt[:], d["below"]).then_inc(k.loaded.sem, 16)
                sp.dma_start(gt[:], d["above"]).then_inc(k.loaded.sem, 16)
                sp.dma_start(pick[:], d["pick_group"]).then_inc(k.loaded.sem, 16)
                for g in range(GROUPS):
                    sp.dma_start(dcols[F * g:F * g + F, :, :],
                                 bass.AP(tensor=dst.tensor, offset=g * SPAN,
                                         ap=[[0, F], [CHUNK, NC], [1, SPAN + 2]])).then_inc(k.loaded.sem, 16)
                sp.wait_ge(*k.loaded.at(9))

            @block.vector
            def _(dve):
                order = k.dve
                order.enter(dve)
                dve.wait_ge(*k.loaded.at(9))
                dve.memset(ones[:], 1.0)
                dve.tensor_copy(srcf[:], src_int[:])
                order.settle(dve.tensor_copy(dstf[:], dst_int[:]))
                order.settle(dve.tensor_tensor(k.line_same[:], dstf[:, 1:LINE + 2], dstf[:, 0:LINE + 1], ALU.is_equal))
                order.settle(dve.tensor_scalar(k.line_far[:], k.line_same[:], 1.0, FAR, ALU.subtract, ALU.mult))
                order.settle(dve.tensor_scalar(k.line_diag[:], k.ident[0:SP, 0:SP], dstf[:, 1:2], None, ALU.mult))
                order.settle(dve.tensor_scalar(tmp[:, 0:SP], k.ident[0:SP, 0:SP], dstf[:, LINE:LINE + 1], None, ALU.mult))
                dve.sem_inc(k.line_scanned.sem, 2)
                dve.wait_ge(*k.line_carried.at(2))
                first, last = k.bank[1][0:SP, 0:SP], k.bank[2][0:SP, 0:SP]
                dve.scalar_tensor_tensor(k.line_fwd[:], first, dstf[:, LINE:LINE + 1], lt[0:SP, 0:SP], ALU.is_equal, ALU.mult)
                dve.scalar_tensor_tensor(k.line_bwd[:], last, dstf[:, 1:2], gt[0:SP, 0:SP], ALU.is_equal, ALU.mult)
                dve.scalar_tensor_tensor(k.line_far_fwd[:], last, dstf[:, 1:2], gt[0:SP, 0:SP], ALU.is_equal, ALU.mult)
                order.settle(dve.scalar_tensor_tensor(k.line_far_bwd[:], first, dstf[:, LINE:LINE + 1], lt[0:SP, 0:SP], ALU.is_equal, ALU.mult))
                dve.tensor_scalar(k.line_far_fwd[:], k.line_far_fwd[:], 1.0, FAR, ALU.subtract, ALU.mult)
                order.settle(dve.tensor_scalar(k.line_far_bwd[:], k.line_far_bwd[:], 1.0, FAR, ALU.subtract, ALU.mult))
                dve_line_total(dve, k, ones[:], ALU.add, deg[:], 2)
                order.settle(dve.tensor_scalar(tmp[:], deg[:], 1.0, None, ALU.max))
                order.settle(dve.reciprocal(inv[:], tmp[:]))
                order.settle(dve.tensor_scalar(tmp[:], deg[:], 1.0, 1.0, ALU.add, ALU.max))
                dve.sem_inc(k.prepared.sem, 1)
                dve.wait_ge(*k.prepared.at(2))
                order.settle(dve.reciprocal(isd[:], tmp[:]))
                order.settle(dve.tensor_scalar(store[:], dstf[:, 1:LINE + 1], float(2 * k.NP), None, ALU.subtract))
                order.settle(dve.scalar_tensor_tensor(store[:], k.line_same[:, 1:LINE + 1], 0.0, store[:], ALU.is_equal, ALU.mult))
                order.settle(dve.tensor_scalar(store[:], store[:], float(2 * k.NP), None, ALU.add))
                dve.sem_inc(k.prepared.sem, 1)
                order.settle(dve.tensor_tensor(k.same[:], dcols[:, :, 1:SPAN + 2], dcols[:, :, 0:SPAN + 1], ALU.is_equal))
                dve.memset(k.first_col[:, NC:NC + 1], -2.0)
                dve.memset(k.last_col[:, 0:1], -1.0)
                dve.tensor_copy(k.first_col[:, 0:NC], dcols[:, :, 1])
                order.settle(dve.tensor_copy(k.last_col[:, 1:NC + 1], dcols[:, :, SPAN]))
                dve.sem_inc(k.prepared.sem, 1)
                for g in range(GROUPS):
                    for way, out in enumerate((k.first_all, k.last_all)):
                        n = 2 * g + way
                        dve.wait_ge(*k.counted.at(n + 1))
                        order.settle(dve.tensor_copy(out[:, :, g], k.bank[6 + n % 2][:, 0:NC]))
                        dve.sem_inc(k.onehot.sem, 1)

            @block.tensor
            def _(pe):
                pe.wait_ge(*k.line_scanned.at(2))
                pe.matmul(k.bank[1][0:SP, 0:SP], k.line_ones[:], k.line_diag[:], start=True, stop=True
                          ).then_inc(k.line_carried.sem, 1)
                pe.matmul(k.bank[2][0:SP, 0:SP], k.line_ones[:], tmp[:, 0:SP], start=True, stop=True
                          ).then_inc(k.line_carried.sem, 1)
                pe_line_total(pe, k, ALU.add, 2)
                pe.wait_ge(*k.prepared.at(3))
                n = 0
                for line in (dstf[:, 1:LINE + 1], srcf[:], inv[:], isd[:], store[:]):
                    for part in range(4):
                        if n >= 2:
                            pe.wait_ge(*k.turned_used.at(n - 1))
                        pe.transpose(k.bank[3 + n % 2][:, 0:SP], line[:, part * P:(part + 1) * P],
                                     k.ident[0:SP, 0:SP]).then_inc(k.turned.sem, 1)
                        n += 1
                pe.wait_ge(*k.prepared.at(4))
                for g in range(GROUPS):
                    for way, col in enumerate((k.first_col[:, 0:NC], k.last_col[:, 1:NC + 1])):
                        n = 2 * g + way
                        if n >= 2:
                            pe.wait_ge(*k.onehot.at(n - 1))
                        pe.matmul(k.bank[6 + n % 2][:, 0:NC], pick[:, g, :], col, start=True, stop=True
                                  ).then_inc(k.counted.sem, 1)

            @block.scalar
            def _(act):
                act.wait_ge(*k.prepared.at(1))
                act.activation(tmp[:], tmp[:], ACT.Sqrt).then_inc(k.prepared.sem, 1)
                n = 0
                for out in (k.dst_rows, k.src_index, k.inv_deg, k.inv_sqrt_deg, k.store_rows):
                    for part in range(4):
                        gl, b = part // 2, part % 2
                        view = out[:] if len(out.shape) == 3 else out[:].rearrange("p (c q) -> p c q", q=Q)
                        view = view.rearrange("p c (b j l) -> p c b j l", b=2, j=2)[:, :, b, :, gl]
                        act.wait_ge(*k.turned.at(n + 1))
                        act.activation(view, k.bank[3 + n % 2][:, 0:SP].rearrange("p (c j) -> p c j", j=2),
                                       ACT.Copy).then_inc(k.turned_used.sem, 1)
                        n += 1
                act.wait_ge(*k.turned_used.at(n))
                act.activation(k.dst_index[:], k.dst_rows[:].rearrange("p c q -> p (c q)"), ACT.Copy
                               ).then_inc(k.turned_used.sem, 1)
    k.loaded.close(9)
    k.prepared.close(4)
    k.line_scanned.close(4)
    k.line_carried.close(4)
    k.turned.close(20)
    k.turned_used.close(21)
    k.counted.close(8)
    k.onehot.close(8)
    k.dve.close()


def row_of_edge(dve, order, e):
    dve.tensor_scalar(e[:, 1, :], e[:, 0, :], 127, 3, ALU.bitwise_and, ALU.logical_shift_left)
    dve.tensor_scalar(e[:, 2, :], e[:, 0, :], 128, 5, ALU.bitwise_and, ALU.logical_shift_right)
    dve.tensor_scalar(e[:, 3, :], e[:, 0, :], 768, 8, ALU.bitwise_and, ALU.logical_shift_right)
    order.settle(dve.tensor_scalar(e[:, 0, :], e[:, 0, :], 10, 10, ALU.arith_shift_right, ALU.logical_shift_left))
    for part in (1, 2, 3):
        order.settle(dve.tensor_tensor(e[:, 0, :], e[:, 0, :], e[:, part, :], ALU.bitwise_or))


def gather_destinations(k):
    nc, d, NC, JN = k.nc, k.d, k.NC, k.JN
    half = JN // 2
    with ExitStack() as ctx:
        sb = allocator(k, ctx, "dest")
        ring = sb("ring", [P, RING, Q, F])
        index_ring = sb("index_ring", [P, RING, Q], U32)
        iota_lo = sb("iota_lo", [P, JN])
        iota_hi = sb("iota_hi", [P, P])
        before = sb("before", [P, P])
        node = sb("node", [P, JN])
        hi = sb("hi", [P, NC * Q])
        lo = sb("lo", [P, NC * Q])
        fix = sb("fix", [P, NC * Q])
        hi_int = sb("hi_int", [P, NC * Q], I32)
        hot_lo = sb("hot_lo", [P, 2, JN], BF16)
        hot_hi = sb("hot_hi", [P, 2, P], BF16)
        zeros = sb("zeros", [P, max(half, P)], BF16)
        degree = sb("degree", [P, JN])
        upto = sb("upto", [P, JN])
        ones = sb("ones_jn", [P, JN], BF16)
        carry = sb("carry", [P, 1])
        e_int = sb("e_int", [P, 4, JN], I32)
        pos = sb("pos", [P, JN], I32)
        xin = sb("xin", [P, RING, NODE_COLS, F])
        table = sb("table", [P, RING, NODE_COLS, F + 1])
        t = NormTiles(sb, "ln", NODE_COLS)
        counts = [k.bank[0][:, 0:half], k.bank[1][:, 0:half]]
        with nc.Block() as block:
            @block.gpsimd
            def _(pool):
                for c, place, i in chunks(pool, NC):
                    pool.wait_ge(*k.index_set.at(c + 1))
                    pool.wait_ge(*k.ring_free[place].at(i + 1))
                    gather(pool, k, d["x"], ring, index_ring, place)

            @block.scalar
            def _(act):
                start_ring(act, k, k.dst_index, index_ring)
                for place in range(RING):
                    act.sem_inc(k.ring_free[place].sem, 1)
                for c, place, i, ahead in chunks_ahead(act, NC):
                    act.wait_ge(*k.gathered[place].at(i + 1))
                    if ahead:
                        act_index(act, k, k.dst_index, index_ring, c + RING, place).then_inc(k.index_set.sem, 1)
                    act.activation(flat(k.state[:, bass.ds(c, 1), :]),
                                   ring[:, place, :, :].rearrange("p q f -> p (q f)"), ACT.Copy
                                   ).then_inc(k.ring_free[place].sem, 1)
                for c, place, i in chunks(act, NC):
                    ln_square(act, k, k.n_ln, c, t)
                    ln_root(act, k, k.n_ln, c, t)

            @block.vector
            def _(dve):
                order = k.dve
                order.enter(dve)
                dve.memset(zeros[:], 0.0)
                dve.memset(ones[:], 1.0)
                dst = k.dst_rows[:].rearrange("p c q -> p (c q)")
                order.settle(dve.tensor_scalar(hi[:], dst, 1.0 / JN, 0.5, ALU.mult, ALU.subtract))
                order.settle(dve.tensor_copy(hi_int[:], hi[:]))
                order.settle(dve.tensor_copy(hi[:], hi_int[:]))
                for _ in range(2):
                    order.settle(dve.scalar_tensor_tensor(lo[:], hi[:], -float(JN), dst, ALU.mult, ALU.add))
                    order.settle(dve.tensor_scalar(fix[:], lo[:], 0.0, None, ALU.is_lt))
                    order.settle(dve.tensor_tensor(hi[:], hi[:], fix[:], ALU.subtract))
                    order.settle(dve.tensor_scalar(fix[:], lo[:], float(JN), None, ALU.is_ge))
                    order.settle(dve.tensor_tensor(hi[:], hi[:], fix[:], ALU.add))
                order.settle(dve.scalar_tensor_tensor(lo[:], hi[:], -float(JN), dst, ALU.mult, ALU.add))
                dve.wait_ge(*k.loaded.at(4))
                dve.sem_inc(k.prepared.sem, 1)
                with dve.Fori(0, NC) as c:
                    for q in range(Q):
                        dve.wait_ge(*k.counted.at(c * Q + q + 1))
                        dve.tensor_scalar(hot_hi[:, q % 2, :], iota_hi[:], hi[:, bass.ds(c * Q + q, 1)], None, ALU.is_equal)
                        dve.tensor_scalar(hot_lo[:, q % 2, :], iota_lo[:], lo[:, bass.ds(c * Q + q, 1)], None, ALU.is_equal
                                          ).then_inc(k.onehot.sem, 1)
                dve.wait_ge(*k.counted.at(NC * Q + 3))
                for part in range(2):
                    order.settle(dve.tensor_copy(degree[:, part * half:(part + 1) * half], counts[part]))
                order.settle(dve.tensor_tensor_scan(upto[:], ones[:], degree[:], 0.0, ALU.mult, ALU.add))
                dve.sem_inc(k.onehot.sem, 1)
                dve.wait_ge(*k.counted.at(NC * Q + 4))
                order.settle(dve.tensor_scalar(carry[:], k.bank[2][:, 0:1], 1.0, None, ALU.subtract))
                order.settle(dve.tensor_scalar(upto[:], upto[:], carry[:], None, ALU.add))
                order.settle(dve.tensor_copy(e_int[:, 0, :], upto[:]))
                row_of_edge(dve, order, e_int)
                order.settle(dve.tensor_copy(upto[:], e_int[:, 0, :]))
                order.settle(dve.scalar_tensor_tensor(upto[:], upto[:], float(k.NP), node[:], ALU.add, ALU.subtract))
                order.settle(dve.scalar_tensor_tensor(upto[:], degree[:], 0.0, upto[:], ALU.is_gt, ALU.mult))
                order.settle(dve.tensor_tensor(pos[:], upto[:], node[:], ALU.add))
                order.close()
                for c, place, i in chunks(dve, NC):
                    order.enter(dve, c, 2)
                    dve.wait_ge(*k.n_loaded[place].at(i + 1))
                    ln_centre(dve, k, k.n_ln, xin[:, place, :, :], NODE_COLS, t)
                    ln_variance(dve, k, k.n_ln, c, t)
                    dve.wait_ge(*k.n_stored[place].at(i + 1))
                    dve.tensor_copy(table[:, place, :, F].bitcast(I32), pos[:, bass.ds(c * NODE_COLS, NODE_COLS)])
                    ln_scale(dve, k, k.n_ln, c, NODE_COLS, t, table[:, place, :, 0:F]).then_inc(k.n_out.sem, 1)
                    order.leave()
                order.close(NC)

            @block.tensor
            def _(pe):
                pe.wait_ge(*k.prepared.at(1))
                for part in range(2):
                    pe.matmul(counts[part], zeros[:, 0:P], zeros[:, 0:half], start=True, stop=False
                              ).then_inc(k.counted.sem, 1)
                with pe.Fori(0, NC) as c:
                    for q in range(Q):
                        pe.wait_ge(*k.onehot.at(c * Q + q + 1))
                        pe.matmul(counts[0], hot_hi[:, q % 2, :], hot_lo[:, q % 2, 0:half], start=False, stop=False)
                        pe.matmul(counts[1], hot_hi[:, q % 2, :], hot_lo[:, q % 2, half:JN], start=False, stop=False
                                  ).then_inc(k.counted.sem, 1)
                for part in range(2):
                    last = pe.matmul(counts[part], zeros[:, 0:P], zeros[:, 0:half], start=False, stop=True)
                last.then_inc(k.counted.sem, 1)
                pe.wait_ge(*k.onehot.at(NC * Q + 1))
                pe.matmul(k.bank[2][:, 0:1], before[:], upto[:, JN - 1:JN], start=True, stop=True
                          ).then_inc(k.counted.sem, 1)

            @block.sync
            def _(sp):
                sp.dma_start(iota_lo[:], d["count_up"][0:JN].partition_broadcast(P)).then_inc(k.loaded.sem, 16)
                sp.dma_start(iota_hi[:], d["count_up"][0:P].partition_broadcast(P)).then_inc(k.loaded.sem, 16)
                sp.dma_start(before[:], d["below"]).then_inc(k.loaded.sem, 16)
                sp.dma_start(node[:], d["node_number"]).then_inc(k.loaded.sem, 16)
                for place in range(RING):
                    sp.sem_inc(k.n_stored[place].sem, 16)
                    sp.dma_start(xin[:, place, :, :].rearrange("p n f -> p (n f)"), node_rows(d["x"], place, k.NP)
                                 ).then_inc(k.n_loaded[place].sem, 16)
                for c, place, i, ahead in chunks_ahead(sp, NC):
                    sp.wait_ge(*k.n_out.at(c + 1))
                    sp.dma_start(node_rows(k.t01, c, k.NP), table[:, place, :, :].rearrange("p n f -> p (n f)")
                                 ).then_inc(k.n_stored[place].sem, 16)
                    if ahead:
                        sp.dma_start(xin[:, place, :, :].rearrange("p n f -> p (n f)"), node_rows(d["x"], c + RING, k.NP)
                                     ).then_inc(k.n_loaded[place].sem, 16)
                wait_ring(sp, k.n_stored, NC, 1)
    close_ring(k.gathered, NC)
    close_ring(k.ring_free, NC, 1)
    k.index_set.close(NC)
    k.loaded.close(4)
    k.prepared.close(1)
    k.counted.close(NC * Q + 4)
    k.onehot.close(NC * Q + 1)
    ln_close(k.n_ln, NC)
    k.n_out.close(NC)
    close_ring(k.n_stored, NC, 1)
    close_ring(k.n_loaded, NC)


def layer0(k):
    nc, d, NC = k.nc, k.d, k.NC
    with ExitStack() as ctx:
        sb = allocator(k, ctx, "l0")
        ring = sb("ring", [P, RING, Q, F + 1])
        index_ring = sb("index_ring", [P, RING, Q], U32)
        rows = sb("rows", [P, SPAN])
        x1 = sb("x1", [P, Q, F])
        out = sb("out", [P, RING, Q, F + 1])
        s = SumTiles(sb)
        te = NormTiles(sb, "lne", Q)
        n = NodeTiles(sb)
        h_in = sb("h_in", [P, RING, NODE_COLS, F + 1])
        columns, carry, projected = k.bank[0][:, 0:SPAN], k.bank[0][:, SPAN:SPAN + 1], k.bank[1][:, 0:SPAN]
        n_columns, n_projected = k.bank[2], k.bank[3]

        with nc.Block() as block:
            @block.gpsimd
            def _(pool):
                for c, place, i in chunks(pool, NC):
                    pool.wait_ge(*k.index_set.at(c + 1))
                    pool.wait_ge(*k.ring_free[place].at(i + 1))
                    gather(pool, k, k.t01[0:k.NP, :], ring, index_ring, place)

            @block.scalar
            def _(act):
                start_ring(act, k, k.src_index, index_ring)
                for place in range(RING):
                    act.sem_inc(k.ring_free[place].sem, 1)
                for c, place, i, ahead in chunks_ahead(act, NC):
                    act.wait_ge(*k.n_loaded[place].at(2 * (i + 1)))
                    act.activation(n.rows[:], h_in[:, place, :, 0:F], ACT.Copy).then_inc(k.n_rows.sem, 1)
                    act.wait_ge(*k.gathered[place].at(i + 1))
                    if ahead:
                        act_index(act, k, k.src_index, index_ring, c + RING, place).then_inc(k.index_set.sem, 1)
                    act.activation(k.table_index[:, bass.ds(c * Q, Q)], ring[:, place, :, F].bitcast(I32), ACT.Copy)
                    act.activation(rows[:].rearrange("p (q f) -> p q f", f=F), ring[:, place, :, 0:F], ACT.Copy
                                   ).then_inc(k.rows_ready.sem, 1)
                    act.wait_ge(*k.rows_ready.at(c + 1))
                    act.sem_inc(k.ring_free[place].sem, 1)
                    act.wait_ge(*k.n_columns.at(c + 1))
                    act.activation(n.kept[:], n_columns[:], ACT.Copy).then_inc(k.n_columns_kept.sem, 1)
                    ln_square(act, k, k.n_ln, c, n.ln)
                    act.wait_ge(*k.scanned.at(c + 1))
                    act.activation(k.sums0[:, bass.ds(c * SPAN, SPAN)], s.sums[:], ACT.Copy)
                    ln_square(act, k, k.e_ln, c, te)
                    ln_root(act, k, k.n_ln, c, n.ln)
                    ln_root(act, k, k.e_ln, c, te)

            @block.tensor
            def _(pe):
                for c, place, i in chunks(pe, NC):
                    pe.wait_ge(*k.n_rows.at(c + 1))
                    for part in range(4):
                        last = pe.transpose(n_columns[:, part * P:(part + 1) * P],
                                            n.rows[:].rearrange("p n f -> p (n f)")[:, part * P:(part + 1) * P], k.ident[:])
                    last.then_inc(k.n_columns.sem, 1)
                    pe.wait_ge(*k.rows_ready.at(c + 1))
                    pe_turn(pe, k, rows, columns).then_inc(k.columns_ready.sem, 1)
                    pe.wait_ge(*k.n_columns_kept.at(c + 1))
                    for part in range(4):
                        pe.matmul(n_projected[:, part * P:(part + 1) * P], n.kept[:, part * P:(part + 1) * P], k.w1[:],
                                  start=True, stop=False)
                        last = pe.matmul(n_projected[:, part * P:(part + 1) * P], k.ones_row[:],
                                         k.b1_row[:, part * P:(part + 1) * P], start=False, stop=True)
                    last.then_inc(k.n_projected.sem, 1)
                    pe_carry(pe, k, s, c, s.sums[:, SPAN - 1:SPAN], carry)
                    pe.wait_ge(*k.scanned.at(c + 1))
                    for h in range(HALVES):
                        last = pe.matmul(projected[:, h * P:(h + 1) * P], s.sums[:, h * P:(h + 1) * P],
                                         k.w0[:], start=True, stop=True)
                    last.then_inc(k.projected.sem, 1)

            @block.vector
            def _(dve):
                order = k.dve
                order.enter(dve)
                order.settle(dve.memset(s.sums[:], 0.0))
                for place in range(RING):
                    order.settle(dve.memset(out[:, place, :, F], 0.0))
                order.close()
                for c, place, i in chunks(dve, NC):
                    order.enter(dve, c, 6)
                    dve_scan_alone(dve, k, s, c, columns)
                    dve.wait_ge(*k.n_projected.at(c + 1))
                    dve.wait_ge(*k.n_stored[place].at(2 * (i + 1)))
                    order.settle(dve.tensor_tensor(n.x[:, place, :], n.x[:, place, :], n_projected[:], ALU.add))
                    ln_centre(dve, k, k.n_ln, n.x[:, place, :].rearrange("p (n f) -> p n f", f=F), NODE_COLS, n.ln)
                    dve_scan(dve, k, c, columns, carry, s.sums[:])
                    ln_variance(dve, k, k.n_ln, c, n.ln)
                    dve.wait_ge(*k.projected.at(c + 1))
                    order.settle(dve.tensor_tensor(x1[:].rearrange("p q f -> p (q f)"), flat(k.state[:, bass.ds(c, 1), :]),
                                                   projected, ALU.add))
                    ln_centre(dve, k, k.e_ln, x1[:], Q, te)
                    ln_scale(dve, k, k.n_ln, c, NODE_COLS, n.ln, n.out[:, place, :, :]).then_inc(k.n_out.sem, 1)
                    ln_variance(dve, k, k.e_ln, c, te)
                    dve.wait_ge(*k.e_stored[place].at(i + 1))
                    ln_scale(dve, k, k.e_ln, c, Q, te, out[:, place, :, 0:F]).then_inc(k.e_out.sem, 1)
                    order.leave()
                order.close(NC)

            @block.sync
            def _(sp):
                def fetch(c, place):
                    sp.dma_start(n.x[:, place, :], node_rows(d["x"], c, k.NP)).then_inc(k.n_loaded[place].sem, 16)
                    sp.dma_start(h_in[:, place, :, :].rearrange("p n f -> p (n f)"), node_rows(k.t01, c, k.NP)
                                 ).then_inc(k.n_loaded[place].sem, 16)

                for place in range(RING):
                    sp.sem_inc(k.n_stored[place].sem, 32)
                    sp.sem_inc(k.e_stored[place].sem, 16)
                    fetch(place, place)
                for c, place, i, ahead in chunks_ahead(sp, NC):
                    sp.wait_ge(*k.n_out.at(c + 1))
                    sp.dma_start(node_rows(k.xa, c, k.NP), n.x[:, place, :]).then_inc(k.n_stored[place].sem, 16)
                    sp.dma_start(node_rows(k.t2, c, k.NP), n.out[:, place, :, :].rearrange("p n f -> p (n f)")
                                 ).then_inc(k.n_stored[place].sem, 16)
                    sp.wait_ge(*k.e_out.at(c + 1))
                    sp.dma_start(edge_rows(k.t01, k.NP, c), out[:, place, :, :].rearrange("p q f -> p (q f)")
                                 ).then_inc(k.e_stored[place].sem, 16)
                    if ahead:
                        sp.wait_ge(*k.n_stored[place].at(2 * (i + 2)))
                        fetch(c + RING, place)
                wait_twice(sp, k.n_stored, NC, 1)
                wait_ring(sp, k.e_stored, NC, 1)
    close_ring(k.gathered, NC)
    close_ring(k.ring_free, NC, 1)
    for signal in (k.index_set, k.n_rows, k.rows_ready, k.n_columns, k.n_columns_kept, k.n_projected, k.n_out, k.e_out,
                   k.projected):
        signal.close(NC)
    close_sums(k)
    ln_close(k.n_ln, NC)
    ln_close(k.e_ln, NC)
    close_ring(k.n_loaded, NC)
    close_ring(k.n_loaded, NC)
    close_ring(k.n_stored, NC, 1)
    close_ring(k.n_stored, NC, 1)
    close_ring(k.e_stored, NC, 1)


def wait_twice(eng, signals, n, more=0):
    for place, s in enumerate(signals):
        eng.wait_ge(*s.at(2 * (len(range(place, n, RING)) + more)))


def close_sums(k):
    for signal in (k.columns_ready, k.scanned_alone, k.carried, k.scanned):
        signal.close(k.NC)


def pe_project(pe, sums, weight, out):
    for h in range(HALVES):
        last = pe.matmul(out[:, h * P:(h + 1) * P], sums[:, h * P:(h + 1) * P], weight[:], start=True, stop=True)
    return last


def layer1_logits(k):
    nc, d, NC = k.nc, k.d, k.NC
    with ExitStack() as ctx:
        sb = allocator(k, ctx, "l1a")
        ring = sb("ring", [P, RING, Q, F + 1])
        index_ring = sb("index_ring", [P, RING, Q], U32)
        rows = sb("rows", [P, SPAN])
        goes_on = sb("goes_on", [P, SPAN], BF16)
        ends = sb("ends", [P, SPAN])
        x1 = sb("x1", [P, Q, F])
        h1 = sb("h1", [P, Q, F])
        kept = sb("kept", [P, 2 * SPAN])
        hidden = sb("hidden", [P, 2, 2 * SPAN])
        attr = sb("attr", [P, RING, 2 * Q, F])
        gap = sb("gap", [P, RING, 2 * Q, F])
        top = sb("top", [P, 2 * Q])
        s = SumTiles(sb)
        t = NormTiles(sb, "ln", Q)
        carry, projected, both = k.bank[0][:, 0:1], k.bank[1][:, 0:SPAN], k.bank[2]
        en, z, own, logit = k.bank[3], k.bank[4], k.bank[5][:, 0:SPAN], k.bank[6][:, 0:2 * Q]
        REV = NC - 1

        with nc.Block() as block:
            @block.gpsimd
            def _(pool):
                for m, place, i in chunks(pool, NC):
                    pool.wait_ge(*k.index_set.at(m + 1))
                    pool.wait_ge(*k.ring_free[place].at(i + 1))
                    gather(pool, k, k.t01, ring, index_ring, place)

            @block.scalar
            def _(act):
                start_ring(act, k, k.table_index, index_ring, REV)
                for place in range(RING):
                    act.sem_inc(k.ring_free[place].sem, 1)
                for m, place, i, ahead in chunks_ahead(act, NC):
                    c = REV - m
                    act.wait_ge(*k.gathered[place].at(i + 1))
                    if ahead:
                        act_index(act, k, k.table_index, index_ring, m + RING, place, REV).then_inc(k.index_set.sem, 1)
                    act.activation(rows[:].rearrange("p (q f) -> p q f", f=F), ring[:, place, :, 0:F], ACT.Copy
                                   ).then_inc(k.rows_ready.sem, 1)
                    act.wait_ge(*k.rows_ready.at(m + 1))
                    act.sem_inc(k.ring_free[place].sem, 1)
                    ln_square(act, k, k.e_ln, m, t)
                    ln_root(act, k, k.e_ln, m, t)
                    act.wait_ge(*k.e_columns.at(m + 1))
                    act.activation(kept[:], both[:], ACT.Copy).then_inc(k.e_columns_kept.sem, 1)
                    act.wait_ge(*k.e_hidden.at(m + 1))
                    act.activation(hidden[:, 0, :], z[:], ACT.Identity, bias=k.bz[:, 0:1])
                    act.activation(hidden[:, 1, :], z[:], ACT.Relu, bias=k.bz[:, 0:1]).then_inc(k.e_hidden_kept.sem, 1)
                    act.wait_ge(*k.e_logits.at(m + 1))
                    planes = k.logits[:].rearrange("p (l b h) n -> p l b h n", l=2, b=2)
                    for b in range(HALVES):
                        act.activation(planes[:, :, b, :, bass.ds(c * 2, 2)].rearrange("p l h j -> p j l h"),
                                       logit[:, b * Q:(b + 1) * Q].rearrange("p (j l h) -> p j l h", j=2, l=2), ACT.Copy)

            @block.tensor
            def _(pe):
                for m, place, i in chunks(pe, NC):
                    pe.wait_ge(*k.scanned_alone.at(m + 1))
                    pe.matmul(carry, s.carry[:, 0, :], s.alone[:, 0:1], start=True, stop=False)
                    pe.matmul(carry, s.carry[:, 1, :], s.sums[:, 0:1], start=False, stop=True).then_inc(k.carried.sem, 1)
                    pe.wait_ge(*k.scanned.at(m + 1))
                    pe_project(pe, s.sums, k.w0, projected).then_inc(k.projected.sem, 1)
                    pe.wait_ge(*k.rows_ready.at(m + 1))
                    pe_turn(pe, k, rows, both[:, SPAN:2 * SPAN])
                    pe.wait_ge(*k.e_out.at(m + 1))
                    pe_turn(pe, k, h1[:].rearrange("p q f -> p (q f)"), both[:, 0:SPAN]).then_inc(k.e_columns.sem, 1)
                    pe.wait_ge(*k.e_columns_kept.at(m + 1))
                    for j in range(2):
                        pe.matmul(z[:, j * SPAN:(j + 1) * SPAN], k.w2s[:, j * P:(j + 1) * P], kept[:, SPAN:2 * SPAN],
                                  start=True, stop=False)
                        last = pe.matmul(z[:, j * SPAN:(j + 1) * SPAN], k.w2d[:, j * P:(j + 1) * P], kept[:, 0:SPAN],
                                         start=False, stop=True)
                    last.then_inc(k.e_hidden.sem, 1)
                    for h in range(HALVES):
                        at = slice(h * 2 * P, (h + 1) * 2 * P)
                        pe.matmul(en[:, at], kept[:, SPAN + h * P:SPAN + (h + 1) * P], k.w2s[:], start=True, stop=False)
                        last = pe.matmul(en[:, at], k.ones_row[:], k.b2s_row[:, at], start=False, stop=True)
                    last.then_inc(k.e_en.sem, 1)
                    for h in range(HALVES):
                        at = slice(h * P, (h + 1) * P)
                        pe.matmul(own[:, at], kept[:, at], k.w1[:], start=True, stop=False)
                        last = pe.matmul(own[:, at], k.ones_row[:], k.b1_row[:, at], start=False, stop=True)
                    last.then_inc(k.e_state.sem, 1)
                    pe.wait_ge(*k.e_hidden_kept.at(m + 1))
                    for h in range(HALVES):
                        for j in range(2):
                            for part in range(2):
                                last = pe.matmul(logit[:, h * Q + j * 4:h * Q + j * 4 + 4],
                                                 hidden[:, part, j * SPAN + h * P:j * SPAN + (h + 1) * P],
                                                 k.attn_parts[:, part, :], start=(part == 0), stop=(part == 1))
                    last.then_inc(k.e_logits.sem, 1)

            @block.vector
            def _(dve):
                order = k.dve
                order.enter(dve)
                order.settle(dve.memset(s.sums[:], 0.0))
                order.close()
                for m, place, i in chunks(dve, NC):
                    order.enter(dve, m, 8)
                    c = REV - m
                    groups = spread(k.last_all[:, bass.ds(c, 1), :].rearrange("p o g -> p (o g)"), GROUPS, F)
                    for n, (pattern, col) in enumerate(((BACKWARD, c), (BACKWARD_AFTER, c + 1))):
                        dve.scalar_tensor_tensor(s.carry[:, n, :].rearrange("p (g f) -> p g f", g=GROUPS), groups,
                                                 k.first_col[:, bass.ds(col, 1)],
                                                 k.carry_base[:, pattern, :].rearrange("p (g f) -> p g f", g=GROUPS),
                                                 ALU.is_equal, ALU.mult)
                    after = flat(k.same[:, bass.ds(c, 1), 1:SPAN + 1])
                    order.note(dve.tensor_copy(goes_on[:], after))
                    order.settle(dve.scalar_tensor_tensor(ends[:], after, 0.0, k.sums0[:, bass.ds(c * SPAN, SPAN)],
                                                          ALU.is_equal, ALU.mult))
                    dve.tensor_tensor_scan(s.alone[:, ::-1], goes_on[:, ::-1], ends[:, ::-1], 0.0, ALU.mult, ALU.add
                                           ).then_inc(k.scanned_alone.sem, 1)
                    dve.wait_ge(*k.carried.at(m + 1))
                    dve.tensor_tensor_scan(s.sums[:, ::-1], goes_on[:, ::-1], ends[:, ::-1], carry, ALU.mult, ALU.add
                                           ).then_inc(k.scanned.sem, 1)
                    state = flat(k.state[:, bass.ds(c, 1), :])
                    dve.wait_ge(*k.projected.at(m + 1))
                    order.settle(dve.tensor_tensor(x1[:].rearrange("p q f -> p (q f)"), state, projected, ALU.add))
                    ln_centre(dve, k, k.e_ln, x1[:], Q, t)
                    ln_variance(dve, k, k.e_ln, m, t)
                    ln_scale(dve, k, k.e_ln, m, Q, t, h1[:]).then_inc(k.e_out.sem, 1)
                    dve.wait_ge(*k.e_loaded[place].at(i + 1))
                    dve.wait_ge(*k.e_stored[place].at(i + 1))
                    dve.wait_ge(*k.e_en.at(m + 1))
                    order.settle(dve.tensor_tensor(attr[:, place, :, :], attr[:, place, :, :],
                                                   en[:].rearrange("p (n f) -> p n f", f=F), ALU.mult))
                    order.settle(dve.tensor_reduce(top[:], attr[:, place, :, :], AX, ALU.max))
                    dve.tensor_tensor(gap[:, place, :, :], attr[:, place, :, :], spread(top[:], 2 * Q, F), ALU.subtract
                                      ).then_inc(k.e_gap.sem, 1)
                    dve.wait_ge(*k.e_state.at(m + 1))
                    order.note(dve.tensor_tensor(state, x1[:].rearrange("p q f -> p (q f)"), own, ALU.add))
                    order.leave()
                order.close(NC)

            @block.sync
            def _(sp):
                def fetch(m, place):
                    sp.dma_start(attr[:, place, :, :].rearrange("p n f -> p (n f)"), edge_rows(k.attr_sorted, 0, m * -1 + REV)
                                 ).then_inc(k.e_loaded[place].sem, 16)

                sp.wait_ge(*k.attr_ready.at(1))
                for place in range(RING):
                    sp.sem_inc(k.e_stored[place].sem, 16)
                    fetch(place, place)
                for m, place, i, ahead in chunks_ahead(sp, NC):
                    sp.wait_ge(*k.e_gap.at(m + 1))
                    sp.dma_start(edge_rows(k.gap_rows, 0, m * -1 + REV), gap[:, place, :, :].rearrange("p n f -> p (n f)")
                                 ).then_inc(k.e_stored[place].sem, 16)
                    if ahead:
                        fetch(m + RING, place)
                wait_ring(sp, k.e_stored, NC, 1)
    close_ring(k.gathered, NC)
    close_ring(k.ring_free, NC, 1)
    for signal in (k.index_set, k.rows_ready, k.e_columns, k.e_columns_kept, k.e_hidden, k.e_hidden_kept, k.e_logits,
                   k.e_en, k.e_state, k.e_out, k.e_gap, k.projected, k.scanned_alone, k.carried, k.scanned):
        signal.close(NC)
    ln_close(k.e_ln, NC)
    close_ring(k.e_loaded, NC)
    close_ring(k.e_stored, NC, 1)


def layer1_softmax(k):
    nc, NC, SP = k.nc, k.NC, k.SP
    with ExitStack() as ctx:
        sb = allocator(k, ctx, "l1s")
        logit = sb("logit", [SP, 2, LINE])
        top = sb("top", [SP, LINE])
        guarded = sb("guarded", [SP, LINE])
        finite = sb("finite", [SP, LINE], I32)
        raised = sb("raised", [SP, 2, LINE])
        total = sb("total", [SP, LINE])
        alpha = sb("alpha", [SP, 2, LINE])
        with nc.Block() as block:
            @block.vector
            def _(dve):
                order = k.dve
                order.enter(dve)
                for h in range(2):
                    dve.wait_ge(*k.turned_used.at(h + 1))
                    dve_line_total(dve, k, logit[:, h, :], ALU.max, top[:], 2 * h)
                    order.settle(dve.tensor_scalar(guarded[:], top[:], 0.0, None, ALU.mult))
                    order.settle(dve.tensor_scalar(finite[:], guarded[:], 0.0, None, ALU.is_equal))
                    order.settle(dve.memset(guarded[:], 0.0))
                    order.settle(dve.copy_predicated(guarded[:], finite[:], top[:]))
                    dve.tensor_tensor(logit[:, h, :], logit[:, h, :], guarded[:], ALU.subtract).then_inc(k.weighted.sem, 1)
                for h in range(2):
                    dve.wait_ge(*k.raised.at(h + 1))
                    dve_line_total(dve, k, raised[:, h, :], ALU.add, total[:], 4 + 2 * h)
                    order.settle(dve.tensor_scalar(total[:], total[:], 1e-9, None, ALU.max))
                    order.settle(dve.reciprocal(total[:], total[:]))
                    dve.tensor_tensor(alpha[:, h, :], raised[:, h, :], total[:], ALU.mult).then_inc(k.summed.sem, 1)

            @block.scalar
            def _(act):
                for h in range(2):
                    act.wait_ge(*k.turned.at(4 * (h + 1)))
                    act.activation(logit[:, h, :], k.bank[3 + h][0:SP, :], ACT.Copy).then_inc(k.turned_used.sem, 1)
                for h in range(2):
                    act.wait_ge(*k.weighted.at(h + 1))
                    act.activation(raised[:, h, :], logit[:, h, :], ACT.Exp).then_inc(k.raised.sem, 1)
                view = k.alpha[:].rearrange("p c (b j l h) -> p c b j l h", b=2, j=2, l=2)
                for h in range(2):
                    for part in range(4):
                        gl, b, n = part // 2, part % 2, 4 * h + part
                        act.wait_ge(*k.turned.at(8 + n + 1))
                        act.activation(view[:, :, b, :, gl, h], k.bank[5 + n % 2][:, 0:SP].rearrange("p (c j) -> p c j", j=2),
                                       ACT.Copy).then_inc(k.turned_used.sem, 1)

            @block.tensor
            def _(pe):
                for h in range(2):
                    for part in range(4):
                        pe.transpose(k.bank[3 + h][0:SP, part * P:(part + 1) * P], k.logits[:, 2 * part + h, :], k.ident[:]
                                     ).then_inc(k.turned.sem, 1)
                for turn, op in enumerate((ALU.max, ALU.max, ALU.add, ALU.add)):
                    pe_line_total(pe, k, op, 2 * turn)
                for h in range(2):
                    pe.wait_ge(*k.summed.at(h + 1))
                    for part in range(4):
                        n = 4 * h + part
                        if n >= 2:
                            pe.wait_ge(*k.turned_used.at(2 + n - 1))
                        pe.transpose(k.bank[5 + n % 2][:, 0:SP], alpha[:, h, part * P:(part + 1) * P],
                                     k.ident[0:SP, 0:SP]).then_inc(k.turned.sem, 1)
    k.line_scanned.close(8)
    k.line_carried.close(8)
    k.turned.close(16)
    k.turned_used.close(10)
    for signal in (k.weighted, k.raised, k.summed):
        signal.close(2)
    k.dve.close()


def layer1_sums(k):
    nc, NC = k.nc, k.NC
    with ExitStack() as ctx:
        sb = allocator(k, ctx, "l1b")
        gap = sb("gap", [P, RING, 2 * Q, F])
        scaled = sb("scaled", [P, 2 * Q, F])
        raised = sb("raised", [P, 2 * Q, F])
        msg = sb("msg", [P, HALVES, 2, GROUPS, F])
        total = sb("total", [P, 2 * Q])
        inv = sb("inv", [P, 2 * Q])
        var = sb("var", [P, Q])
        power = sb("power", [P, Q])
        x2 = sb("x2", [P, Q, F])
        out = sb("out", [P, RING, Q, F])
        s = SumTiles(sb)
        t = NormTiles(sb, "ln", Q)
        columns, carry, projected = k.bank[0][:, 0:SPAN], k.bank[1][:, SPAN:SPAN + 1], k.bank[1][:, 0:SPAN]

        with nc.Block() as block:
            @block.gpsimd
            def _(pool):
                for place in range(RING):
                    pool.sem_inc(k.ring_free[place].sem, 1)
                pool.memset(power[:], -0.5).then_inc(k.prepared.sem, 1)
                pool.wait_ge(*k.prepared.at(1))
                for c, place, i in chunks(pool, NC):
                    pool.wait_ge(*k.e_loaded[place].at(i + 1))
                    pool.tensor_tensor(scaled[:], gap[:, place, :, :],
                                       spread(flat(k.alpha[:, bass.ds(c, 1), :]), 2 * Q, F), ALU.mult
                                       ).then_inc(k.weighted.sem, 1)
                    pool.wait_ge(*k.summed.at(c + 1))
                    for b in range(HALVES):
                        last = pool.tensor_tensor(msg[:, b, :, :, :].rearrange("p h g f -> p g h f"),
                                                  raised[:, b * Q:(b + 1) * Q, :].rearrange("p (g h) f -> p g h f", h=2),
                                                  inv[:, b * Q:(b + 1) * Q].rearrange("p (g h) -> p g h", h=2).unsqueeze(3)
                                                  .to_broadcast([P, GROUPS, 2, F]), ALU.mult)
                    last.then_inc(k.rows_ready.sem, 1)
                    pool.wait_ge(*k.e_ln.varied.at(c + 1))
                    pool.tensor_tensor(t.inv, var[:], power[:], ALU.pow).then_inc(k.e_ln.rooted.sem, 1)

            @block.scalar
            def _(act):
                for c, place, i in chunks(act, NC):
                    act.wait_ge(*k.weighted.at(c + 1))
                    act.activation(raised[:], scaled[:], ACT.Exp).then_inc(k.raised.sem, 1)
                    act.wait_ge(*k.e_ln.centred.at(c + 1))
                    act.activation(flat(k.state[:, bass.ds(c, 1), :]), x2[:].rearrange("p q f -> p (q f)"), ACT.Copy)
                    ln_square(act, k, k.e_ln, c, t)

            @block.tensor
            def _(pe):
                for c, place, i in chunks(pe, NC):
                    pe.wait_ge(*k.rows_ready.at(c + 1))
                    for b in range(HALVES):
                        for h in range(2):
                            last = pe.matmul(columns[:, b * P:(b + 1) * P], msg[:, b, h, :, :].rearrange("p g f -> p (g f)"),
                                             k.ident[:], start=(h == 0), stop=(h == 1))
                    last.then_inc(k.columns_ready.sem, 1)
                    pe_carry(pe, k, s, c, s.sums[:, SPAN - 1:SPAN], carry)
                    pe.wait_ge(*k.scanned.at(c + 1))
                    pe_project(pe, s.sums, k.w1, projected).then_inc(k.projected.sem, 1)

            @block.vector
            def _(dve):
                order = k.dve
                order.enter(dve)
                order.settle(dve.memset(s.sums[:], 0.0))
                order.close()
                for c, place, i in chunks(dve, NC):
                    order.enter(dve, c, 4)
                    dve.wait_ge(*k.raised.at(c + 1))
                    order.settle(dve.tensor_reduce(total[:], raised[:], AX, ALU.add))
                    dve.reciprocal(inv[:], total[:]).then_inc(k.summed.sem, 1)
                    dve_scan_alone(dve, k, s, c, columns)
                    dve_scan(dve, k, c, columns, carry, s.sums[:])
                    dve.wait_ge(*k.projected.at(c + 1))
                    order.settle(dve.tensor_tensor(x2[:].rearrange("p q f -> p (q f)"),
                                                   flat(k.state[:, bass.ds(c, 1), :]), projected, ALU.add))
                    ln_centre(dve, k, k.e_ln, x2[:], Q, t)
                    dve.wait_ge(*k.e_ln.squared.at(c + 1))
                    order.settle(dve.tensor_reduce(t.var, t.squares, AX, ALU.add))
                    dve.tensor_scalar(var[:], t.var, 1.0 / F, EPS, ALU.mult, ALU.add).then_inc(k.e_ln.varied.sem, 1)
                    dve.wait_ge(*k.e_ln.rooted.at(c + 1))
                    dve.wait_ge(*k.e_stored[place].at(i + 1))
                    dve.scalar_tensor_tensor(out[:, place, :, :], t.centred, 0.0, spread(t.inv, Q, F), ALU.max, ALU.mult
                                             ).then_inc(k.e_out.sem, 1)
                    order.leave()
                order.close(NC)

            @block.sync
            def _(sp):
                def fetch(c, place):
                    sp.dma_start(gap[:, place, :, :].rearrange("p n f -> p (n f)"), edge_rows(k.gap_rows, 0, c)
                                 ).then_inc(k.e_loaded[place].sem, 16)

                for place in range(RING):
                    sp.sem_inc(k.e_stored[place].sem, 16)
                    fetch(place, place)
                for c, place, i, ahead in chunks_ahead(sp, NC):
                    if ahead:
                        sp.wait_ge(*k.weighted.at(c + 1))
                        fetch(c + RING, place)
                    sp.wait_ge(*k.e_out.at(c + 1))
                    sp.dma_start(edge_rows(k.t2, k.NP, c), out[:, place, :, :].rearrange("p q f -> p (q f)")
                                 ).then_inc(k.e_stored[place].sem, 16)
                wait_ring(sp, k.e_stored, NC, 1)
    for signal in (k.weighted, k.summed, k.rows_ready, k.raised, k.projected, k.e_out):
        signal.close(NC)
    for signal in k.ring_free:
        signal.close(1)
    k.prepared.close(1)
    close_sums(k)
    ln_close(k.e_ln, NC)
    close_ring(k.e_loaded, NC)
    close_ring(k.e_stored, NC, 1)


def dve_average(dve, k, c, place, i, ring, rows):
    dve.wait_ge(*k.gathered[place].at(i + 1))
    dve.tensor_tensor(rows[:].rearrange("p (q f) -> p q f", f=F), ring[:, place, :, :],
                      spread(flat(k.inv_deg[:, bass.ds(c, 1), :]), Q, F), ALU.mult).then_inc(k.rows_ready.sem, 1)


def act_next_index(act, k, index, index_ring, c, place, i, ahead):
    act.wait_ge(*k.gathered[place].at(i + 1))
    if ahead:
        act_index(act, k, index, index_ring, c + RING, place).then_inc(k.index_set.sem, 1)


def layer2_first(k):
    nc, d, NC = k.nc, k.d, k.NC
    with ExitStack() as ctx:
        sb = allocator(k, ctx, "l2a")
        ring = sb("ring", [P, RING, Q, F])
        index_ring = sb("index_ring", [P, RING, Q], U32)
        rows = sb("rows", [P, SPAN])
        h2 = sb("h2", [P, RING, SPAN])
        kept = sb("kept", [P, SPAN])
        hidden = sb("hidden", [P, 2, SPAN])
        xnew = sb("xnew", [P, Q, F])
        out = sb("out", [P, RING, Q, F])
        s = SumTiles(sb)
        n_h2 = sb("n_h2", [P, RING, 4 * P])
        n_x = sb("n_x", [P, RING, NODE_COLS, F])
        n_kept = sb("n_kept", [P, 4 * P])
        n_hidden = sb("n_hidden", [P, 2, 4 * P])
        n_out = sb("n_out", [P, RING, NODE_COLS, F])
        columns, carry = k.bank[0][:, 0:SPAN], k.bank[0][:, SPAN:SPAN + 1]
        turned, e_hidden, e_rows = k.bank[1][:, 0:SPAN], k.bank[2], k.bank[3]
        n_columns, n_hid, n_rows = k.bank[4], (k.bank[5], k.bank[6]), (k.bank[7], k.bank[4])

        with nc.Block() as block:
            @block.gpsimd
            def _(pool):
                for c, place, i in chunks(pool, NC):
                    pool.wait_ge(*k.index_set.at(c + 1))
                    pool.wait_ge(*k.ring_free[place].at(i + 1))
                    gather(pool, k, k.t2, ring, index_ring, place)

            @block.scalar
            def _(act):
                start_ring(act, k, k.table_index, index_ring)
                for place in range(RING):
                    act.sem_inc(k.ring_free[place].sem, 1)
                for c, place, i, ahead in chunks_ahead(act, NC):
                    act.wait_ge(*k.n_columns.at(c + 1))
                    act.activation(n_kept[:], n_columns[:], ACT.Copy).then_inc(k.n_columns_kept.sem, 1)
                    act_next_index(act, k, k.table_index, index_ring, c, place, i, ahead)
                    act.wait_ge(*k.rows_ready.at(c + 1))
                    act.sem_inc(k.ring_free[place].sem, 1)
                    act.wait_ge(*k.e_columns.at(c + 1))
                    act.activation(kept[:], turned, ACT.Copy).then_inc(k.e_columns_kept.sem, 1)
                    act.wait_ge(*k.n_hidden.at(c + 1))
                    for j in range(2):
                        last = act.activation(n_hidden[:, j, :], n_hid[j][:], ACT.Relu, bias=k.b1_col[:])
                    last.then_inc(k.n_hidden_kept.sem, 1)
                    act.wait_ge(*k.e_hidden.at(c + 1))
                    act.activation(hidden[:].rearrange("p j n -> p (j n)"), e_hidden[:], ACT.Relu, bias=k.b1_col[:]
                                   ).then_inc(k.e_hidden_kept.sem, 1)
                    act.wait_ge(*k.n_out.at(c + 1))
                    act.wait_ge(*k.n_stored[place].at(2 * (i + 1)))
                    for part in range(2):
                        last = act.activation(n_out[:, place, 8 * part:8 * part + 8, :],
                                              n_rows[part][:].rearrange("p (n f) -> p n f", f=2 * F)[:, :, 0:F], ACT.Copy)
                    last.then_inc(k.n_out2.sem, 1)
                    act.wait_ge(*k.e_state.at(c + 1))
                    act.wait_ge(*k.e_stored[place].at(i + 1))
                    act.activation(out[:, place, :, :], e_rows[:].rearrange("p (n f) -> p n f", f=2 * F)[:, :, 0:F], ACT.Copy
                                   ).then_inc(k.e_out.sem, 1)

            @block.tensor
            def _(pe):
                for c, place, i in chunks(pe, NC):
                    pe.wait_ge(*k.n_loaded[place].at(2 * (i + 1)))
                    for part in range(4):
                        last = pe.transpose(n_columns[:, part * P:(part + 1) * P], n_h2[:, place, part * P:(part + 1) * P],
                                            k.ident[:])
                    last.then_inc(k.n_columns.sem, 1)
                    pe.wait_ge(*k.e_loaded[place].at(i + 1))
                    pe_turn(pe, k, h2[:, place, :], turned).then_inc(k.e_columns.sem, 1)
                    pe.wait_ge(*k.n_columns_kept.at(c + 1))
                    for j in range(2):
                        last = pe.matmul(n_hid[j][:], k.w1r[:, j * P:(j + 1) * P], n_kept[:], start=True, stop=True)
                    last.then_inc(k.n_hidden.sem, 1)
                    pe.wait_ge(*k.rows_ready.at(c + 1))
                    pe_turn(pe, k, rows, columns).then_inc(k.columns_ready.sem, 1)
                    pe_carry(pe, k, s, c, s.sums[:, SPAN - 1:SPAN], carry)
                    pe.wait_ge(*k.n_hidden_kept.at(c + 1))
                    for part in range(4):
                        for j in range(2):
                            last = pe.matmul(n_rows[part // 2][:, (part % 2 * 2 + j) * P:(part % 2 * 2 + j + 1) * P],
                                             n_hidden[:, j, part * P:(part + 1) * P], k.w2lr[:], start=True, stop=True)
                    last.then_inc(k.n_projected.sem, 1)
                    pe.wait_ge(*k.e_columns_kept.at(c + 1))
                    pe.wait_ge(*k.scanned.at(c + 1))
                    for j in range(2):
                        pe.matmul(e_hidden[:, j * SPAN:(j + 1) * SPAN], k.w1l[:, j * P:(j + 1) * P], s.sums[:],
                                  start=True, stop=False)
                        last = pe.matmul(e_hidden[:, j * SPAN:(j + 1) * SPAN], k.w1r[:, j * P:(j + 1) * P], kept[:],
                                         start=False, stop=True)
                    last.then_inc(k.e_hidden.sem, 1)
                    pe.wait_ge(*k.e_hidden_kept.at(c + 1))
                    for h in range(HALVES):
                        for j in range(2):
                            last = pe.matmul(e_rows[:, (2 * h + j) * P:(2 * h + j + 1) * P], hidden[:, j, h * P:(h + 1) * P],
                                             k.w2lr[:], start=True, stop=True)
                    last.then_inc(k.e_projected.sem, 1)
                    pe.wait_ge(*k.n_out2.at(c + 1))

            @block.vector
            def _(dve):
                order = k.dve
                order.enter(dve)
                order.settle(dve.memset(s.sums[:], 0.0))
                order.close()
                for c, place, i in chunks(dve, NC):
                    order.enter(dve, c, 2)
                    dve_average(dve, k, c, place, i, ring, rows)
                    dve_scan_alone(dve, k, s, c, columns)
                    dve_scan(dve, k, c, columns, carry, s.sums[:])
                    dve.wait_ge(*k.n_projected.at(c + 1))
                    for part in range(2):
                        at = n_x[:, place, 8 * part:8 * part + 8, :]
                        last = dve.tensor_tensor(at, at, n_rows[part][:].rearrange("p (n f) -> p n f", f=2 * F)[:, :, F:2 * F],
                                                 ALU.add)
                    order.settle(last)
                    dve.tensor_tensor(n_x[:, place, :, :], n_x[:, place, :, :],
                                      k.b2[:].unsqueeze(1).to_broadcast([P, NODE_COLS, F]), ALU.add).then_inc(k.n_out.sem, 1)
                    dve.wait_ge(*k.e_projected.at(c + 1))
                    order.settle(dve.tensor_tensor(xnew[:], e_rows[:].rearrange("p (n f) -> p n f", f=2 * F)[:, :, F:2 * F],
                                                   k.b2[:].unsqueeze(1).to_broadcast([P, Q, F]), ALU.add))
                    state = flat(k.state[:, bass.ds(c, 1), :])
                    dve.tensor_tensor(state, state, xnew[:].rearrange("p q f -> p (q f)"), ALU.add
                                      ).then_inc(k.e_state.sem, 1)
                    order.leave()
                order.close(NC)

            @block.sync
            def _(sp):
                def fetch(c, place):
                    sp.dma_start(n_x[:, place, :, :].rearrange("p n f -> p (n f)"), node_rows(k.xa, c, k.NP)
                                 ).then_inc(k.n_loaded[place].sem, 16)
                    sp.dma_start(n_h2[:, place, :], node_rows(k.t2, c, k.NP)).then_inc(k.n_loaded[place].sem, 16)
                    sp.dma_start(h2[:, place, :], edge_rows(k.t2, k.NP, c)).then_inc(k.e_loaded[place].sem, 16)

                for place in range(RING):
                    sp.sem_inc(k.n_stored[place].sem, 32)
                    sp.sem_inc(k.e_stored[place].sem, 16)
                    fetch(place, place)
                for c, place, i, ahead in chunks_ahead(sp, NC):
                    sp.wait_ge(*k.n_out.at(c + 1))
                    sp.dma_start(node_rows(k.xb, c, k.NP), n_x[:, place, :, :].rearrange("p n f -> p (n f)")
                                 ).then_inc(k.n_stored[place].sem, 16)
                    sp.wait_ge(*k.n_out2.at(c + 1))
                    sp.dma_start(node_rows(k.t2b, c, k.NP), n_out[:, place, :, :].rearrange("p n f -> p (n f)")
                                 ).then_inc(k.n_stored[place].sem, 16)
                    sp.wait_ge(*k.e_out.at(c + 1))
                    sp.dma_start(edge_rows(k.t2b, k.NP, c), out[:, place, :, :].rearrange("p q f -> p (q f)")
                                 ).then_inc(k.e_stored[place].sem, 16)
                    if ahead:
                        sp.wait_ge(*k.n_stored[place].at(2 * (i + 2)))
                        fetch(c + RING, place)
                wait_twice(sp, k.n_stored, NC, 1)
                wait_ring(sp, k.e_stored, NC, 1)
    close_ring(k.gathered, NC)
    close_ring(k.ring_free, NC, 1)
    for signal in (k.index_set, k.rows_ready, k.n_columns, k.n_columns_kept, k.e_columns, k.e_columns_kept, k.n_hidden,
                   k.n_hidden_kept, k.e_hidden, k.e_hidden_kept, k.n_out, k.n_out2, k.e_state, k.e_out, k.n_projected,
                   k.e_projected):
        signal.close(NC)
    close_sums(k)
    for _ in range(2):
        close_ring(k.n_loaded, NC)
        close_ring(k.n_stored, NC, 1)
    close_ring(k.e_loaded, NC)
    close_ring(k.e_stored, NC, 1)


def layer2_second(k):
    nc, d, NC = k.nc, k.d, k.NC
    with ExitStack() as ctx:
        sb = allocator(k, ctx, "l2b")
        ring = sb("ring", [P, RING, Q, F])
        index_ring = sb("index_ring", [P, RING, Q], U32)
        rows = sb("rows", [P, SPAN])
        x3 = sb("x3", [P, Q, F])
        h3 = sb("h3", [P, Q, F])
        kept = sb("kept", [P, SPAN])
        out = sb("out", [P, RING, SPAN])
        s = SumTiles(sb)
        te = NormTiles(sb, "lne", Q)
        n_x = sb("n_x", [P, RING, NODE_COLS * F])
        n_h3 = sb("n_h3", [P, NODE_COLS, F])
        n_kept = sb("n_kept", [P, 4 * P])
        n_out = sb("n_out", [P, RING, NODE_COLS * F])
        n_final = sb("n_final", [P, RING, NODE_COLS * F])
        tn = NormTiles(sb, "lnn", NODE_COLS)
        columns, carry, projected = k.bank[0][:, 0:SPAN], k.bank[0][:, SPAN:SPAN + 1], k.bank[1][:, 0:SPAN]
        turned, e_rows, n_columns, n_rows = k.bank[2][:, 0:SPAN], k.bank[3][:, 0:SPAN], k.bank[4], k.bank[5]

        with nc.Block() as block:
            @block.gpsimd
            def _(pool):
                for c, place, i in chunks(pool, NC):
                    pool.wait_ge(*k.index_set.at(c + 1))
                    pool.wait_ge(*k.ring_free[place].at(i + 1))
                    gather(pool, k, k.t2b, ring, index_ring, place)

            @block.scalar
            def _(act):
                start_ring(act, k, k.table_index, index_ring)
                for place in range(RING):
                    act.sem_inc(k.ring_free[place].sem, 1)
                for c, place, i, ahead in chunks_ahead(act, NC):
                    ln_square(act, k, k.n_ln, c, tn)
                    ln_root(act, k, k.n_ln, c, tn)
                    act_next_index(act, k, k.table_index, index_ring, c, place, i, ahead)
                    act.wait_ge(*k.rows_ready.at(c + 1))
                    act.sem_inc(k.ring_free[place].sem, 1)
                    act.wait_ge(*k.n_columns.at(c + 1))
                    act.activation(n_kept[:], n_columns[:], ACT.Copy).then_inc(k.n_columns_kept.sem, 1)
                    ln_square(act, k, k.e_ln, c, te)
                    act.activation(flat(k.state[:, bass.ds(c, 1), :]), x3[:].rearrange("p q f -> p (q f)"), ACT.Copy)
                    ln_root(act, k, k.e_ln, c, te)
                    act.wait_ge(*k.n_projected.at(c + 1))
                    act.wait_ge(*k.n_stored[place].at(2 * (i + 1)))
                    act.activation(n_out[:, place, :], n_rows[:], ACT.Copy).then_inc(k.n_out.sem, 1)
                    act.wait_ge(*k.e_columns.at(c + 1))
                    act.activation(kept[:], turned, ACT.Copy).then_inc(k.e_columns_kept.sem, 1)
                    act.wait_ge(*k.e_projected.at(c + 1))
                    act.wait_ge(*k.e_stored[place].at(i + 1))
                    act.activation(out[:, place, :], e_rows, ACT.Copy).then_inc(k.e_out.sem, 1)

            @block.tensor
            def _(pe):
                for c, place, i in chunks(pe, NC):
                    pe.wait_ge(*k.n_rows.at(c + 1))
                    for part in range(4):
                        last = pe.transpose(n_columns[:, part * P:(part + 1) * P],
                                            n_h3[:].rearrange("p n f -> p (n f)")[:, part * P:(part + 1) * P], k.ident[:])
                    last.then_inc(k.n_columns.sem, 1)
                    pe.wait_ge(*k.rows_ready.at(c + 1))
                    pe_turn(pe, k, rows, columns).then_inc(k.columns_ready.sem, 1)
                    pe_carry(pe, k, s, c, s.sums[:, SPAN - 1:SPAN], carry)
                    pe.wait_ge(*k.scanned.at(c + 1))
                    pe_project(pe, s.sums, k.ident, projected).then_inc(k.projected.sem, 1)
                    pe.wait_ge(*k.n_columns_kept.at(c + 1))
                    for part in range(4):
                        at = slice(part * P, (part + 1) * P)
                        last = pe.matmul(n_rows[:, at], n_kept[:, at], k.w3[:], start=True, stop=True)
                    last.then_inc(k.n_projected.sem, 1)
                    pe.wait_ge(*k.e_en.at(c + 1))
                    pe_turn(pe, k, h3[:].rearrange("p q f -> p (q f)"), turned).then_inc(k.e_columns.sem, 1)
                    pe.wait_ge(*k.e_columns_kept.at(c + 1))
                    pe_project(pe, kept, k.w3, e_rows).then_inc(k.e_projected.sem, 1)

            @block.vector
            def _(dve):
                order = k.dve
                order.enter(dve)
                order.settle(dve.memset(s.sums[:], 0.0))
                order.close()
                for c, place, i in chunks(dve, NC):
                    order.enter(dve, c, 7)
                    dve.wait_ge(*k.n_loaded[place].at(i + 1))
                    ln_centre(dve, k, k.n_ln, n_x[:, place, :].rearrange("p (n f) -> p n f", f=F), NODE_COLS, tn)
                    ln_variance(dve, k, k.n_ln, c, tn)
                    ln_scale(dve, k, k.n_ln, c, NODE_COLS, tn, n_h3[:]).then_inc(k.n_rows.sem, 1)
                    dve_average(dve, k, c, place, i, ring, rows)
                    dve_scan_alone(dve, k, s, c, columns)
                    dve_scan(dve, k, c, columns, carry, s.sums[:])
                    dve.wait_ge(*k.projected.at(c + 1))
                    order.settle(dve.tensor_tensor(x3[:].rearrange("p q f -> p (q f)"),
                                                   flat(k.state[:, bass.ds(c, 1), :]), projected, ALU.add))
                    ln_centre(dve, k, k.e_ln, x3[:], Q, te)
                    ln_variance(dve, k, k.e_ln, c, te)
                    dve.wait_ge(*k.n_out.at(c + 1))
                    dve.wait_ge(*k.n_stored[place].at(2 * (i + 1)))
                    final = n_final[:, place, :]
                    order.settle(dve.tensor_tensor(final.rearrange("p (n f) -> p n f", f=F),
                                                   n_out[:, place, :].rearrange("p (n f) -> p n f", f=F),
                                                   k.b3[:].unsqueeze(1).to_broadcast([P, NODE_COLS, F]), ALU.add))
                    dve.scalar_tensor_tensor(final, final, 0.0, n_x[:, place, :], ALU.max, ALU.add).then_inc(k.n_out2.sem, 1)
                    dve.wait_ge(*k.e_ln.rooted.at(c + 1))
                    order.settle(dve.reciprocal(te.inv, te.dev))
                    order.settle(dve.tensor_tensor(te.inv, te.inv, flat(k.inv_sqrt_deg[:, bass.ds(c, 1), :]), ALU.mult))
                    dve.scalar_tensor_tensor(h3[:], te.centred, 0.0, spread(te.inv, Q, F), ALU.max, ALU.mult
                                             ).then_inc(k.e_en.sem, 1)
                    order.leave()
                order.close(NC)

            @block.sync
            def _(sp):
                def fetch(c, place):
                    sp.dma_start(n_x[:, place, :], node_rows(k.xb, c, k.NP)).then_inc(k.n_loaded[place].sem, 16)

                for place in range(RING):
                    sp.sem_inc(k.n_stored[place].sem, 32)
                    sp.sem_inc(k.e_stored[place].sem, 16)
                    fetch(place, place)
                for c, place, i, ahead in chunks_ahead(sp, NC):
                    sp.wait_ge(*k.n_out.at(c + 1))
                    sp.dma_start(node_rows(k.t3, c, k.NP), n_out[:, place, :]).then_inc(k.n_stored[place].sem, 16)
                    sp.wait_ge(*k.n_out2.at(c + 1))
                    sp.dma_start(node_rows(d["out"], c, k.NP), n_final[:, place, :]).then_inc(k.n_stored[place].sem, 16)
                    if ahead:
                        fetch(c + RING, place)
                    sp.wait_ge(*k.e_out.at(c + 1))
                    sp.dma_start(edge_rows(k.t3, k.NP, c), out[:, place, :]).then_inc(k.e_stored[place].sem, 16)
                wait_twice(sp, k.n_stored, NC, 1)
                wait_ring(sp, k.e_stored, NC, 1)
    close_ring(k.gathered, NC)
    close_ring(k.ring_free, NC, 1)
    for signal in (k.index_set, k.rows_ready, k.n_columns, k.n_columns_kept, k.e_columns, k.e_columns_kept, k.n_rows,
                   k.n_out, k.n_out2, k.e_en, k.e_out, k.n_projected, k.e_projected, k.projected):
        signal.close(NC)
    close_sums(k)
    ln_close(k.n_ln, NC)
    ln_close(k.e_ln, NC)
    for _ in range(2):
        close_ring(k.n_stored, NC, 1)
    close_ring(k.n_loaded, NC)
    close_ring(k.e_stored, NC, 1)


def layer3(k):
    nc, d, NC = k.nc, k.d, k.NC
    with ExitStack() as ctx:
        sb = allocator(k, ctx, "l3")
        ring = sb("ring", [P, RING, Q, F])
        index_ring = sb("index_ring", [P, RING, Q], U32)
        store_ring = sb("store_ring", [P, RING, Q], U32)
        own = sb("own", [P, RING, SPAN])
        t = sb("t", [P, Q, F])
        out = sb("out", [P, RING, Q, F])
        s = SumTiles(sb)
        columns, carry, projected = k.bank[0][:, 0:SPAN], k.bank[0][:, SPAN:SPAN + 1], k.bank[1][:, 0:SPAN]

        with nc.Block() as block:
            @block.gpsimd
            def _(pool):
                def gathers(c, place, i):
                    pool.wait_ge(*k.index_set.at(c + 1))
                    pool.wait_ge(*k.ring_free[place].at(i + 1))
                    gather(pool, k, k.t3, ring, index_ring, place)

                def scatters(c, place):
                    pool.wait_ge(*k.e_out.at(c + 1))
                    pool.sem_inc(k.gather_started.sem, 1)
                    for q in range(Q):
                        pool.indirect_dma_start(
                            out=d["out"], out_offset=bass.IndirectOffsetOnAxis(ap=store_ring[:, place, q:q + 1], axis=0),
                            in_=out[:, place, q, :], in_offset=None, bounds_check=k.NP - 1, oob_is_err=False
                        ).then_inc(k.scattered[place].sem, 16)

                gathers(0, 0, 0)
                turns = (NC - 1) // RING
                assert turns * RING == NC - 1
                with pool.Fori(0, turns) as i:
                    for n in range(RING):
                        c = i * RING + n + 1
                        gathers(c, (n + 1) % RING, i + (n + 1) // RING)
                        scatters(c - 1, n)
                scatters(NC - 1, 0)
                wait_ring(pool, k.scattered, NC)

            @block.scalar
            def _(act):
                start_ring(act, k, k.table_index, index_ring)
                for place in range(RING):
                    act.sem_inc(k.ring_free[place].sem, 1)

                def turn(c, place, i, ahead, first=False):
                    act_next_index(act, k, k.table_index, index_ring, c, place, i, ahead)
                    act.wait_ge(*k.columns_ready.at(c + 1))
                    act.sem_inc(k.ring_free[place].sem, 1)
                    if not first:
                        act.wait_ge(*k.scattered[place].at(i))
                    act.activation(store_ring[:, place, :], flat(k.store_rows[:, bass.ds(c, 1), :]), ACT.Copy
                                   ).then_inc(k.e_state.sem, 1)

                for c in range(RING):
                    turn(c, c, 0, True, first=True)
                for c, place, i in chunks(act, NC - RING, RING):
                    turn(c, place, i + 1, True)
                for c in range(NC - RING, NC):
                    turn(c, c % RING, c // RING, False)

            @block.tensor
            def _(pe):
                for c, place, i in chunks(pe, NC):
                    pe.wait_ge(*k.gathered[place].at(i + 1))
                    pe_turn(pe, k, ring[:, place, :, :].rearrange("p q f -> p (q f)"), columns
                            ).then_inc(k.columns_ready.sem, 1)
                    pe_carry(pe, k, s, c, s.sums[:, SPAN - 1:SPAN], carry)
                    pe.wait_ge(*k.e_loaded[place].at(i + 1))
                    pe.wait_ge(*k.scanned.at(c + 1))
                    for h in range(HALVES):
                        at = slice(h * P, (h + 1) * P)
                        pe.matmul(projected[:, at], s.sums[:, at], k.ident[:], start=True, stop=False)
                        last = pe.matmul(projected[:, at], k.ident[:], own[:, place, at], start=False, stop=True)
                    last.then_inc(k.projected.sem, 1)

            @block.vector
            def _(dve):
                order = k.dve
                order.enter(dve)
                order.settle(dve.memset(s.sums[:], 0.0))
                order.close()
                for c, place, i in chunks(dve, NC):
                    order.enter(dve, c, 2)
                    dve_scan_alone(dve, k, s, c, columns)
                    dve_scan(dve, k, c, columns, carry, s.sums[:])
                    dve.wait_ge(*k.projected.at(c + 1))
                    order.settle(dve.tensor_tensor(t[:], projected.rearrange("p (q f) -> p q f", f=F),
                                                   spread(flat(k.inv_sqrt_deg[:, bass.ds(c, 1), :]), Q, F), ALU.mult))
                    order.settle(dve.tensor_tensor(t[:], t[:], k.b3[:].unsqueeze(1).to_broadcast([P, Q, F]), ALU.add))
                    dve.wait_ge(*k.e_state.at(c + 1))
                    dve.scalar_tensor_tensor(out[:, place, :, :].rearrange("p q f -> p (q f)"),
                                             t[:].rearrange("p q f -> p (q f)"), 0.0, flat(k.state[:, bass.ds(c, 1), :]),
                                             ALU.max, ALU.add).then_inc(k.e_out.sem, 1)
                    order.leave()
                order.close(NC)

            @block.sync
            def _(sp):
                def fetch(c, place):
                    sp.dma_start(own[:, place, :], edge_rows(k.t3, k.NP, c)).then_inc(k.e_loaded[place].sem, 16)

                for place in range(RING):
                    fetch(place, place)
                for c, place, i, ahead in chunks_ahead(sp, NC):
                    if ahead:
                        sp.wait_ge(*k.projected.at(c + 1))
                        fetch(c + RING, place)



def layout(inputs):
    x = np.asarray(inputs["x"])
    src, dst = np.asarray(inputs["src"]), np.asarray(inputs["dst"])
    gaps = np.asarray(inputs["edge_attr3_2x32"])
    nodes, edges = x.shape[0], src.shape[0]
    NC = max(-(-edges // CHUNK), -(-(nodes + 1) // (NODE_COLS * P)), 3)
    NP, EP, JN = NC * NODE_COLS * P, NC * CHUNK, NC * NODE_COLS
    a = {}
    a["x"] = np.concatenate([x, np.zeros((NP - nodes, F), x.dtype)])
    a["dst_line"] = np.concatenate([np.full(1, -1, dst.dtype), dst, np.full(EP - edges, nodes, dst.dtype),
                                    np.full(1, -2, dst.dtype)])
    a["src_line"] = np.concatenate([src, np.zeros(EP - edges, src.dtype)])
    gaps = np.concatenate([gaps.reshape(edges, 2 * F), np.zeros((EP - edges, 2 * F), gaps.dtype)])
    a["edge_attr"] = np.ascontiguousarray(
        gaps.reshape(NC, GROUPS, HALVES, P, 2 * F).transpose(0, 3, 2, 1, 4).reshape(EP, 2 * F))
    for name in ("L0_gnn_W", "L1_gnn_W1", "L1_gnn_b1", "L1_gnn_W2s", "L1_gnn_b2s", "L1_gnn_W2d", "L1_gnn_b2d",
                 "L1_gnn_attn", "L2_gnn_W1_l", "L2_gnn_b1", "L2_gnn_W1_r", "L2_gnn_W2_l", "L2_gnn_b2",
                 "L2_gnn_W2_r", "L3_gnn_bias"):
        a[name] = np.ascontiguousarray(np.asarray(inputs[name]))
    a["L3_gnn_W_turned"] = np.ascontiguousarray(np.asarray(inputs["L3_gnn_W"]).T)
    f, g = np.arange(P) % F, np.arange(P) // F
    same_f = f[:, None] == f[None, :]
    a["identity"] = np.eye(P, dtype=np.float32)
    a["carry_patterns"] = np.stack([same_f & (g[:, None] < g[None, :]), same_f & (g[:, None] == GROUPS - 1),
                                    same_f & (g[:, None] > g[None, :]), same_f & (g[:, None] == 0)],
                                   axis=1).astype(np.float32)
    a["below"] = (np.arange(P)[:, None] < np.arange(P)[None, :]).astype(np.float32)
    a["above"] = (np.arange(P)[:, None] > np.arange(P)[None, :]).astype(np.float32)
    pick = np.zeros((P, GROUPS, P), np.float32)
    for group in range(GROUPS):
        pick[F * group, group, :] = 1.0
    a["pick_group"] = pick
    a["count_up"] = np.arange(max(JN, P), dtype=np.float32)
    a["edge_number"] = np.arange(EP, dtype=np.float32)
    a["edge_number_rows"] = np.ascontiguousarray(
        a["edge_number"].reshape(NC, GROUPS, HALVES, P).transpose(3, 0, 2, 1).reshape(P, NC * Q))
    a["node_number"] = np.arange(NP, dtype=np.float32).reshape(P, JN)
    return a, NC, nodes


def kernel(**inputs):
    import concourse.bacc as _bacc
    from concourse.bass_utils import run_bass_kernel_spmd as _run

    arrays, NC, nodes = layout(inputs)
    nc = _bacc.Bacc("TRN2", target_bir_lowering=False, num_devices=1)
    d = {name: nc.dram_tensor(name, a.shape, mybir.dt.from_np(a.dtype), kind="ExternalInput").ap()
         for name, a in arrays.items()}
    d["out"] = nc.dram_tensor("out", (NC * NODE_COLS * P, F), F32, kind="ExternalOutput").ap()
    build(nc, d, NC)
    result = _run(nc, [arrays], core_ids=[0])
    return result.results[0]["out"][:nodes]
```

```python
import numpy as np
from contextlib import ExitStack

import concourse.bass as bass
from concourse import mybir

F32 = mybir.dt.float32
BF16 = mybir.dt.bfloat16
F16 = mybir.dt.float16
I32 = mybir.dt.int32
U32 = mybir.dt.uint32
ALU = mybir.AluOpType
ACT = mybir.ActivationFunctionType
AX = mybir.AxisListType.X

P = 128
F = 32
GROUPS = 4
HALVES = 2
Q = GROUPS * HALVES
SPAN = HALVES * P
CHUNK = GROUPS * SPAN
LINE = 512
NODE_COLS = 16
RING = 2
FAR = 1.0e30
EPS = 1e-5
SLOPE = 0.2


class Kernel:
    pass


class NormSignals:

    def __init__(self, signal, name):
        self.centred, self.squared = signal(name + "_centred"), signal(name + "_squared")
        self.varied, self.rooted = signal(name + "_varied"), signal(name + "_rooted")


class NormTiles:
    def __init__(self, sb, name, n, squares=None):
        self.total, self.centred = sb(name + "_total", [P, n])[:], sb(name + "_centred", [P, n, F])[:]
        self.squares = sb(name + "_squares", [P, n, F])[:] if squares is None else squares
        self.var, self.dev, self.inv = sb(name + "_var", [P, n])[:], sb(name + "_dev", [P, n])[:], sb(name + "_inv", [P, n])[:]


def norm_ring(sb, name, n):
    first = NormTiles(sb, name + "0", n)
    return [first] + [NormTiles(sb, f"{name}{place}", n, first.squares) for place in range(1, RING)]


class SumTiles:
    def __init__(self, sb):
        self.carry, self.alone, self.sums = sb("carry", [P, 2, P]), sb("alone", [P, SPAN]), sb("sums", [P, SPAN])


class SumRing:
    def __init__(self, sb):
        self.carry, self.alone, self.sums = sb("carry", [P, 2, P]), sb("alone", [P, SPAN]), sb("sums", [P, RING, SPAN])

    def last(self, place):
        return self.sums[:, 1 - place, SPAN - 1:SPAN]


class SortSemaphores:
    def __init__(self, sem):
        self.loaded, self.flags, self.counted = sem("sort_loaded"), sem("sort_flags"), sem("sort_counted")
        self.known, self.piece, self.piece_used = sem("sort_known"), sem("sort_piece"), sem("sort_piece_used")
        self.rows, self.set, self.free = sem("sort_rows"), sem("sort_set"), sem("sort_free")
        self.stored, self.ends = sem("sort_stored"), sem("sort_ends")


class Signal:

    def __init__(self, sem, unit=1):
        self.sem, self.unit, self.before = sem, unit, 0

    def at(self, n):
        return self.sem, self.before + n * self.unit

    def close(self, n):
        self.before += n * self.unit


class Order:

    def __init__(self, sem):
        self.sem, self.before, self.base, self.k = sem, 0, 0, 0

    def enter(self, eng, turn=0, per_turn=None):
        self.eng, self.k, self.per_turn = eng, 0, per_turn
        self.base = self.before + turn * (per_turn or 0)

    def settle(self, instruction):
        instruction.then_inc(self.sem, 1)
        self.k += 1
        self.eng.wait_ge(self.sem, self.base + self.k)

    def note(self, instruction):
        instruction.then_inc(self.sem, 1)
        self.k += 1

    def leave(self):
        assert self.per_turn is None or self.k == self.per_turn, f"a turn has {self.k} steps"

    def close(self, turns=1):
        self.before += self.k * turns

    def enter_turn(self, eng, turn, per_turn):
        self.eng, self.k = eng, 0
        self.base = self.before if turn.i is None else self.before + (turn.i * turn.unroll + turn.n) * per_turn

    def leave_turn(self, turn, per_turn):
        if turn.i is None:
            self.before += self.k
        else:
            assert self.k == per_turn, f"a turn has {self.k} steps"
            if turn.n == turn.unroll - 1:
                self.before += turn.turns * turn.unroll * per_turn


def chunks(eng, n, start=0):
    turns = (n - start) // RING
    if turns:
        with eng.Fori(0, turns) as i:
            for place in range(RING):
                yield i * RING + place + start, place, i
    for rest in range(turns * RING, n - start):
        yield rest + start, rest % RING, turns


def chunks_ahead(eng, n):
    for c, place, i in chunks(eng, n - RING):
        yield c, place, i, True
    for c in range(n - RING, n):
        yield c, c % RING, c // RING, False


class Chunk:

    def __init__(self, n, place, uses, again, ahead):
        self.n, self.place, self.uses, self.again, self.ahead = n, place, uses, again, ahead
        self.first = isinstance(n, int) and n == 0


class Turn:

    def __init__(self, NC, at, i=None, turns=0, n=0, unroll=RING):
        self.NC, self.at, self.i, self.turns, self.n, self.unroll = NC, at, i, turns, n, unroll

    def late(self, by=0):
        at = self.at - by
        if self.i is None:
            return [Chunk(at, at % RING, at // RING, at >= RING, at + RING < self.NC)] if 0 <= at < self.NC else []
        return [Chunk(self.i * self.unroll + at, at % RING, self.i * (self.unroll // RING) + at // RING, True, True)]


def skewed(eng, NC, depth, unroll=RING):
    head = min(depth + RING, NC - RING)
    turns = (NC - RING - head) // unroll
    for t in range(head):
        yield Turn(NC, t)
    if turns:
        with eng.Fori(0, turns) as i:
            for n in range(unroll):
                yield Turn(NC, head + n, i, turns, n, unroll)
    for t in range(head + turns * unroll, NC + depth):
        yield Turn(NC, t)


def close_ring(signals, n, more=0):
    for place, s in enumerate(signals):
        s.close(len(range(place, n, RING)) + more)


def wait_ring(eng, signals, n, more=0):
    for place, s in enumerate(signals):
        eng.wait_ge(*s.at(len(range(place, n, RING)) + more))


def spread(ap, n, width):
    return ap.unsqueeze(2).to_broadcast([ap.shape[0], n, width])


def build(nc, d, NC):
    k = Kernel()
    k.nc, k.d, k.NC = nc, d, NC
    k.NP, k.EP, k.JN, k.SP = NC * NODE_COLS * P, NC * CHUNK, NC * NODE_COLS, NC * CHUNK // LINE
    with ExitStack() as ctx:
        def sb(name, shape, dt=F32):
            return ctx.enter_context(nc.sbuf_tensor(name, shape, dt))

        k.bank = [ctx.enter_context(nc.psum_tensor(f"bank{n}", [P, 512], F32)) for n in range(8)]

        k.ident = sb("ident", [P, P])
        k.ones_row = sb("ones_row", [1, P])
        k.carry_base = sb("carry_base", [P, 4, P])
        k.eps = sb("eps", [P, 1])
        k.w0 = sb("w0", [P, P])
        k.w1 = sb("w1", [P, P])
        k.w2s = sb("w2s", [P, 256])
        k.w2d = sb("w2d", [P, 256])
        k.w1l = sb("w1l", [P, 256])
        k.w1r = sb("w1r", [P, 256])
        k.w2lr = sb("w2lr", [P, P])
        k.w3 = sb("w3", [P, P])
        k.attn = sb("attn", [P, 4])
        k.attn_parts = sb("attn_parts", [P, 2, 4])
        k.bz = sb("bz", [P, 2])
        k.b1_col = sb("b1_col", [P, 1])
        k.b1_row = sb("b1_row", [1, 512])
        k.b2s_row = sb("b2s_row", [1, 512])
        k.b2 = sb("b2", [P, F])
        k.b3 = sb("b3", [P, F])
        k.dst_rows = sb("dst_rows", [P, NC, Q])
        k.dst_index = sb("dst_index", [P, NC * Q], U32)
        k.src_index = sb("src_index", [P, NC * Q], U32)
        k.table_index = sb("table_index", [P, NC * Q], U32)
        k.store_rows = sb("store_rows", [P, NC, Q])
        k.inv_deg = sb("inv_deg", [P, NC, Q])
        k.inv_sqrt_deg = sb("inv_sqrt_deg", [P, NC, Q])
        k.same = sb("same", [P, NC, SPAN + 1], BF16)
        k.first_col = sb("first_col", [P, NC + 1])
        k.last_col = sb("last_col", [P, NC + 1])
        k.first_all = sb("first_all", [P, NC, GROUPS])
        k.last_all = sb("last_all", [P, NC, GROUPS])
        k.line_same = sb("line_same", [k.SP, LINE + 1])
        k.line_far = sb("line_far", [k.SP, LINE + 1])
        k.line_fwd = sb("line_fwd", [k.SP, k.SP])
        k.line_bwd = sb("line_bwd", [k.SP, k.SP])
        k.line_far_fwd = sb("line_far_fwd", [k.SP, k.SP])
        k.line_far_bwd = sb("line_far_bwd", [k.SP, k.SP])
        k.line_ones = sb("line_ones", [k.SP, k.SP])
        k.carry_col = sb("carry_col", [k.SP, 1])
        k.line_a = sb("line_a", [k.SP, LINE])
        k.line_f = sb("line_f", [k.SP, LINE])
        k.line_b = sb("line_b", [k.SP, LINE])
        k.line_diag = sb("line_diag", [k.SP, k.SP])
        k.logits = sb("logits", [P, 8, NC * 2])
        k.alpha = sb("alpha", [P, NC, 2 * Q])

        def sem(name):
            return ctx.enter_context(nc.semaphore(name))

        k.dve, k.act, k.pool = Order(sem("dve_done")), Order(sem("act_done")), Order(sem("pool_done"))

        def signal(name, unit=1):
            return Signal(sem(name), unit)

        k.loaded = signal("loaded", 16)
        k.prepared = signal("prepared")
        k.line_carried = signal("line_carried")
        k.line_scanned = signal("line_scanned")
        k.turned = signal("turned")
        k.turned_used = signal("turned_used")
        k.gathered = [signal(f"gathered{n}", 16 * Q) for n in range(RING)]
        k.attr_ready = signal("attr_ready", 16)
        k.index_set = signal("index_set")
        k.gather_started = signal("gather_started")
        k.ring_free = [signal(f"ring_free{n}") for n in range(RING)]
        k.rows_ready = signal("rows_ready")
        k.columns_ready = signal("columns_ready")
        k.scanned_alone = signal("scanned_alone")
        k.carried = signal("carried")
        k.scanned = signal("scanned")
        k.projected = signal("projected")
        k.projected_used = signal("projected_used")
        k.e_ln, k.n_ln = NormSignals(signal, "e"), NormSignals(signal, "n")
        k.e_out = signal("e_out")
        k.e_stored = [signal(f"e_stored{n}", 16) for n in range(RING)]
        k.e_loaded = [signal(f"e_loaded{n}", 16) for n in range(RING)]
        k.e_load_used = signal("e_load_used")
        k.n_loaded = [signal(f"n_loaded{n}", 16) for n in range(RING)]
        k.n_load_used = signal("n_load_used")
        k.h_loaded = [signal(f"h_loaded{n}", 16) for n in range(RING)]
        k.x_stored = [signal(f"x_stored{n}", 16) for n in range(RING)]
        k.n_out = signal("n_out")
        k.n_out2 = signal("n_out2")
        k.n_stored = [signal(f"n_stored{n}", 16) for n in range(RING)]
        k.n_rows = signal("n_rows")
        k.n_columns = signal("n_columns")
        k.n_columns_kept = signal("n_columns_kept")
        k.n_hidden = signal("n_hidden")
        k.n_hidden_kept = signal("n_hidden_kept")
        k.n_projected = signal("n_projected")
        k.e_columns = signal("e_columns")
        k.e_columns_kept = signal("e_columns_kept")
        k.e_hidden = signal("e_hidden")
        k.e_hidden_kept = signal("e_hidden_kept")
        k.e_projected = signal("e_projected")
        k.e_gap = signal("e_gap")
        k.e_en = signal("e_en")
        k.e_state = signal("e_state")
        k.e_logits = signal("e_logits")
        k.e_logits_kept = signal("e_logits_kept")
        k.weighted = signal("weighted")
        k.raised = signal("raised")
        k.summed = signal("summed")
        k.counted = signal("counted")
        k.onehot = signal("onehot")
        k.scattered = [signal(f"scattered{n}", 16 * Q) for n in range(RING)]

        k.sort_dve = Order(sem("sort_dve_done"))
        k.sort = SortSemaphores(sem)
        k.dst_sorted = nc.dram_tensor("dst_sorted", (k.EP + 2,), I32).ap()
        k.src_sorted = nc.dram_tensor("src_sorted", (k.EP,), I32).ap()
        k.attr_sorted = nc.dram_tensor("attr_sorted", (k.EP, 2 * F), F32).ap()
        k.t01 = nc.dram_tensor("table01", (k.NP + k.EP, F + 1), F32).ap()
        k.t2 = nc.dram_tensor("table2", (k.NP + k.EP, F), F32).ap()
        k.t2b = nc.dram_tensor("table2b", (k.NP + k.EP, F), F32).ap()
        k.t3 = nc.dram_tensor("table3", (k.NP + k.EP, F), F32).ap()
        k.xa = nc.dram_tensor("nodes_after1", (k.NP, F), F32).ap()
        k.xb = nc.dram_tensor("nodes_after2", (k.NP, F), F32).ap()
        k.gap_rows = nc.dram_tensor("edge_gaps", (k.EP, 2 * F), F32).ap()

        load_constants(k)
        sort_edges(k)
        k.state = sb("state", [P, NC, Q * F])
        prepare_edges(k)
        gather_destinations(k)
        with ExitStack() as inner:
            k.sums0 = inner.enter_context(nc.sbuf_tensor("sums0", [P, NC * SPAN], F32))
            layer0(k)
            layer1_logits(k)
        layer1_softmax(k)
        layer1_sums(k)
        layer2_first(k)
        layer2_second(k)
        layer3(k)



def allocator(k, ctx, phase):
    def sb(name, shape, dt=F32):
        return ctx.enter_context(k.nc.sbuf_tensor(f"{phase}_{name}", shape, dt))
    return sb


def edge_rows(table, base, c):
    width = table.shape[1]
    return table[bass.ds(base + c * CHUNK, CHUNK), :].rearrange("(p q) f -> p (q f)", p=P)


def node_rows(table, c, nodes):
    whole = table[0:nodes, :].rearrange("(p j) f -> p (j f)", p=P)
    width = NODE_COLS * table.shape[1]
    return whole[:, bass.ds(c * width, width)]


def gather(pool, k, table, ring, index_ring, place):
    pool.sem_inc(k.gather_started.sem, 1)
    for q in range(Q):
        pool.indirect_dma_start(out=ring[:, place, q, :], out_offset=None, in_=table,
                                in_offset=bass.IndirectOffsetOnAxis(ap=index_ring[:, place, q:q + 1], axis=0)
                                ).then_inc(k.gathered[place].sem, 16)


def ln_centre(dve, k, ln, x, n, s):
    k.dve.settle(dve.tensor_reduce(s.total, x, AX, ALU.add))
    dve.scalar_tensor_tensor(s.centred, spread(s.total, n, F), -1.0 / F, x, ALU.mult, ALU.add
                             ).then_inc(ln.centred.sem, 1)


def ln_square(act, k, ln, c, s):
    act.wait_ge(*ln.centred.at(c + 1))
    act.activation(s.squares, s.centred, ACT.Square).then_inc(ln.squared.sem, 1)


def ln_variance(dve, k, ln, c, s):
    dve.wait_ge(*ln.squared.at(c + 1))
    dve.tensor_reduce(s.var, s.squares, AX, ALU.add).then_inc(ln.varied.sem, 1)


def ln_root(act, k, ln, c, s):
    act.wait_ge(*ln.varied.at(c + 1))
    act.activation(s.dev, s.var, ACT.Sqrt, bias=k.eps[:], scale=1.0 / F).then_inc(ln.rooted.sem, 1)


def ln_scale(dve, k, ln, c, n, s, out):
    dve.wait_ge(*ln.rooted.at(c + 1))
    k.dve.settle(dve.reciprocal(s.inv, s.dev))
    return dve.scalar_tensor_tensor(out, s.centred, 0.0, spread(s.inv, n, F), ALU.max, ALU.mult)


def ln_close(ln, n):
    for s in (ln.centred, ln.squared, ln.varied, ln.rooted):
        s.close(n)


FORWARD, FORWARD_BEFORE, BACKWARD, BACKWARD_AFTER = range(4)


def pe_turn(pe, k, rows, columns):
    for h in range(HALVES):
        last = pe.transpose(columns[:, h * P:(h + 1) * P], rows[:, h * P:(h + 1) * P], k.ident[:])
    return last


def dve_scan_alone(dve, k, t, c, columns):
    dve.scalar_tensor_tensor(t.carry[:, 0, :].rearrange("p (g f) -> p g f", g=GROUPS),
                             spread(k.first_all[:, bass.ds(c, 1), :].rearrange("p o g -> p (o g)"), GROUPS, F),
                             k.last_col[:, bass.ds(c + 1, 1)],
                             k.carry_base[:, FORWARD, :].rearrange("p (g f) -> p g f", g=GROUPS),
                             ALU.is_equal, ALU.mult)
    dve.scalar_tensor_tensor(t.carry[:, 1, :].rearrange("p (g f) -> p g f", g=GROUPS),
                             spread(k.first_all[:, bass.ds(c, 1), :].rearrange("p o g -> p (o g)"), GROUPS, F),
                             k.last_col[:, bass.ds(c, 1)],
                             k.carry_base[:, FORWARD_BEFORE, :].rearrange("p (g f) -> p g f", g=GROUPS),
                             ALU.is_equal, ALU.mult)
    dve.wait_ge(*k.columns_ready.at(c + 1))
    dve.tensor_tensor_scan(t.alone[:], flat(k.same[:, bass.ds(c, 1), 0:SPAN]), columns, 0.0, ALU.mult, ALU.add
                           ).then_inc(k.scanned_alone.sem, 1)


def flat(ap):
    return ap.rearrange("p o n -> p (o n)")


def pe_carry(pe, k, t, c, before, out):
    pe.wait_ge(*k.scanned_alone.at(c + 1))
    pe.matmul(out, t.carry[:, 0, :], t.alone[:, SPAN - 1:SPAN], start=True, stop=False)
    pe.matmul(out, t.carry[:, 1, :], before, start=False, stop=True).then_inc(k.carried.sem, 1)


def dve_scan(dve, k, c, columns, carry, sums):
    dve.wait_ge(*k.carried.at(c + 1))
    dve.tensor_tensor_scan(sums, flat(k.same[:, bass.ds(c, 1), 0:SPAN]), columns, carry, ALU.mult, ALU.add
                           ).then_inc(k.scanned.sem, 1)


def act_index(act, k, index, index_ring, c, place, reverse=None):
    col = c * Q if reverse is None else (reverse - c) * Q
    return act.activation(index_ring[:, place, :], index[:, bass.ds(col, Q)], ACT.Copy)


def start_ring(act, k, index, index_ring, reverse=None):
    for place in range(RING):
        act_index(act, k, index, index_ring, place, place, reverse).then_inc(k.index_set.sem, 1)



def load_constants(k):
    nc, d = k.nc, k.d
    k.n_loads = 3 + 6 + 2 + 28 + 4 + 4 + 1
    squares = [(k.w0, d["L0_gnn_W"], F), (k.w1, d["L1_gnn_W1"], F), (k.w3, d["L3_gnn_W_turned"], F),
               (k.w2s, d["L1_gnn_W2s"], 2 * F), (k.w2d, d["L1_gnn_W2d"], 2 * F),
               (k.w1l, d["L2_gnn_W1_l"], 2 * F), (k.w1r, d["L2_gnn_W1_r"], 2 * F)]
    zeroed = [w for w, _, _ in squares] + [k.w2lr, k.attn]
    with nc.Block() as block:
        @block.vector
        def _(dve):
            dve.memset(k.ones_row[:], 1.0)
            dve.memset(k.eps[:], EPS)
            dve.memset(k.line_ones[:], 1.0)
            for w in zeroed:
                last = dve.memset(w[:], 0.0)
            last.then_inc(k.prepared.sem, 1)
            dve.wait_ge(*k.loaded.at(k.n_loads))
            dve.tensor_scalar(k.attn_parts[:, 0, :], k.attn[:], SLOPE, None, ALU.mult)
            dve.tensor_scalar(k.attn_parts[:, 1, :], k.attn[:], 1.0 - SLOPE, None, ALU.mult)
            dve.tensor_tensor(k.bz[:, 0:1], k.bz[:, 0:1], k.bz[:, 1:2], ALU.add).then_inc(k.prepared.sem, 1)
            dve.wait_ge(*k.prepared.at(2))

        @block.sync
        def _(sp):
            n = 0

            def load(out, in_):
                sp.dma_start(out, in_).then_inc(k.loaded.sem, 16)
                return 1

            n += load(k.ident[:], d["identity"])
            n += load(k.carry_base[:], d["carry_patterns"])
            n += load(k.b3[:], d["L3_gnn_bias"].partition_broadcast(P))
            n += load(k.b2[:], d["L2_gnn_b2"].partition_broadcast(P))
            for gl in range(2):
                n += load(k.b1_col[64 * gl:64 * gl + 64, :], d["L2_gnn_b1"].unsqueeze(1))
                n += load(k.bz[64 * gl:64 * gl + 64, 0:1], d["L1_gnn_b2s"].unsqueeze(1))
                n += load(k.bz[64 * gl:64 * gl + 64, 1:2], d["L1_gnn_b2d"].unsqueeze(1))
            n += load(k.b1_row[:].rearrange("o (n f) -> o n f", f=F),
                      d["L1_gnn_b1"].unsqueeze(0).unsqueeze(1).to_broadcast([1, 16, F]))
            n += load(k.b2s_row[:].rearrange("o (n f) -> o n f", f=2 * F),
                      d["L1_gnn_b2s"].unsqueeze(0).unsqueeze(1).to_broadcast([1, 8, 2 * F]))
            sp.wait_ge(*k.prepared.at(1))
            for w, src, width in squares:
                for g in range(GROUPS):
                    n += load(w[F * g:F * g + F, width * g:width * g + width], src)
            for gl in range(2):
                n += load(k.w2lr[64 * gl:64 * gl + 64, 64 * gl:64 * gl + 32], d["L2_gnn_W2_l"])
                n += load(k.w2lr[64 * gl:64 * gl + 64, 64 * gl + 32:64 * gl + 64], d["L2_gnn_W2_r"])
                for h in range(2):
                    at = 64 * gl + 32 * h
                    n += load(k.attn[at:at + 32, 2 * gl + h:2 * gl + h + 1], d["L1_gnn_attn"][0, h, :].unsqueeze(1))
            assert n == k.n_loads, n
            sp.wait_ge(*k.loaded.at(n))
    k.loaded.close(k.n_loads)
    k.prepared.close(2)


def sort_edges(k):
    nc, d, NC, SP, EP = k.nc, k.d, k.NC, k.SP, k.EP
    pieces = next(n for n in range(1, NC + 1) if NC % n == 0 and EP // n <= 8 * CHUNK)
    width = EP // pieces
    s, order = k.sort, k.sort_dve
    with ExitStack() as ctx:
        sb = allocator(k, ctx, "sort")
        line = sb("line", [SP, LINE + 2], I32)
        falls = sb("falls", [SP, LINE])
        fall_count = sb("fall_count", [SP, 1])
        unsorted = sb("unsorted", [1, 1], I32)
        dst_all = sb("dst_all", [P, width], I32)
        number_all = sb("number_all", [P, width])
        ahead = sb("ahead", [P, width])
        dst_own = sb("dst_own", [P, NC, Q], I32)
        src_own = sb("src_own", [P, NC, Q], I32)
        dst_f = sb("dst_f", [P, NC * Q])
        number_own = sb("number_own", [P, NC * Q])
        found = sb("found", [P, 1])
        rank = sb("rank", [P, NC * Q])
        row = sb("row", [P, 4, NC * Q], I32)
        targets = sb("targets", [P, 3, Q], U32)
        own = sb("own", [P, 2, Q], I32)
        attr = sb("attr", [P, Q, 2 * F])
        count = k.bank[0][0:1, 0:1]

        with nc.Block() as block:
            @block.sync
            def _(sp):
                sp.dma_start(line[:], bass.AP(tensor=d["dst_line"].tensor, offset=0, ap=[[LINE, SP], [1, LINE + 2]])
                             ).then_inc(s.loaded, 16)
                sp.wait_ge(s.known, 1)
                falling = sp.value_load(unsorted[0:1, 0:1])
                with sp.If(falling == 0):
                    sp.dma_start(k.dst_sorted, d["dst_line"]).then_inc(s.ends, 16)
                    sp.dma_start(k.src_sorted, d["src_line"]).then_inc(s.ends, 16)
                    sp.dma_start(k.attr_sorted, d["edge_attr"]).then_inc(k.attr_ready.sem, 16)
                    sp.wait_ge(s.ends, 32)
                with sp.Else():
                    for b in range(HALVES):
                        for c in range(NC):
                            at = c * CHUNK + b * P
                            with nc.allow_non_contiguous_dma("the edges of a lane lie apart"):
                                sp.dma_start(dst_own[:, c, b * GROUPS:(b + 1) * GROUPS],
                                             bass.AP(tensor=d["dst_line"].tensor, offset=1 + at, ap=[[1, P], [SPAN, GROUPS]])
                                             ).then_inc(s.rows, 16)
                                sp.dma_start(src_own[:, c, b * GROUPS:(b + 1) * GROUPS],
                                             bass.AP(tensor=d["src_line"].tensor, offset=at, ap=[[1, P], [SPAN, GROUPS]])
                                             ).then_inc(s.rows, 16)
                    sp.dma_start(number_own[:], d["edge_number_rows"]).then_inc(s.rows, 16)
                    for n in range(pieces):
                        if n:
                            sp.wait_ge(s.piece_used, n)
                        at = slice(n * width, (n + 1) * width)
                        sp.dma_start(dst_all[:], d["dst_line"][1 + n * width:1 + (n + 1) * width].partition_broadcast(P)
                                     ).then_inc(s.piece, 16)
                        sp.dma_start(number_all[:], d["edge_number"][at].partition_broadcast(P)).then_inc(s.piece, 16)
                    for at in (0, EP + 1):
                        sp.dma_start(k.dst_sorted[at:at + 1], d["dst_line"][at:at + 1]).then_inc(s.ends, 16)
                    with sp.Fori(0, NC) as c:
                        sp.wait_ge(s.free, c + 1)
                        sp.dma_start(attr[:].rearrange("p q f -> p (q f)"), edge_rows(d["edge_attr"], 0, c)).then_inc(s.loaded, 16)
                    sp.wait_ge(s.ends, 32)
                    sp.wait_ge(s.free, NC + 1)
                    sp.sem_inc(k.attr_ready.sem, 16)

            @block.tensor
            def _(pe):
                pe.wait_ge(s.flags, 1)
                pe.matmul(count, fall_count[:], k.line_ones[:, 0:1], start=True, stop=True).then_inc(s.counted, 1)

            @block.vector
            def _(dve):
                order.enter(dve)
                dve.wait_ge(s.loaded, 16)
                order.settle(dve.tensor_tensor(falls[:], line[:, 0:LINE], line[:, 1:LINE + 1], ALU.is_gt))
                dve.tensor_reduce(fall_count[:], falls[:], AX, ALU.add).then_inc(s.flags, 1)
                dve.wait_ge(s.counted, 1)
                dve.tensor_copy(unsorted[:], count).then_inc(s.known, 1)
                dve.wait_ge(s.known, 1)
                falling = dve.value_load(unsorted[0:1, 0:1])
                with dve.If(falling == 0):
                    dve.sem_inc(s.flags, 1)
                with dve.Else():
                    dve.wait_ge(s.rows, 16 * (4 * NC + 1))
                    order.settle(dve.tensor_copy(dst_f[:], dst_own[:].rearrange("p c q -> p (c q)")))
                    order.settle(dve.memset(rank[:], 0.0))
                    order.close()
                    for n in range(pieces):
                        dve.wait_ge(s.piece, 32 * (n + 1))
                        with dve.Fori(0, NC * Q) as t:
                            order.enter(dve, t, 5)
                            order.settle(dve.tensor_scalar(ahead[:], number_all[:], number_own[:, bass.ds(t, 1)], None, ALU.is_lt))
                            order.settle(dve.scalar_tensor_tensor(ahead[:], dst_all[:], dst_f[:, bass.ds(t, 1)], ahead[:],
                                                                  ALU.is_equal, ALU.mult))
                            order.settle(dve.scalar_tensor_tensor(ahead[:], dst_all[:], dst_f[:, bass.ds(t, 1)], ahead[:],
                                                                  ALU.is_lt, ALU.add))
                            order.settle(dve.tensor_reduce(found[:], ahead[:], AX, ALU.add))
                            order.note(dve.tensor_tensor(rank[:, bass.ds(t, 1)], rank[:, bass.ds(t, 1)], found[:], ALU.add))
                            order.leave()
                        order.close(NC * Q)
                        order.enter(dve)
                        dve.wait_ge(order.sem, order.base)
                        dve.sem_inc(s.piece_used, 1)
                    order.enter(dve)
                    order.settle(dve.tensor_copy(row[:, 0, :], rank[:]))
                    row_of_edge(dve, order, row)
                    order.close()
                    with dve.Fori(0, NC) as c:
                        order.enter(dve, c, 4)
                        dve.wait_ge(s.free, c + 1)
                        order.note(dve.tensor_scalar(targets[:, 0, :], rank[:, bass.ds(c * Q, Q)], 1.0, None, ALU.add))
                        order.note(dve.tensor_copy(targets[:, 1, :], rank[:, bass.ds(c * Q, Q)]))
                        order.note(dve.tensor_copy(targets[:, 2, :], row[:, 0, bass.ds(c * Q, Q)]))
                        order.note(dve.tensor_copy(own[:, 0, :], flat(dst_own[:, bass.ds(c, 1), :])))
                        dve.tensor_copy(own[:, 1, :], flat(src_own[:, bass.ds(c, 1), :])).then_inc(s.set, 1)
                        order.leave()
                    order.close(NC)

            @block.gpsimd
            def _(pool):
                pool.wait_ge(s.known, 1)
                falling = pool.value_load(unsorted[0:1, 0:1])
                with pool.If(falling == 0):
                    pool.sem_inc(s.flags, 1)
                with pool.Else():
                    pool.sem_inc(s.free, 1)
                    with pool.Fori(0, NC) as c:
                        pool.wait_ge(s.set, c + 1)
                        pool.wait_ge(s.loaded, 16 * (c + 2))
                        pool.sem_inc(s.flags, 1)
                        for q in range(Q):
                            for n, (out, data) in enumerate(((k.dst_sorted, own[:, 0, q:q + 1]), (k.src_sorted, own[:, 1, q:q + 1]),
                                                             (k.attr_sorted, attr[:, q, :]))):
                                pool.indirect_dma_start(
                                    out=out.unsqueeze(1) if n < 2 else out,
                                    out_offset=bass.IndirectOffsetOnAxis(ap=targets[:, n, q:q + 1], axis=0),
                                    in_=data, in_offset=None).then_inc(s.stored, 16)
                        pool.wait_ge(s.stored, (c + 1) * (16 * 3 * Q))
                        pool.sem_inc(s.free, 1)


def line_carry(k):
    return k.bank[0][0:k.SP, 0:1], k.bank[0][0:k.SP, 0:k.SP]


def dve_line_total(dve, k, values, op, out, turn):
    same, op0, start = (k.line_same, ALU.mult, 0.0) if op == ALU.add else (k.line_far, ALU.add, -FAR)
    carry, everyone = line_carry(k)
    for way in range(2):
        if way == 0:
            flags, data, result = same[:, 0:LINE], values, k.line_f[:]
            alone, tail, far = k.line_a[:], k.line_a[:, LINE - 1:LINE], k.line_far_fwd
        else:
            flags, data, result = same[:, 1:LINE + 1][:, ::-1], values[:, ::-1], k.line_b[:, ::-1]
            alone, tail, far = k.line_a[:, ::-1], k.line_a[:, 0:1], k.line_far_bwd
        if op == ALU.add:
            dve.tensor_tensor_scan(alone, flags, data, start, op0, op).then_inc(k.line_scanned.sem, 1)
            dve.wait_ge(*k.line_carried.at(turn + way + 1))
            k.dve.settle(dve.tensor_tensor_scan(result, flags, data, carry, op0, op))
        else:
            k.dve.settle(dve.tensor_tensor_scan(alone, flags, data, start, op0, op))
            dve.tensor_scalar(k.line_diag[:], k.ident[0:k.SP, 0:k.SP], tail, None, ALU.mult
                              ).then_inc(k.line_scanned.sem, 1)
            dve.wait_ge(*k.line_carried.at(turn + way + 1))
            k.dve.settle(dve.tensor_tensor(k.line_diag[:], everyone, far[:], ALU.add))
            k.dve.settle(dve.tensor_reduce(k.carry_col[:], k.line_diag[:], AX, ALU.max))
            k.dve.settle(dve.tensor_tensor_scan(result, flags, data, k.carry_col[:], op0, op))
    if op == ALU.add:
        k.dve.settle(dve.tensor_tensor(out, k.line_f[:], k.line_b[:], ALU.add))
        k.dve.settle(dve.tensor_tensor(out, out, values, ALU.subtract))
    else:
        k.dve.settle(dve.tensor_tensor(out, k.line_f[:], k.line_b[:], ALU.max))


def pe_line_total(pe, k, op, turn):
    carry, everyone = line_carry(k)
    for way in range(2):
        pe.wait_ge(*k.line_scanned.at(turn + way + 1))
        if op == ALU.add:
            reach, tail = ((k.line_fwd, k.line_a[:, LINE - 1:LINE]), (k.line_bwd, k.line_a[:, 0:1]))[way]
            pe.matmul(carry, reach[:], tail, start=True, stop=True).then_inc(k.line_carried.sem, 1)
        else:
            pe.matmul(everyone, k.line_ones[:], k.line_diag[:], start=True, stop=True).then_inc(k.line_carried.sem, 1)


def prepare_edges(k):
    nc, d, NC, SP = k.nc, k.d, k.NC, k.SP
    dst, src = k.dst_sorted, k.src_sorted
    with ExitStack() as ctx:
        sb = allocator(k, ctx, "prep")
        dst_int = sb("dst_int", [SP, LINE + 2], I32)
        src_int = sb("src_int", [SP, LINE], I32)
        dstf = sb("dstf", [SP, LINE + 2])
        srcf = sb("srcf", [SP, LINE])
        tmp = sb("tmp", [SP, LINE])
        ones = sb("ones", [SP, LINE])
        deg = sb("deg", [SP, LINE])
        inv = sb("inv", [SP, LINE])
        isd = sb("isd", [SP, LINE])
        store = sb("store", [SP, LINE])
        lt = sb("lt", [P, P])
        gt = sb("gt", [P, P])
        dcols = sb("dcols", [P, NC, SPAN + 2], I32)
        pick = sb("pick", [P, GROUPS, P])

        with nc.Block() as block:
            @block.sync
            def _(sp):
                sp.dma_start(dst_int[:], bass.AP(tensor=dst.tensor, offset=0, ap=[[LINE, SP], [1, LINE + 2]])
                             ).then_inc(k.loaded.sem, 16)
                sp.dma_start(src_int[:], src.rearrange("(p n) -> p n", n=LINE)).then_inc(k.loaded.sem, 16)
                sp.dma_start(lt[:], d["below"]).then_inc(k.loaded.sem, 16)
                sp.dma_start(gt[:], d["above"]).then_inc(k.loaded.sem, 16)
                sp.dma_start(pick[:], d["pick_group"]).then_inc(k.loaded.sem, 16)
                for g in range(GROUPS):
                    sp.dma_start(dcols[F * g:F * g + F, :, :],
                                 bass.AP(tensor=dst.tensor, offset=g * SPAN,
                                         ap=[[0, F], [CHUNK, NC], [1, SPAN + 2]])).then_inc(k.loaded.sem, 16)
                sp.wait_ge(*k.loaded.at(9))

            @block.vector
            def _(dve):
                order = k.dve
                order.enter(dve)
                dve.wait_ge(*k.loaded.at(9))
                dve.memset(ones[:], 1.0)
                dve.tensor_copy(srcf[:], src_int[:])
                order.settle(dve.tensor_copy(dstf[:], dst_int[:]))
                order.settle(dve.tensor_tensor(k.line_same[:], dstf[:, 1:LINE + 2], dstf[:, 0:LINE + 1], ALU.is_equal))
                order.settle(dve.tensor_scalar(k.line_far[:], k.line_same[:], 1.0, FAR, ALU.subtract, ALU.mult))
                order.settle(dve.tensor_scalar(k.line_diag[:], k.ident[0:SP, 0:SP], dstf[:, 1:2], None, ALU.mult))
                order.settle(dve.tensor_scalar(tmp[:, 0:SP], k.ident[0:SP, 0:SP], dstf[:, LINE:LINE + 1], None, ALU.mult))
                dve.sem_inc(k.line_scanned.sem, 2)
                dve.wait_ge(*k.line_carried.at(2))
                first, last = k.bank[1][0:SP, 0:SP], k.bank[2][0:SP, 0:SP]
                dve.scalar_tensor_tensor(k.line_fwd[:], first, dstf[:, LINE:LINE + 1], lt[0:SP, 0:SP], ALU.is_equal, ALU.mult)
                dve.scalar_tensor_tensor(k.line_bwd[:], last, dstf[:, 1:2], gt[0:SP, 0:SP], ALU.is_equal, ALU.mult)
                dve.scalar_tensor_tensor(k.line_far_fwd[:], last, dstf[:, 1:2], gt[0:SP, 0:SP], ALU.is_equal, ALU.mult)
                order.settle(dve.scalar_tensor_tensor(k.line_far_bwd[:], first, dstf[:, LINE:LINE + 1], lt[0:SP, 0:SP], ALU.is_equal, ALU.mult))
                dve.tensor_scalar(k.line_far_fwd[:], k.line_far_fwd[:], 1.0, FAR, ALU.subtract, ALU.mult)
                order.settle(dve.tensor_scalar(k.line_far_bwd[:], k.line_far_bwd[:], 1.0, FAR, ALU.subtract, ALU.mult))
                dve_line_total(dve, k, ones[:], ALU.add, deg[:], 2)
                order.settle(dve.tensor_scalar(tmp[:], deg[:], 1.0, None, ALU.max))
                order.settle(dve.reciprocal(inv[:], tmp[:]))
                order.settle(dve.tensor_scalar(tmp[:], deg[:], 1.0, 1.0, ALU.add, ALU.max))
                dve.sem_inc(k.prepared.sem, 1)
                dve.wait_ge(*k.prepared.at(2))
                order.settle(dve.reciprocal(isd[:], tmp[:]))
                order.settle(dve.tensor_scalar(store[:], dstf[:, 1:LINE + 1], float(2 * k.NP), None, ALU.subtract))
                order.settle(dve.scalar_tensor_tensor(store[:], k.line_same[:, 1:LINE + 1], 0.0, store[:], ALU.is_equal, ALU.mult))
                order.settle(dve.tensor_scalar(store[:], store[:], float(2 * k.NP), None, ALU.add))
                dve.sem_inc(k.prepared.sem, 1)
                order.settle(dve.tensor_tensor(k.same[:], dcols[:, :, 1:SPAN + 2], dcols[:, :, 0:SPAN + 1], ALU.is_equal))
                dve.memset(k.first_col[:, NC:NC + 1], -2.0)
                dve.memset(k.last_col[:, 0:1], -1.0)
                dve.tensor_copy(k.first_col[:, 0:NC], dcols[:, :, 1])
                order.settle(dve.tensor_copy(k.last_col[:, 1:NC + 1], dcols[:, :, SPAN]))
                dve.sem_inc(k.prepared.sem, 1)
                for g in range(GROUPS):
                    for way, out in enumerate((k.first_all, k.last_all)):
                        n = 2 * g + way
                        dve.wait_ge(*k.counted.at(n + 1))
                        order.settle(dve.tensor_copy(out[:, :, g], k.bank[6 + n % 2][:, 0:NC]))
                        dve.sem_inc(k.onehot.sem, 1)

            @block.tensor
            def _(pe):
                pe.wait_ge(*k.line_scanned.at(2))
                pe.matmul(k.bank[1][0:SP, 0:SP], k.line_ones[:], k.line_diag[:], start=True, stop=True
                          ).then_inc(k.line_carried.sem, 1)
                pe.matmul(k.bank[2][0:SP, 0:SP], k.line_ones[:], tmp[:, 0:SP], start=True, stop=True
                          ).then_inc(k.line_carried.sem, 1)
                pe_line_total(pe, k, ALU.add, 2)
                pe.wait_ge(*k.prepared.at(3))
                n = 0
                for line in (dstf[:, 1:LINE + 1], srcf[:], inv[:], isd[:], store[:]):
                    for part in range(4):
                        if n >= 2:
                            pe.wait_ge(*k.turned_used.at(n - 1))
                        pe.transpose(k.bank[3 + n % 2][:, 0:SP], line[:, part * P:(part + 1) * P],
                                     k.ident[0:SP, 0:SP]).then_inc(k.turned.sem, 1)
                        n += 1
                pe.wait_ge(*k.prepared.at(4))
                for g in range(GROUPS):
                    for way, col in enumerate((k.first_col[:, 0:NC], k.last_col[:, 1:NC + 1])):
                        n = 2 * g + way
                        if n >= 2:
                            pe.wait_ge(*k.onehot.at(n - 1))
                        pe.matmul(k.bank[6 + n % 2][:, 0:NC], pick[:, g, :], col, start=True, stop=True
                                  ).then_inc(k.counted.sem, 1)

            @block.scalar
            def _(act):
                act.wait_ge(*k.prepared.at(1))
                act.activation(tmp[:], tmp[:], ACT.Sqrt).then_inc(k.prepared.sem, 1)
                n = 0
                for out in (k.dst_rows, k.src_index, k.inv_deg, k.inv_sqrt_deg, k.store_rows):
                    for part in range(4):
                        gl, b = part // 2, part % 2
                        view = out[:] if len(out.shape) == 3 else out[:].rearrange("p (c q) -> p c q", q=Q)
                        view = view.rearrange("p c (b j l) -> p c b j l", b=2, j=2)[:, :, b, :, gl]
                        act.wait_ge(*k.turned.at(n + 1))
                        act.activation(view, k.bank[3 + n % 2][:, 0:SP].rearrange("p (c j) -> p c j", j=2),
                                       ACT.Copy).then_inc(k.turned_used.sem, 1)
                        n += 1
                act.wait_ge(*k.turned_used.at(n))
                act.activation(k.dst_index[:], k.dst_rows[:].rearrange("p c q -> p (c q)"), ACT.Copy
                               ).then_inc(k.turned_used.sem, 1)
    k.loaded.close(9)
    k.prepared.close(4)
    k.line_scanned.close(4)
    k.line_carried.close(4)
    k.turned.close(20)
    k.turned_used.close(21)
    k.counted.close(8)
    k.onehot.close(8)
    k.dve.close()


def row_of_edge(dve, order, e):
    dve.tensor_scalar(e[:, 1, :], e[:, 0, :], 127, 3, ALU.bitwise_and, ALU.logical_shift_left)
    dve.tensor_scalar(e[:, 2, :], e[:, 0, :], 128, 5, ALU.bitwise_and, ALU.logical_shift_right)
    dve.tensor_scalar(e[:, 3, :], e[:, 0, :], 768, 8, ALU.bitwise_and, ALU.logical_shift_right)
    order.settle(dve.tensor_scalar(e[:, 0, :], e[:, 0, :], 10, 10, ALU.arith_shift_right, ALU.logical_shift_left))
    for part in (1, 2, 3):
        order.settle(dve.tensor_tensor(e[:, 0, :], e[:, 0, :], e[:, part, :], ALU.bitwise_or))


def gather_destinations(k):
    nc, d, NC, JN = k.nc, k.d, k.NC, k.JN
    half = JN // 2
    with ExitStack() as ctx:
        sb = allocator(k, ctx, "dest")
        ring = sb("ring", [P, RING, Q, F])
        index_ring = sb("index_ring", [P, RING, Q], U32)
        iota_lo = sb("iota_lo", [P, JN], F16)
        iota_hi = sb("iota_hi", [P, P], F16)
        before = sb("before", [P, P])
        node = sb("node", [P, JN])
        hi = sb("hi", [P, NC * Q])
        lo = sb("lo", [P, NC * Q])
        fix = sb("fix", [P, NC * Q])
        hi_int = sb("hi_int", [P, NC * Q], I32)
        hot_lo = sb("hot_lo", [P, Q, JN], BF16)
        hot_hi = sb("hot_hi", [P, Q, P], BF16)
        zeros = sb("zeros", [P, max(half, P)], BF16)
        degree = sb("degree", [P, JN])
        upto = sb("upto", [P, JN])
        ones = sb("ones_jn", [P, JN], BF16)
        carry = sb("carry", [P, 1])
        e_int = sb("e_int", [P, 4, JN], I32)
        pos = sb("pos", [P, JN], I32)
        xin = sb("xin", [P, RING, NODE_COLS, F])
        table = sb("table", [P, RING, NODE_COLS, F + 1])
        t = norm_ring(sb, "ln", NODE_COLS)
        LATEST, UNROLL = 1, 4
        kept_alone = NC - (NC + LATEST) // 2
        assert NC % 2 == 1 and (NC + LATEST) % 2 == 0
        counts = [k.bank[0][:, 0:half], k.bank[1][:, 0:half]]
        with nc.Block() as block:
            @block.gpsimd
            def _(pool):
                for c, place, i in chunks(pool, NC):
                    pool.wait_ge(*k.index_set.at(c + 1))
                    pool.wait_ge(*k.ring_free[place].at(i + 1))
                    gather(pool, k, d["x"], ring, index_ring, place)

            @block.scalar
            def _(act):
                start_ring(act, k, k.dst_index, index_ring)
                for place in range(RING):
                    act.sem_inc(k.ring_free[place].sem, 1)

                def keep(c):
                    act.wait_ge(*k.gathered[c.place].at(c.uses + 1))
                    if c.ahead:
                        act_index(act, k, k.dst_index, index_ring, c.n + RING, c.place).then_inc(k.index_set.sem, 1)
                    act.activation(flat(k.state[:, bass.ds(c.n, 1), :]),
                                   ring[:, c.place, :, :].rearrange("p q f -> p (q f)"), ACT.Copy
                                   ).then_inc(k.ring_free[c.place].sem, 1)

                for c, place, i in chunks(act, kept_alone):
                    keep(Chunk(c, place, i, False, True))
                for turn in skewed(act, NC, LATEST, UNROLL):
                    for c in turn.late(1):
                        ln_root(act, k, k.n_ln, c.n, t[c.place])
                    for c in turn.late(0):
                        ln_square(act, k, k.n_ln, c.n, t[c.place])
                    if turn.at % 2:
                        at = kept_alone + turn.at // 2
                        if turn.i is None:
                            keep(Chunk(at, at % RING, at // RING, True, at + RING < NC))
                        else:
                            keep(Chunk(turn.i * (UNROLL // 2) + at, at % RING, turn.i + at // RING, True, True))

            @block.vector
            def _(dve):
                order = k.dve
                order.enter(dve)
                dve.memset(zeros[:], 0.0)
                dve.memset(ones[:], 1.0)
                dst = k.dst_rows[:].rearrange("p c q -> p (c q)")
                order.settle(dve.tensor_scalar(hi[:], dst, 1.0 / JN, 0.5, ALU.mult, ALU.subtract))
                order.settle(dve.tensor_copy(hi_int[:], hi[:]))
                order.settle(dve.tensor_copy(hi[:], hi_int[:]))
                for _ in range(2):
                    order.settle(dve.scalar_tensor_tensor(lo[:], hi[:], -float(JN), dst, ALU.mult, ALU.add))
                    order.settle(dve.tensor_scalar(fix[:], lo[:], 0.0, None, ALU.is_lt))
                    order.settle(dve.tensor_tensor(hi[:], hi[:], fix[:], ALU.subtract))
                    order.settle(dve.tensor_scalar(fix[:], lo[:], float(JN), None, ALU.is_ge))
                    order.settle(dve.tensor_tensor(hi[:], hi[:], fix[:], ALU.add))
                order.settle(dve.scalar_tensor_tensor(lo[:], hi[:], -float(JN), dst, ALU.mult, ALU.add))
                dve.wait_ge(*k.loaded.at(4))
                dve.sem_inc(k.prepared.sem, 1)

                def one_hot(c, q, wait):
                    if wait:
                        dve.wait_ge(*k.counted.at((c - 1) * Q + q + 3))
                    at = bass.ds(c * Q + q, 1)
                    dve.tensor_scalar(hot_hi[:, q, :], iota_hi[:], hi[:, at], None, ALU.is_equal)
                    dve.tensor_scalar(hot_lo[:, q, :], iota_lo[:], lo[:, at], None, ALU.is_equal).then_inc(k.onehot.sem, 1)

                for q in range(Q):
                    one_hot(0, q, False)
                with dve.Fori(0, NC - 1) as c:
                    for q in range(Q):
                        one_hot(c + 1, q, True)
                dve.wait_ge(*k.counted.at(NC * Q + 3))
                for part in range(2):
                    order.settle(dve.tensor_copy(degree[:, part * half:(part + 1) * half], counts[part]))
                order.settle(dve.tensor_tensor_scan(upto[:], ones[:], degree[:], 0.0, ALU.mult, ALU.add))
                dve.sem_inc(k.onehot.sem, 1)
                dve.wait_ge(*k.counted.at(NC * Q + 4))
                order.settle(dve.tensor_scalar(carry[:], k.bank[2][:, 0:1], 1.0, None, ALU.subtract))
                order.settle(dve.tensor_scalar(upto[:], upto[:], carry[:], None, ALU.add))
                order.settle(dve.tensor_copy(e_int[:, 0, :], upto[:]))
                row_of_edge(dve, order, e_int)
                order.settle(dve.tensor_copy(upto[:], e_int[:, 0, :]))
                order.settle(dve.scalar_tensor_tensor(upto[:], upto[:], float(k.NP), node[:], ALU.add, ALU.subtract))
                order.settle(dve.scalar_tensor_tensor(upto[:], degree[:], 0.0, upto[:], ALU.is_gt, ALU.mult))
                order.settle(dve.tensor_tensor(pos[:], upto[:], node[:], ALU.add))
                order.close()
                for turn in skewed(dve, NC, LATEST, UNROLL):
                    order.enter_turn(dve, turn, 2)
                    for c in turn.late(0):
                        dve.wait_ge(*k.n_loaded[c.place].at(c.uses + 1))
                        ln_centre(dve, k, k.n_ln, xin[:, c.place, :, :], NODE_COLS, t[c.place])
                    for c in turn.late(1):
                        dve.wait_ge(*k.n_stored[c.place].at(c.uses + 1))
                        dve.tensor_copy(table[:, c.place, :, F].bitcast(I32), pos[:, bass.ds(c.n * NODE_COLS, NODE_COLS)])
                        ln_scale(dve, k, k.n_ln, c.n, NODE_COLS, t[c.place], table[:, c.place, :, 0:F]
                                 ).then_inc(k.n_out.sem, 1)
                    for c in turn.late(0):
                        ln_variance(dve, k, k.n_ln, c.n, t[c.place])
                    order.leave_turn(turn, 2)

            @block.tensor
            def _(pe):
                pe.wait_ge(*k.prepared.at(1))
                for part in range(2):
                    pe.matmul(counts[part], zeros[:, 0:P], zeros[:, 0:half], start=True, stop=False
                              ).then_inc(k.counted.sem, 1)
                with pe.Fori(0, NC) as c:
                    for q in range(Q):
                        pe.wait_ge(*k.onehot.at(c * Q + q + 1))
                        pe.matmul(counts[0], hot_hi[:, q, :], hot_lo[:, q, 0:half], start=False, stop=False)
                        pe.matmul(counts[1], hot_hi[:, q, :], hot_lo[:, q, half:JN], start=False, stop=False
                                  ).then_inc(k.counted.sem, 1)
                for part in range(2):
                    last = pe.matmul(counts[part], zeros[:, 0:P], zeros[:, 0:half], start=False, stop=True)
                last.then_inc(k.counted.sem, 1)
                pe.wait_ge(*k.onehot.at(NC * Q + 1))
                pe.matmul(k.bank[2][:, 0:1], before[:], upto[:, JN - 1:JN], start=True, stop=True
                          ).then_inc(k.counted.sem, 1)

            @block.sync
            def _(sp):
                sp.dma_start(iota_lo[:], d["count_up"][0:JN].partition_broadcast(P)).then_inc(k.loaded.sem, 16)
                sp.dma_start(iota_hi[:], d["count_up"][0:P].partition_broadcast(P)).then_inc(k.loaded.sem, 16)
                sp.dma_start(before[:], d["below"]).then_inc(k.loaded.sem, 16)
                sp.dma_start(node[:], d["node_number"]).then_inc(k.loaded.sem, 16)
                def fetch(c, place):
                    sp.dma_start(xin[:, place, :, :].rearrange("p n f -> p (n f)"), node_rows(d["x"], c, k.NP)
                                 ).then_inc(k.n_loaded[place].sem, 16)

                for place in range(RING):
                    sp.sem_inc(k.n_stored[place].sem, 16)
                    fetch(place, place)
                for turn in skewed(sp, NC, LATEST, UNROLL):
                    for c in turn.late(0):
                        if c.ahead:
                            sp.wait_ge(*k.n_ln.centred.at(c.n + 1))
                            fetch(c.n + RING, c.place)
                    for c in turn.late(1):
                        sp.wait_ge(*k.n_out.at(c.n + 1))
                        sp.dma_start(node_rows(k.t01, c.n, k.NP), table[:, c.place, :, :].rearrange("p n f -> p (n f)")
                                     ).then_inc(k.n_stored[c.place].sem, 16)
                wait_ring(sp, k.n_stored, NC, 1)
    close_ring(k.gathered, NC)
    close_ring(k.ring_free, NC, 1)
    k.index_set.close(NC)
    k.loaded.close(4)
    k.prepared.close(1)
    k.counted.close(NC * Q + 4)
    k.onehot.close(NC * Q + 1)
    ln_close(k.n_ln, NC)
    k.n_out.close(NC)
    close_ring(k.n_stored, NC, 1)
    close_ring(k.n_loaded, NC)


def layer0(k):
    nc, d, NC = k.nc, k.d, k.NC
    with ExitStack() as ctx:
        sb = allocator(k, ctx, "l0")
        ring = sb("ring", [P, RING, Q, F + 1])
        index_ring = sb("index_ring", [P, RING, Q], U32)
        rows = sb("rows", [P, SPAN])
        x1 = sb("x1", [P, Q, F])
        out = sb("out", [P, RING, Q, F + 1])
        s = SumRing(sb)
        te = norm_ring(sb, "lne", Q)
        n_h = sb("n_h", [P, RING, NODE_COLS, F + 1])
        n_rows = sb("n_rows", [P, NODE_COLS, F])
        n_kept = sb("n_kept", [P, RING, 4 * P])
        n_x = sb("n_x", [P, RING, NODE_COLS * F])
        n_out = sb("n_out", [P, RING, NODE_COLS, F])
        tn = norm_ring(sb, "lnn", NODE_COLS)
        columns, carry, projected = k.bank[0][:, 0:SPAN], k.bank[0][:, SPAN:SPAN + 1], k.bank[1][:, 0:SPAN]
        n_columns, n_projected = k.bank[2], k.bank[3]
        LATEST = 2

        with nc.Block() as block:
            @block.gpsimd
            def _(pool):
                for c, place, i in chunks(pool, NC):
                    pool.wait_ge(*k.index_set.at(c + 1))
                    pool.wait_ge(*k.ring_free[place].at(i + 1))
                    gather(pool, k, k.t01[0:k.NP, :], ring, index_ring, place)

            @block.scalar
            def _(act):
                start_ring(act, k, k.src_index, index_ring)
                for place in range(RING):
                    act.sem_inc(k.ring_free[place].sem, 1)
                for turn in skewed(act, NC, LATEST):
                    for c in turn.late(2):
                        ln_root(act, k, k.e_ln, c.n, te[c.place])
                    for c in turn.late(0):
                        act.wait_ge(*k.h_loaded[c.place].at(c.uses + 1))
                        act.activation(n_rows[:], n_h[:, c.place, :, 0:F], ACT.Copy).then_inc(k.n_rows.sem, 1)
                    for c in turn.late(2):
                        ln_root(act, k, k.n_ln, c.n, tn[c.place])
                    for c in turn.late(1):
                        act.wait_ge(*k.scanned.at(c.n + 1))
                        act.activation(k.sums0[:, bass.ds(c.n * SPAN, SPAN)], s.sums[:, c.place, :], ACT.Copy)
                    for c in turn.late(0):
                        act.wait_ge(*k.gathered[c.place].at(c.uses + 1))
                        act.activation(rows[:].rearrange("p (q f) -> p q f", f=F), ring[:, c.place, :, 0:F], ACT.Copy
                                       ).then_inc(k.rows_ready.sem, 1)
                        if c.ahead:
                            act_index(act, k, k.src_index, index_ring, c.n + RING, c.place).then_inc(k.index_set.sem, 1)
                        act.activation(k.table_index[:, bass.ds(c.n * Q, Q)], ring[:, c.place, :, F].bitcast(I32), ACT.Copy
                                       ).then_inc(k.ring_free[c.place].sem, 1)
                        act.wait_ge(*k.n_columns.at(c.n + 1))
                        act.activation(n_kept[:, c.place, :], n_columns[:], ACT.Copy).then_inc(k.n_columns_kept.sem, 1)
                    for c in turn.late(1):
                        ln_square(act, k, k.n_ln, c.n, tn[c.place])
                        ln_square(act, k, k.e_ln, c.n, te[c.place])

            @block.tensor
            def _(pe):
                for turn in skewed(pe, NC, LATEST):
                    for c in turn.late(1):
                        pe.wait_ge(*k.n_columns_kept.at(c.n + 1))
                        if not c.first:
                            pe.wait_ge(*k.n_ln.centred.at(c.n))
                        for part in range(4):
                            at = slice(part * P, (part + 1) * P)
                            pe.matmul(n_projected[:, at], n_kept[:, c.place, at], k.w1[:], start=True, stop=False)
                            last = pe.matmul(n_projected[:, at], k.ones_row[:], k.b1_row[:, at], start=False, stop=True)
                        last.then_inc(k.n_projected.sem, 1)
                        pe.wait_ge(*k.scanned.at(c.n + 1))
                        pe_project(pe, s.sums[:, c.place, :], k.w0, projected).then_inc(k.projected.sem, 1)
                    for c in turn.late(0):
                        pe.wait_ge(*k.n_rows.at(c.n + 1))
                        for part in range(4):
                            last = pe.transpose(n_columns[:, part * P:(part + 1) * P],
                                                n_rows[:].rearrange("p n f -> p (n f)")[:, part * P:(part + 1) * P], k.ident[:])
                        last.then_inc(k.n_columns.sem, 1)
                        pe.wait_ge(*k.rows_ready.at(c.n + 1))
                        pe_turn(pe, k, rows, columns).then_inc(k.columns_ready.sem, 1)
                        pe_carry(pe, k, s, c.n, s.last(c.place), carry)

            @block.vector
            def _(dve):
                order = k.dve
                order.enter(dve)
                order.settle(dve.memset(s.sums[:], 0.0))
                for place in range(RING):
                    order.settle(dve.memset(out[:, place, :, F], 0.0))
                order.close()
                for turn in skewed(dve, NC, LATEST):
                    order.enter_turn(dve, turn, 6)
                    for c in turn.late(1):
                        dve.wait_ge(*k.n_loaded[c.place].at(c.uses + 1))
                        dve.wait_ge(*k.n_projected.at(c.n + 1))
                        order.settle(dve.tensor_tensor(n_x[:, c.place, :], n_x[:, c.place, :], n_projected[:], ALU.add))
                        ln_centre(dve, k, k.n_ln, n_x[:, c.place, :].rearrange("p (n f) -> p n f", f=F), NODE_COLS,
                                  tn[c.place])
                    for c in turn.late(2):
                        dve.wait_ge(*k.e_stored[c.place].at(c.uses + 1))
                        ln_scale(dve, k, k.e_ln, c.n, Q, te[c.place], out[:, c.place, :, 0:F]).then_inc(k.e_out.sem, 1)
                    for c in turn.late(0):
                        dve_scan_alone(dve, k, s, c.n, columns)
                    for c in turn.late(1):
                        dve.wait_ge(*k.projected.at(c.n + 1))
                        order.settle(dve.tensor_tensor(x1[:].rearrange("p q f -> p (q f)"),
                                                       flat(k.state[:, bass.ds(c.n, 1), :]), projected, ALU.add))
                        ln_centre(dve, k, k.e_ln, x1[:], Q, te[c.place])
                    for c in turn.late(2):
                        dve.wait_ge(*k.n_stored[c.place].at(c.uses + 1))
                        ln_scale(dve, k, k.n_ln, c.n, NODE_COLS, tn[c.place], n_out[:, c.place, :, :]).then_inc(k.n_out.sem, 1)
                    for c in turn.late(0):
                        dve_scan(dve, k, c.n, columns, carry, s.sums[:, c.place, :])
                    for c in turn.late(1):
                        ln_variance(dve, k, k.n_ln, c.n, tn[c.place])
                        ln_variance(dve, k, k.e_ln, c.n, te[c.place])
                    order.leave_turn(turn, 6)

            @block.sync
            def _(sp):
                def fetch_x(c, place):
                    sp.dma_start(n_x[:, place, :], node_rows(d["x"], c, k.NP)).then_inc(k.n_loaded[place].sem, 16)

                def fetch_h(c, place):
                    sp.dma_start(n_h[:, place, :, :].rearrange("p n f -> p (n f)"), node_rows(k.t01, c, k.NP)
                                 ).then_inc(k.h_loaded[place].sem, 16)

                for place in range(RING):
                    sp.sem_inc(k.n_stored[place].sem, 16)
                    sp.sem_inc(k.e_stored[place].sem, 16)
                    fetch_h(place, place)
                    fetch_x(place, place)
                for turn in skewed(sp, NC, LATEST):
                    for c in turn.late(0):
                        if c.ahead:
                            sp.wait_ge(*k.n_rows.at(c.n + 1))
                            fetch_h(c.n + RING, c.place)
                    for c in turn.late(1):
                        sp.wait_ge(*k.n_ln.centred.at(c.n + 1))
                        sp.dma_start(node_rows(k.xa, c.n, k.NP), n_x[:, c.place, :]).then_inc(k.x_stored[c.place].sem, 16)
                    for c in turn.late(2):
                        sp.wait_ge(*k.e_out.at(c.n + 1))
                        sp.dma_start(edge_rows(k.t01, k.NP, c.n), out[:, c.place, :, :].rearrange("p q f -> p (q f)")
                                     ).then_inc(k.e_stored[c.place].sem, 16)
                        sp.wait_ge(*k.n_out.at(c.n + 1))
                        sp.dma_start(node_rows(k.t2, c.n, k.NP), n_out[:, c.place, :, :].rearrange("p n f -> p (n f)")
                                     ).then_inc(k.n_stored[c.place].sem, 16)
                        if c.ahead:
                            sp.wait_ge(*k.x_stored[c.place].at(c.uses + 1))
                            fetch_x(c.n + RING, c.place)
                wait_ring(sp, k.x_stored, NC)
                wait_ring(sp, k.n_stored, NC, 1)
                wait_ring(sp, k.e_stored, NC, 1)
    close_ring(k.gathered, NC)
    close_ring(k.ring_free, NC, 1)
    for signal in (k.index_set, k.n_rows, k.rows_ready, k.n_columns, k.n_columns_kept, k.n_projected, k.n_out, k.e_out,
                   k.projected):
        signal.close(NC)
    close_sums(k)
    ln_close(k.n_ln, NC)
    ln_close(k.e_ln, NC)
    close_ring(k.n_loaded, NC)
    close_ring(k.h_loaded, NC)
    close_ring(k.x_stored, NC)
    close_ring(k.n_stored, NC, 1)
    close_ring(k.e_stored, NC, 1)


def wait_twice(eng, signals, n, more=0):
    for place, s in enumerate(signals):
        eng.wait_ge(*s.at(2 * (len(range(place, n, RING)) + more)))


def close_sums(k):
    for signal in (k.columns_ready, k.scanned_alone, k.carried, k.scanned):
        signal.close(k.NC)


def pe_project(pe, sums, weight, out):
    for h in range(HALVES):
        last = pe.matmul(out[:, h * P:(h + 1) * P], sums[:, h * P:(h + 1) * P], weight[:], start=True, stop=True)
    return last


def layer1_logits(k):
    nc, d, NC = k.nc, k.d, k.NC
    with ExitStack() as ctx:
        sb = allocator(k, ctx, "l1a")
        ring = sb("ring", [P, RING, Q, F + 1])
        index_ring = sb("index_ring", [P, RING, Q], U32)
        rows = sb("rows", [P, SPAN])
        goes_on = sb("goes_on", [P, SPAN], BF16)
        ends = sb("ends", [P, SPAN])
        x1 = sb("x1", [P, RING, Q, F])
        h1 = sb("h1", [P, RING, Q, F])
        kept = sb("kept", [P, RING, 2 * SPAN])
        hidden = sb("hidden", [P, RING, 2, 2 * SPAN])
        attr = sb("attr", [P, RING, 2 * Q, F])
        gap = sb("gap", [P, RING, 2 * Q, F])
        top = sb("top", [P, 2 * Q])
        s = SumRing(sb)
        t = norm_ring(sb, "ln", Q)
        carry, projected, both = k.bank[0][:, 0:1], k.bank[1][:, 0:SPAN], k.bank[2]
        en, z, own, logit = k.bank[3], k.bank[4], k.bank[5][:, 0:SPAN], k.bank[6][:, 0:2 * Q]
        REV = NC - 1
        LATEST = 4

        with nc.Block() as block:
            @block.gpsimd
            def _(pool):
                for m, place, i in chunks(pool, NC):
                    pool.wait_ge(*k.index_set.at(m + 1))
                    pool.wait_ge(*k.ring_free[place].at(i + 1))
                    gather(pool, k, k.t01, ring, index_ring, place)

            @block.scalar
            def _(act):
                start_ring(act, k, k.table_index, index_ring, REV)
                for place in range(RING):
                    act.sem_inc(k.ring_free[place].sem, 1)
                for turn in skewed(act, NC, LATEST):
                    for m in turn.late(2):
                        ln_root(act, k, k.e_ln, m.n, t[m.place])
                        act.wait_ge(*k.gathered[m.place].at(m.uses + 1))
                        if m.ahead:
                            act_index(act, k, k.table_index, index_ring, m.n + RING, m.place, REV
                                      ).then_inc(k.index_set.sem, 1)
                        act.activation(rows[:].rearrange("p (q f) -> p q f", f=F), ring[:, m.place, :, 0:F], ACT.Copy
                                       ).then_inc(k.rows_ready.sem, 1)
                        act.wait_ge(*k.rows_ready.at(m.n + 1))
                        act.sem_inc(k.ring_free[m.place].sem, 1)
                    for m in turn.late(3):
                        act.wait_ge(*k.e_hidden.at(m.n + 1))
                        act.activation(hidden[:, m.place, 0, :], z[:], ACT.Identity, bias=k.bz[:, 0:1])
                        act.activation(hidden[:, m.place, 1, :], z[:], ACT.Relu, bias=k.bz[:, 0:1]
                                       ).then_inc(k.e_hidden_kept.sem, 1)
                    for m in turn.late(4):
                        act.wait_ge(*k.e_logits.at(m.n + 1))
                        planes = k.logits[:].rearrange("p (l b h) n -> p l b h n", l=2, b=2)
                        for b in range(HALVES):
                            last = act.activation(
                                planes[:, :, b, :, bass.ds((m.n * -1 + REV) * 2, 2)].rearrange("p l h j -> p j l h"),
                                logit[:, b * Q:(b + 1) * Q].rearrange("p (j l h) -> p j l h", j=2, l=2), ACT.Copy)
                        last.then_inc(k.e_logits_kept.sem, 1)
                    for m in turn.late(2):
                        act.wait_ge(*k.e_columns.at(m.n + 1))
                        act.activation(kept[:, m.place, :], both[:], ACT.Copy).then_inc(k.e_columns_kept.sem, 1)
                    for m in turn.late(1):
                        act.wait_ge(*k.e_ln.centred.at(m.n + 1))
                        act.activation(flat(k.state[:, bass.ds(m.n * -1 + REV, 1), :]),
                                       x1[:, m.place, :, :].rearrange("p q f -> p (q f)"), ACT.Copy)
                        ln_square(act, k, k.e_ln, m.n, t[m.place])

            @block.tensor
            def _(pe):
                for turn in skewed(pe, NC, LATEST):
                    for m in turn.late(4):
                        pe.wait_ge(*k.e_hidden_kept.at(m.n + 1))
                        if not m.first:
                            pe.wait_ge(*k.e_logits_kept.at(m.n))
                        for h in range(HALVES):
                            for j in range(2):
                                for part in range(2):
                                    last = pe.matmul(logit[:, h * Q + j * 4:h * Q + j * 4 + 4],
                                                     hidden[:, m.place, part, j * SPAN + h * P:j * SPAN + (h + 1) * P],
                                                     k.attn_parts[:, part, :], start=(part == 0), stop=(part == 1))
                        last.then_inc(k.e_logits.sem, 1)
                    for m in turn.late(1):
                        pe.wait_ge(*k.scanned.at(m.n + 1))
                        pe_project(pe, s.sums[:, m.place, :], k.w0, projected).then_inc(k.projected.sem, 1)
                    for m in turn.late(3):
                        pe.wait_ge(*k.e_columns_kept.at(m.n + 1))
                        for j in range(2):
                            at = slice(j * SPAN, (j + 1) * SPAN)
                            pe.matmul(z[:, at], k.w2s[:, j * P:(j + 1) * P], kept[:, m.place, SPAN:2 * SPAN],
                                      start=True, stop=False)
                            last = pe.matmul(z[:, at], k.w2d[:, j * P:(j + 1) * P], kept[:, m.place, 0:SPAN],
                                             start=False, stop=True)
                        last.then_inc(k.e_hidden.sem, 1)
                        if not m.first:
                            pe.wait_ge(*k.e_gap.at(m.n))
                        for h in range(HALVES):
                            at = slice(h * P, (h + 1) * P)
                            pe.matmul(own[:, at], kept[:, m.place, at], k.w1[:], start=True, stop=False)
                            last = pe.matmul(own[:, at], k.ones_row[:], k.b1_row[:, at], start=False, stop=True)
                        for h in range(HALVES):
                            at = slice(h * 2 * P, (h + 1) * 2 * P)
                            pe.matmul(en[:, at], kept[:, m.place, SPAN + h * P:SPAN + (h + 1) * P], k.w2s[:],
                                      start=True, stop=False)
                            last = pe.matmul(en[:, at], k.ones_row[:], k.b2s_row[:, at], start=False, stop=True)
                        last.then_inc(k.e_en.sem, 1)
                    for m in turn.late(0):
                        pe.wait_ge(*k.scanned_alone.at(m.n + 1))
                        pe.matmul(carry, s.carry[:, 0, :], s.alone[:, 0:1], start=True, stop=False)
                        pe.matmul(carry, s.carry[:, 1, :], s.sums[:, 1 - m.place, 0:1], start=False, stop=True
                                  ).then_inc(k.carried.sem, 1)
                    for m in turn.late(2):
                        pe.wait_ge(*k.rows_ready.at(m.n + 1))
                        pe_turn(pe, k, rows, both[:, SPAN:2 * SPAN])
                        pe.wait_ge(*k.e_out.at(m.n + 1))
                        pe_turn(pe, k, h1[:, m.place, :, :].rearrange("p q f -> p (q f)"), both[:, 0:SPAN]
                                ).then_inc(k.e_columns.sem, 1)

            @block.vector
            def _(dve):
                order = k.dve
                order.enter(dve)
                order.settle(dve.memset(s.sums[:], 0.0))
                order.close()
                for turn in skewed(dve, NC, LATEST):
                    order.enter_turn(dve, turn, 8)
                    for m in turn.late(2):
                        ln_scale(dve, k, k.e_ln, m.n, Q, t[m.place], h1[:, m.place, :, :]).then_inc(k.e_out.sem, 1)
                    for m in turn.late(1):
                        dve.wait_ge(*k.projected.at(m.n + 1))
                        order.settle(dve.tensor_tensor(x1[:, m.place, :, :].rearrange("p q f -> p (q f)"),
                                                       flat(k.state[:, bass.ds(m.n * -1 + REV, 1), :]), projected, ALU.add))
                        ln_centre(dve, k, k.e_ln, x1[:, m.place, :, :], Q, t[m.place])
                    for m in turn.late(0):
                        c = m.n * -1 + REV
                        groups = spread(k.last_all[:, bass.ds(c, 1), :].rearrange("p o g -> p (o g)"), GROUPS, F)
                        for n, (pattern, col) in enumerate(((BACKWARD, c), (BACKWARD_AFTER, c + 1))):
                            dve.scalar_tensor_tensor(s.carry[:, n, :].rearrange("p (g f) -> p g f", g=GROUPS), groups,
                                                     k.first_col[:, bass.ds(col, 1)],
                                                     k.carry_base[:, pattern, :].rearrange("p (g f) -> p g f", g=GROUPS),
                                                     ALU.is_equal, ALU.mult)
                        after = flat(k.same[:, bass.ds(c, 1), 1:SPAN + 1])
                        order.note(dve.tensor_copy(goes_on[:], after))
                        order.settle(dve.scalar_tensor_tensor(ends[:], after, 0.0, k.sums0[:, bass.ds(c * SPAN, SPAN)],
                                                              ALU.is_equal, ALU.mult))
                        dve.tensor_tensor_scan(s.alone[:, ::-1], goes_on[:, ::-1], ends[:, ::-1], 0.0, ALU.mult, ALU.add
                                               ).then_inc(k.scanned_alone.sem, 1)
                    for m in turn.late(3):
                        dve.wait_ge(*k.e_loaded[m.place].at(m.uses + 1))
                        dve.wait_ge(*k.e_stored[m.place].at(m.uses + 1))
                        dve.wait_ge(*k.e_en.at(m.n + 1))
                        state = flat(k.state[:, bass.ds(m.n * -1 + REV, 1), :])
                        order.note(dve.tensor_tensor(state, state, own, ALU.add))
                        order.settle(dve.tensor_tensor(attr[:, m.place, :, :], attr[:, m.place, :, :],
                                                       en[:].rearrange("p (n f) -> p n f", f=F), ALU.mult))
                        order.settle(dve.tensor_reduce(top[:], attr[:, m.place, :, :], AX, ALU.max))
                        dve.tensor_tensor(gap[:, m.place, :, :], attr[:, m.place, :, :], spread(top[:], 2 * Q, F), ALU.subtract
                                          ).then_inc(k.e_gap.sem, 1)
                    for m in turn.late(0):
                        dve.wait_ge(*k.carried.at(m.n + 1))
                        dve.tensor_tensor_scan(s.sums[:, m.place, ::-1], goes_on[:, ::-1], ends[:, ::-1], carry, ALU.mult, ALU.add
                                               ).then_inc(k.scanned.sem, 1)
                    for m in turn.late(1):
                        ln_variance(dve, k, k.e_ln, m.n, t[m.place])
                    order.leave_turn(turn, 8)

            @block.sync
            def _(sp):
                def fetch(m, place):
                    sp.dma_start(attr[:, place, :, :].rearrange("p n f -> p (n f)"), edge_rows(k.attr_sorted, 0, m * -1 + REV)
                                 ).then_inc(k.e_loaded[place].sem, 16)

                sp.wait_ge(*k.attr_ready.at(1))
                for place in range(RING):
                    sp.sem_inc(k.e_stored[place].sem, 16)
                    fetch(place, place)
                for m, place, i, ahead in chunks_ahead(sp, NC):
                    sp.wait_ge(*k.e_gap.at(m + 1))
                    sp.dma_start(edge_rows(k.gap_rows, 0, m * -1 + REV), gap[:, place, :, :].rearrange("p n f -> p (n f)")
                                 ).then_inc(k.e_stored[place].sem, 16)
                    if ahead:
                        fetch(m + RING, place)
                wait_ring(sp, k.e_stored, NC, 1)
    close_ring(k.gathered, NC)
    close_ring(k.ring_free, NC, 1)
    for signal in (k.index_set, k.rows_ready, k.e_columns, k.e_columns_kept, k.e_hidden, k.e_hidden_kept, k.e_logits,
                   k.e_en, k.e_logits_kept, k.e_out, k.e_gap, k.projected, k.scanned_alone, k.carried, k.scanned):
        signal.close(NC)
    ln_close(k.e_ln, NC)
    close_ring(k.e_loaded, NC)
    close_ring(k.e_stored, NC, 1)


def layer1_softmax(k):
    nc, NC, SP = k.nc, k.NC, k.SP
    with ExitStack() as ctx:
        sb = allocator(k, ctx, "l1s")
        logit = sb("logit", [SP, 2, LINE])
        top = sb("top", [SP, LINE])
        guarded = sb("guarded", [SP, LINE])
        finite = sb("finite", [SP, LINE], I32)
        raised = sb("raised", [SP, 2, LINE])
        total = sb("total", [SP, LINE])
        alpha = sb("alpha", [SP, 2, LINE])
        with nc.Block() as block:
            @block.vector
            def _(dve):
                order = k.dve
                order.enter(dve)
                for h in range(2):
                    dve.wait_ge(*k.turned_used.at(h + 1))
                    dve_line_total(dve, k, logit[:, h, :], ALU.max, top[:], 2 * h)
                    order.settle(dve.tensor_scalar(guarded[:], top[:], 0.0, None, ALU.mult))
                    order.settle(dve.tensor_scalar(finite[:], guarded[:], 0.0, None, ALU.is_equal))
                    order.settle(dve.memset(guarded[:], 0.0))
                    order.settle(dve.copy_predicated(guarded[:], finite[:], top[:]))
                    dve.tensor_tensor(logit[:, h, :], logit[:, h, :], guarded[:], ALU.subtract).then_inc(k.weighted.sem, 1)
                for h in range(2):
                    dve.wait_ge(*k.raised.at(h + 1))
                    dve_line_total(dve, k, raised[:, h, :], ALU.add, total[:], 4 + 2 * h)
                    order.settle(dve.tensor_scalar(total[:], total[:], 1e-9, None, ALU.max))
                    order.settle(dve.reciprocal(total[:], total[:]))
                    dve.tensor_tensor(alpha[:, h, :], raised[:, h, :], total[:], ALU.mult).then_inc(k.summed.sem, 1)

            @block.scalar
            def _(act):
                for h in range(2):
                    act.wait_ge(*k.turned.at(4 * (h + 1)))
                    act.activation(logit[:, h, :], k.bank[3 + h][0:SP, :], ACT.Copy).then_inc(k.turned_used.sem, 1)
                for h in range(2):
                    act.wait_ge(*k.weighted.at(h + 1))
                    act.activation(raised[:, h, :], logit[:, h, :], ACT.Exp).then_inc(k.raised.sem, 1)
                view = k.alpha[:].rearrange("p c (b j l h) -> p c b j l h", b=2, j=2, l=2)
                for h in range(2):
                    for part in range(4):
                        gl, b, n = part // 2, part % 2, 4 * h + part
                        act.wait_ge(*k.turned.at(8 + n + 1))
                        act.activation(view[:, :, b, :, gl, h], k.bank[5 + n % 2][:, 0:SP].rearrange("p (c j) -> p c j", j=2),
                                       ACT.Copy).then_inc(k.turned_used.sem, 1)

            @block.tensor
            def _(pe):
                for h in range(2):
                    for part in range(4):
                        pe.transpose(k.bank[3 + h][0:SP, part * P:(part + 1) * P], k.logits[:, 2 * part + h, :], k.ident[:]
                                     ).then_inc(k.turned.sem, 1)
                for turn, op in enumerate((ALU.max, ALU.max, ALU.add, ALU.add)):
                    pe_line_total(pe, k, op, 2 * turn)
                for h in range(2):
                    pe.wait_ge(*k.summed.at(h + 1))
                    for part in range(4):
                        n = 4 * h + part
                        if n >= 2:
                            pe.wait_ge(*k.turned_used.at(2 + n - 1))
                        pe.transpose(k.bank[5 + n % 2][:, 0:SP], alpha[:, h, part * P:(part + 1) * P],
                                     k.ident[0:SP, 0:SP]).then_inc(k.turned.sem, 1)
    k.line_scanned.close(8)
    k.line_carried.close(8)
    k.turned.close(16)
    k.turned_used.close(10)
    for signal in (k.weighted, k.raised, k.summed):
        signal.close(2)
    k.dve.close()


def layer1_sums(k):
    nc, NC = k.nc, k.NC
    with ExitStack() as ctx:
        sb = allocator(k, ctx, "l1b")
        gap = sb("gap", [P, RING, 2 * Q, F])
        scaled = sb("scaled", [P, RING, 2 * Q, F])
        raised = sb("raised", [P, RING, 2 * Q, F])
        msg = sb("msg", [P, RING, HALVES, 2, GROUPS, F])
        total = sb("total", [P, RING, 2 * Q])
        inv = sb("inv", [P, RING, 2 * Q])
        var = sb("var", [P, RING, Q])
        power = sb("power", [P, Q])
        x2 = sb("x2", [P, RING, Q, F])
        out = sb("out", [P, RING, Q, F])
        s = SumRing(sb)
        t = norm_ring(sb, "ln", Q)
        columns = [k.bank[place][:, 0:SPAN] for place in range(RING)]
        carry = [k.bank[place][:, SPAN:SPAN + 1] for place in range(RING)]
        projected = [k.bank[RING + place][:, 0:SPAN] for place in range(RING)]
        LATEST = 4

        with nc.Block() as block:
            @block.gpsimd
            def _(pool):
                for place in range(RING):
                    pool.sem_inc(k.ring_free[place].sem, 1)
                pool.memset(power[:], -0.5).then_inc(k.prepared.sem, 1)
                pool.wait_ge(*k.prepared.at(1))
                for turn in skewed(pool, NC, LATEST):
                    for c in turn.late(0):
                        pool.wait_ge(*k.e_loaded[c.place].at(c.uses + 1))
                        if c.again:
                            pool.wait_ge(*k.raised.at(c.n - 1))
                        pool.tensor_tensor(scaled[:, c.place, :, :], gap[:, c.place, :, :],
                                           spread(flat(k.alpha[:, bass.ds(c.n, 1), :]), 2 * Q, F), ALU.mult
                                           ).then_inc(k.weighted.sem, 1)
                    for c in turn.late(1):
                        pool.wait_ge(*k.summed.at(c.n + 1))
                        if c.again:
                            pool.wait_ge(*k.columns_ready.at(c.n - 1))
                        for b in range(HALVES):
                            last = pool.tensor_tensor(
                                msg[:, c.place, b, :, :, :].rearrange("p h g f -> p g h f"),
                                raised[:, c.place, b * Q:(b + 1) * Q, :].rearrange("p (g h) f -> p g h f", h=2),
                                inv[:, c.place, b * Q:(b + 1) * Q].rearrange("p (g h) -> p g h", h=2).unsqueeze(3)
                                .to_broadcast([P, GROUPS, 2, F]), ALU.mult)
                        last.then_inc(k.rows_ready.sem, 1)
                    for c in turn.late(4):
                        pool.wait_ge(*k.e_ln.varied.at(c.n + 1))
                        pool.tensor_tensor(t[c.place].inv, var[:, c.place, :], power[:], ALU.pow
                                           ).then_inc(k.e_ln.rooted.sem, 1)

            @block.scalar
            def _(act):
                for turn in skewed(act, NC, LATEST):
                    for c in turn.late(0):
                        act.wait_ge(*k.weighted.at(c.n + 1))
                        if c.again:
                            act.wait_ge(*k.rows_ready.at(c.n - 1))
                        act.activation(raised[:, c.place, :, :], scaled[:, c.place, :, :], ACT.Exp
                                       ).then_inc(k.raised.sem, 1)
                    for c in turn.late(3):
                        act.wait_ge(*k.e_ln.centred.at(c.n + 1))
                        act.activation(flat(k.state[:, bass.ds(c.n, 1), :]),
                                       x2[:, c.place, :, :].rearrange("p q f -> p (q f)"), ACT.Copy)
                        ln_square(act, k, k.e_ln, c.n, t[c.place])

            @block.tensor
            def _(pe):
                for turn in skewed(pe, NC, LATEST):
                    for c in turn.late(3):
                        pe.wait_ge(*k.scanned.at(c.n + 1))
                        pe_project(pe, s.sums[:, c.place, :], k.w1, projected[c.place]).then_inc(k.projected.sem, 1)
                    for c in turn.late(2):
                        pe.wait_ge(*k.rows_ready.at(c.n + 1))
                        for b in range(HALVES):
                            for h in range(2):
                                last = pe.matmul(columns[c.place][:, b * P:(b + 1) * P],
                                                 msg[:, c.place, b, h, :, :].rearrange("p g f -> p (g f)"),
                                                 k.ident[:], start=(h == 0), stop=(h == 1))
                        last.then_inc(k.columns_ready.sem, 1)
                        pe_carry(pe, k, s, c.n, s.last(c.place), carry[c.place])

            @block.vector
            def _(dve):
                order = k.dve
                order.enter(dve)
                order.settle(dve.memset(s.sums[:], 0.0))
                order.close()
                for turn in skewed(dve, NC, LATEST):
                    order.enter_turn(dve, turn, 4)
                    for c in turn.late(1):
                        dve.wait_ge(*k.raised.at(c.n + 1))
                        order.settle(dve.tensor_reduce(total[:, c.place, :], raised[:, c.place, :, :], AX, ALU.add))
                        dve.reciprocal(inv[:, c.place, :], total[:, c.place, :]).then_inc(k.summed.sem, 1)
                    for c in turn.late(2):
                        dve_scan_alone(dve, k, s, c.n, columns[c.place])
                    for c in turn.late(3):
                        dve.wait_ge(*k.projected.at(c.n + 1))
                        order.settle(dve.tensor_tensor(x2[:, c.place, :, :].rearrange("p q f -> p (q f)"),
                                                       flat(k.state[:, bass.ds(c.n, 1), :]), projected[c.place], ALU.add))
                        ln_centre(dve, k, k.e_ln, x2[:, c.place, :, :], Q, t[c.place])
                    for c in turn.late(2):
                        dve_scan(dve, k, c.n, columns[c.place], carry[c.place], s.sums[:, c.place, :])
                    for c in turn.late(4):
                        dve.wait_ge(*k.e_ln.rooted.at(c.n + 1))
                        dve.wait_ge(*k.e_stored[c.place].at(c.uses + 1))
                        dve.scalar_tensor_tensor(out[:, c.place, :, :], t[c.place].centred, 0.0,
                                                 spread(t[c.place].inv, Q, F), ALU.max, ALU.mult).then_inc(k.e_out.sem, 1)
                    for c in turn.late(3):
                        dve.wait_ge(*k.e_ln.squared.at(c.n + 1))
                        order.settle(dve.tensor_reduce(t[c.place].var, t[c.place].squares, AX, ALU.add))
                        dve.tensor_scalar(var[:, c.place, :], t[c.place].var, 1.0 / F, EPS, ALU.mult, ALU.add
                                          ).then_inc(k.e_ln.varied.sem, 1)
                    order.leave_turn(turn, 4)

            @block.sync
            def _(sp):
                def fetch(c, place):
                    sp.dma_start(gap[:, place, :, :].rearrange("p n f -> p (n f)"), edge_rows(k.gap_rows, 0, c)
                                 ).then_inc(k.e_loaded[place].sem, 16)

                for place in range(RING):
                    sp.sem_inc(k.e_stored[place].sem, 16)
                    fetch(place, place)
                for turn in skewed(sp, NC, LATEST):
                    for c in turn.late(0):
                        if c.ahead:
                            sp.wait_ge(*k.weighted.at(c.n + 1))
                            fetch(c.n + RING, c.place)
                    for c in turn.late(4):
                        sp.wait_ge(*k.e_out.at(c.n + 1))
                        sp.dma_start(edge_rows(k.t2, k.NP, c.n), out[:, c.place, :, :].rearrange("p q f -> p (q f)")
                                     ).then_inc(k.e_stored[c.place].sem, 16)
                wait_ring(sp, k.e_stored, NC, 1)
    for signal in (k.weighted, k.summed, k.rows_ready, k.raised, k.projected, k.e_out):
        signal.close(NC)
    for signal in k.ring_free:
        signal.close(1)
    k.prepared.close(1)
    close_sums(k)
    ln_close(k.e_ln, NC)
    close_ring(k.e_loaded, NC)
    close_ring(k.e_stored, NC, 1)


def dve_average(dve, k, c, place, i, ring, rows):
    dve.wait_ge(*k.gathered[place].at(i + 1))
    dve.tensor_tensor(rows[:].rearrange("p (q f) -> p q f", f=F), ring[:, place, :, :],
                      spread(flat(k.inv_deg[:, bass.ds(c, 1), :]), Q, F), ALU.mult).then_inc(k.rows_ready.sem, 1)


def act_next_index(act, k, index, index_ring, c, place, i, ahead):
    act.wait_ge(*k.gathered[place].at(i + 1))
    if ahead:
        act_index(act, k, index, index_ring, c + RING, place).then_inc(k.index_set.sem, 1)


def layer2_first(k):
    nc, d, NC = k.nc, k.d, k.NC
    with ExitStack() as ctx:
        sb = allocator(k, ctx, "l2a")
        ring = sb("ring", [P, RING, Q, F])
        index_ring = sb("index_ring", [P, RING, Q], U32)
        rows = sb("rows", [P, SPAN])
        h2 = sb("h2", [P, RING, SPAN])
        kept = sb("kept", [P, SPAN])
        hidden = sb("hidden", [P, 2, SPAN])
        xnew = sb("xnew", [P, Q, F])
        out = sb("out", [P, RING, Q, F])
        s = SumTiles(sb)
        n_h2 = sb("n_h2", [P, RING, 4 * P])
        n_x = sb("n_x", [P, RING, NODE_COLS, F])
        n_kept = sb("n_kept", [P, 4 * P])
        n_hidden = sb("n_hidden", [P, 2, 4 * P])
        n_out = sb("n_out", [P, RING, NODE_COLS, F])
        columns, carry = k.bank[0][:, 0:SPAN], k.bank[0][:, SPAN:SPAN + 1]
        turned, e_hidden, e_rows = k.bank[1][:, 0:SPAN], k.bank[2], k.bank[3]
        n_columns, n_hid, n_rows = k.bank[4], (k.bank[5], k.bank[6]), (k.bank[7], k.bank[4])

        with nc.Block() as block:
            @block.gpsimd
            def _(pool):
                for c, place, i in chunks(pool, NC):
                    pool.wait_ge(*k.index_set.at(c + 1))
                    pool.wait_ge(*k.ring_free[place].at(i + 1))
                    gather(pool, k, k.t2, ring, index_ring, place)

            @block.scalar
            def _(act):
                start_ring(act, k, k.table_index, index_ring)
                for place in range(RING):
                    act.sem_inc(k.ring_free[place].sem, 1)
                for c, place, i, ahead in chunks_ahead(act, NC):
                    act.wait_ge(*k.n_columns.at(c + 1))
                    act.activation(n_kept[:], n_columns[:], ACT.Copy).then_inc(k.n_columns_kept.sem, 1)
                    act_next_index(act, k, k.table_index, index_ring, c, place, i, ahead)
                    act.wait_ge(*k.rows_ready.at(c + 1))
                    act.sem_inc(k.ring_free[place].sem, 1)
                    act.wait_ge(*k.e_columns.at(c + 1))
                    act.activation(kept[:], turned, ACT.Copy).then_inc(k.e_columns_kept.sem, 1)
                    act.wait_ge(*k.n_hidden.at(c + 1))
                    for j in range(2):
                        last = act.activation(n_hidden[:, j, :], n_hid[j][:], ACT.Relu, bias=k.b1_col[:])
                    last.then_inc(k.n_hidden_kept.sem, 1)
                    act.wait_ge(*k.e_hidden.at(c + 1))
                    act.activation(hidden[:].rearrange("p j n -> p (j n)"), e_hidden[:], ACT.Relu, bias=k.b1_col[:]
                                   ).then_inc(k.e_hidden_kept.sem, 1)
                    act.wait_ge(*k.n_out.at(c + 1))
                    act.wait_ge(*k.n_stored[place].at(2 * (i + 1)))
                    for part in range(2):
                        last = act.activation(n_out[:, place, 8 * part:8 * part + 8, :],
                                              n_rows[part][:].rearrange("p (n f) -> p n f", f=2 * F)[:, :, 0:F], ACT.Copy)
                    last.then_inc(k.n_out2.sem, 1)
                    act.wait_ge(*k.e_state.at(c + 1))
                    act.wait_ge(*k.e_stored[place].at(i + 1))
                    act.activation(out[:, place, :, :], e_rows[:].rearrange("p (n f) -> p n f", f=2 * F)[:, :, 0:F], ACT.Copy
                                   ).then_inc(k.e_out.sem, 1)

            @block.tensor
            def _(pe):
                for c, place, i in chunks(pe, NC):
                    pe.wait_ge(*k.n_loaded[place].at(2 * (i + 1)))
                    for part in range(4):
                        last = pe.transpose(n_columns[:, part * P:(part + 1) * P], n_h2[:, place, part * P:(part + 1) * P],
                                            k.ident[:])
                    last.then_inc(k.n_columns.sem, 1)
                    pe.wait_ge(*k.e_loaded[place].at(i + 1))
                    pe_turn(pe, k, h2[:, place, :], turned).then_inc(k.e_columns.sem, 1)
                    pe.wait_ge(*k.n_columns_kept.at(c + 1))
                    for j in range(2):
                        last = pe.matmul(n_hid[j][:], k.w1r[:, j * P:(j + 1) * P], n_kept[:], start=True, stop=True)
                    last.then_inc(k.n_hidden.sem, 1)
                    pe.wait_ge(*k.rows_ready.at(c + 1))
                    pe_turn(pe, k, rows, columns).then_inc(k.columns_ready.sem, 1)
                    pe_carry(pe, k, s, c, s.sums[:, SPAN - 1:SPAN], carry)
                    pe.wait_ge(*k.n_hidden_kept.at(c + 1))
                    for part in range(4):
                        for j in range(2):
                            last = pe.matmul(n_rows[part // 2][:, (part % 2 * 2 + j) * P:(part % 2 * 2 + j + 1) * P],
                                             n_hidden[:, j, part * P:(part + 1) * P], k.w2lr[:], start=True, stop=True)
                    last.then_inc(k.n_projected.sem, 1)
                    pe.wait_ge(*k.e_columns_kept.at(c + 1))
                    pe.wait_ge(*k.scanned.at(c + 1))
                    for j in range(2):
                        pe.matmul(e_hidden[:, j * SPAN:(j + 1) * SPAN], k.w1l[:, j * P:(j + 1) * P], s.sums[:],
                                  start=True, stop=False)
                        last = pe.matmul(e_hidden[:, j * SPAN:(j + 1) * SPAN], k.w1r[:, j * P:(j + 1) * P], kept[:],
                                         start=False, stop=True)
                    last.then_inc(k.e_hidden.sem, 1)
                    pe.wait_ge(*k.e_hidden_kept.at(c + 1))
                    for h in range(HALVES):
                        for j in range(2):
                            last = pe.matmul(e_rows[:, (2 * h + j) * P:(2 * h + j + 1) * P], hidden[:, j, h * P:(h + 1) * P],
                                             k.w2lr[:], start=True, stop=True)
                    last.then_inc(k.e_projected.sem, 1)
                    pe.wait_ge(*k.n_out2.at(c + 1))

            @block.vector
            def _(dve):
                order = k.dve
                order.enter(dve)
                order.settle(dve.memset(s.sums[:], 0.0))
                order.close()
                for c, place, i in chunks(dve, NC):
                    order.enter(dve, c, 2)
                    dve_average(dve, k, c, place, i, ring, rows)
                    dve_scan_alone(dve, k, s, c, columns)
                    dve_scan(dve, k, c, columns, carry, s.sums[:])
                    dve.wait_ge(*k.n_projected.at(c + 1))
                    for part in range(2):
                        at = n_x[:, place, 8 * part:8 * part + 8, :]
                        last = dve.tensor_tensor(at, at, n_rows[part][:].rearrange("p (n f) -> p n f", f=2 * F)[:, :, F:2 * F],
                                                 ALU.add)
                    order.settle(last)
                    dve.tensor_tensor(n_x[:, place, :, :], n_x[:, place, :, :],
                                      k.b2[:].unsqueeze(1).to_broadcast([P, NODE_COLS, F]), ALU.add).then_inc(k.n_out.sem, 1)
                    dve.wait_ge(*k.e_projected.at(c + 1))
                    order.settle(dve.tensor_tensor(xnew[:], e_rows[:].rearrange("p (n f) -> p n f", f=2 * F)[:, :, F:2 * F],
                                                   k.b2[:].unsqueeze(1).to_broadcast([P, Q, F]), ALU.add))
                    state = flat(k.state[:, bass.ds(c, 1), :])
                    dve.tensor_tensor(state, state, xnew[:].rearrange("p q f -> p (q f)"), ALU.add
                                      ).then_inc(k.e_state.sem, 1)
                    order.leave()
                order.close(NC)

            @block.sync
            def _(sp):
                def fetch(c, place):
                    sp.dma_start(n_x[:, place, :, :].rearrange("p n f -> p (n f)"), node_rows(k.xa, c, k.NP)
                                 ).then_inc(k.n_loaded[place].sem, 16)
                    sp.dma_start(n_h2[:, place, :], node_rows(k.t2, c, k.NP)).then_inc(k.n_loaded[place].sem, 16)
                    sp.dma_start(h2[:, place, :], edge_rows(k.t2, k.NP, c)).then_inc(k.e_loaded[place].sem, 16)

                for place in range(RING):
                    sp.sem_inc(k.n_stored[place].sem, 32)
                    sp.sem_inc(k.e_stored[place].sem, 16)
                    fetch(place, place)
                for c, place, i, ahead in chunks_ahead(sp, NC):
                    sp.wait_ge(*k.n_out.at(c + 1))
                    sp.dma_start(node_rows(k.xb, c, k.NP), n_x[:, place, :, :].rearrange("p n f -> p (n f)")
                                 ).then_inc(k.n_stored[place].sem, 16)
                    sp.wait_ge(*k.n_out2.at(c + 1))
                    sp.dma_start(node_rows(k.t2b, c, k.NP), n_out[:, place, :, :].rearrange("p n f -> p (n f)")
                                 ).then_inc(k.n_stored[place].sem, 16)
                    sp.wait_ge(*k.e_out.at(c + 1))
                    sp.dma_start(edge_rows(k.t2b, k.NP, c), out[:, place, :, :].rearrange("p q f -> p (q f)")
                                 ).then_inc(k.e_stored[place].sem, 16)
                    if ahead:
                        sp.wait_ge(*k.n_stored[place].at(2 * (i + 2)))
                        fetch(c + RING, place)
                wait_twice(sp, k.n_stored, NC, 1)
                wait_ring(sp, k.e_stored, NC, 1)
    close_ring(k.gathered, NC)
    close_ring(k.ring_free, NC, 1)
    for signal in (k.index_set, k.rows_ready, k.n_columns, k.n_columns_kept, k.e_columns, k.e_columns_kept, k.n_hidden,
                   k.n_hidden_kept, k.e_hidden, k.e_hidden_kept, k.n_out, k.n_out2, k.e_state, k.e_out, k.n_projected,
                   k.e_projected):
        signal.close(NC)
    close_sums(k)
    for _ in range(2):
        close_ring(k.n_loaded, NC)
        close_ring(k.n_stored, NC, 1)
    close_ring(k.e_loaded, NC)
    close_ring(k.e_stored, NC, 1)


def layer2_second(k):
    nc, d, NC = k.nc, k.d, k.NC
    with ExitStack() as ctx:
        sb = allocator(k, ctx, "l2b")
        ring = sb("ring", [P, RING, Q, F])
        index_ring = sb("index_ring", [P, RING, Q], U32)
        rows = sb("rows", [P, SPAN])
        x3 = sb("x3", [P, RING, Q, F])
        h3 = sb("h3", [P, RING, Q, F])
        kept = sb("kept", [P, RING, SPAN])
        out = sb("out", [P, RING, SPAN])
        s = SumRing(sb)
        te = norm_ring(sb, "lne", Q)
        n_x = sb("n_x", [P, RING, NODE_COLS * F])
        n_h3 = sb("n_h3", [P, NODE_COLS, F])
        n_kept = sb("n_kept", [P, RING, 4 * P])
        n_out = sb("n_out", [P, RING, NODE_COLS * F])
        n_final = sb("n_final", [P, RING, NODE_COLS * F])
        tn = NormTiles(sb, "lnn", NODE_COLS)
        columns, carry, projected = k.bank[0][:, 0:SPAN], k.bank[0][:, SPAN:SPAN + 1], k.bank[1][:, 0:SPAN]
        turned, e_rows, n_columns, n_rows = k.bank[2][:, 0:SPAN], k.bank[3][:, 0:SPAN], k.bank[4], k.bank[5]
        LATEST = 3

        with nc.Block() as block:
            @block.gpsimd
            def _(pool):
                for c, place, i in chunks(pool, NC):
                    pool.wait_ge(*k.index_set.at(c + 1))
                    pool.wait_ge(*k.ring_free[place].at(i + 1))
                    gather(pool, k, k.t2b, ring, index_ring, place)

            @block.scalar
            def _(act):
                start_ring(act, k, k.table_index, index_ring)
                for place in range(RING):
                    act.sem_inc(k.ring_free[place].sem, 1)
                for turn in skewed(act, NC, LATEST):
                    for c in turn.late(0):
                        ln_square(act, k, k.n_ln, c.n, tn)
                    for c in turn.late(2):
                        ln_root(act, k, k.e_ln, c.n, te[c.place])
                    for c in turn.late(1):
                        act.wait_ge(*k.n_projected.at(c.n + 1))
                        act.wait_ge(*k.n_stored[c.place].at(2 * (c.uses + 1)))
                        act.activation(n_out[:, c.place, :], n_rows[:], ACT.Copy).then_inc(k.n_out.sem, 1)
                    for c in turn.late(0):
                        act_next_index(act, k, k.table_index, index_ring, c.n, c.place, c.uses, c.ahead)
                        act.wait_ge(*k.rows_ready.at(c.n + 1))
                        act.sem_inc(k.ring_free[c.place].sem, 1)
                        ln_root(act, k, k.n_ln, c.n, tn)
                    for c in turn.late(3):
                        act.wait_ge(*k.e_projected.at(c.n + 1))
                        act.wait_ge(*k.e_stored[c.place].at(c.uses + 1))
                        act.activation(out[:, c.place, :], e_rows, ACT.Copy).then_inc(k.e_out.sem, 1)
                    for c in turn.late(2):
                        act.wait_ge(*k.e_columns.at(c.n + 1))
                        act.activation(kept[:, c.place, :], turned, ACT.Copy).then_inc(k.e_columns_kept.sem, 1)
                    for c in turn.late(1):
                        ln_square(act, k, k.e_ln, c.n, te[c.place])
                        act.activation(flat(k.state[:, bass.ds(c.n, 1), :]),
                                       x3[:, c.place, :, :].rearrange("p q f -> p (q f)"), ACT.Copy)
                    for c in turn.late(0):
                        act.wait_ge(*k.n_columns.at(c.n + 1))
                        act.activation(n_kept[:, c.place, :], n_columns[:], ACT.Copy).then_inc(k.n_columns_kept.sem, 1)

            @block.tensor
            def _(pe):
                for turn in skewed(pe, NC, LATEST):
                    for c in turn.late(1):
                        pe.wait_ge(*k.n_columns_kept.at(c.n + 1))
                        if not c.first:
                            pe.wait_ge(*k.n_out.at(c.n))
                        for part in range(4):
                            at = slice(part * P, (part + 1) * P)
                            last = pe.matmul(n_rows[:, at], n_kept[:, c.place, at], k.w3[:], start=True, stop=True)
                        last.then_inc(k.n_projected.sem, 1)
                        pe.wait_ge(*k.scanned.at(c.n + 1))
                        pe_project(pe, s.sums[:, c.place, :], k.ident, projected).then_inc(k.projected.sem, 1)
                    for c in turn.late(0):
                        pe.wait_ge(*k.rows_ready.at(c.n + 1))
                        pe_turn(pe, k, rows, columns).then_inc(k.columns_ready.sem, 1)
                    for c in turn.late(3):
                        pe.wait_ge(*k.e_columns_kept.at(c.n + 1))
                        if not c.first:
                            pe.wait_ge(*k.e_out.at(c.n))
                        pe_project(pe, kept[:, c.place, :], k.w3, e_rows).then_inc(k.e_projected.sem, 1)
                    for c in turn.late(2):
                        pe.wait_ge(*k.e_en.at(c.n + 1))
                        pe_turn(pe, k, h3[:, c.place, :, :].rearrange("p q f -> p (q f)"), turned
                                ).then_inc(k.e_columns.sem, 1)
                    for c in turn.late(0):
                        pe_carry(pe, k, s, c.n, s.last(c.place), carry)
                        pe.wait_ge(*k.n_rows.at(c.n + 1))
                        for part in range(4):
                            last = pe.transpose(n_columns[:, part * P:(part + 1) * P],
                                                n_h3[:].rearrange("p n f -> p (n f)")[:, part * P:(part + 1) * P], k.ident[:])
                        last.then_inc(k.n_columns.sem, 1)

            @block.vector
            def _(dve):
                order = k.dve
                order.enter(dve)
                order.settle(dve.memset(s.sums[:], 0.0))
                order.close()
                for turn in skewed(dve, NC, LATEST):
                    order.enter_turn(dve, turn, 7)
                    for c in turn.late(0):
                        dve.wait_ge(*k.n_loaded[c.place].at(c.uses + 1))
                        ln_centre(dve, k, k.n_ln, n_x[:, c.place, :].rearrange("p (n f) -> p n f", f=F), NODE_COLS, tn)
                    for c in turn.late(2):
                        dve.wait_ge(*k.e_ln.rooted.at(c.n + 1))
                        order.settle(dve.reciprocal(te[c.place].inv, te[c.place].dev))
                        order.settle(dve.tensor_tensor(te[c.place].inv, te[c.place].inv,
                                                       flat(k.inv_sqrt_deg[:, bass.ds(c.n, 1), :]), ALU.mult))
                        dve.scalar_tensor_tensor(h3[:, c.place, :, :], te[c.place].centred, 0.0,
                                                 spread(te[c.place].inv, Q, F), ALU.max, ALU.mult).then_inc(k.e_en.sem, 1)
                    for c in turn.late(0):
                        dve_average(dve, k, c.n, c.place, c.uses, ring, rows)
                        ln_variance(dve, k, k.n_ln, c.n, tn)
                    for c in turn.late(1):
                        dve.wait_ge(*k.n_out.at(c.n + 1))
                        dve.wait_ge(*k.n_stored[c.place].at(2 * (c.uses + 1)))
                        final = n_final[:, c.place, :]
                        order.settle(dve.tensor_tensor(final.rearrange("p (n f) -> p n f", f=F),
                                                       n_out[:, c.place, :].rearrange("p (n f) -> p n f", f=F),
                                                       k.b3[:].unsqueeze(1).to_broadcast([P, NODE_COLS, F]), ALU.add))
                        dve.scalar_tensor_tensor(final, final, 0.0, n_x[:, c.place, :], ALU.max, ALU.add
                                                 ).then_inc(k.n_out2.sem, 1)
                    for c in turn.late(0):
                        dve_scan_alone(dve, k, s, c.n, columns)
                    for c in turn.late(1):
                        dve.wait_ge(*k.projected.at(c.n + 1))
                        order.settle(dve.tensor_tensor(x3[:, c.place, :, :].rearrange("p q f -> p (q f)"),
                                                       flat(k.state[:, bass.ds(c.n, 1), :]), projected, ALU.add))
                        ln_centre(dve, k, k.e_ln, x3[:, c.place, :, :], Q, te[c.place])
                    for c in turn.late(0):
                        ln_scale(dve, k, k.n_ln, c.n, NODE_COLS, tn, n_h3[:]).then_inc(k.n_rows.sem, 1)
                        dve_scan(dve, k, c.n, columns, carry, s.sums[:, c.place, :])
                    for c in turn.late(1):
                        ln_variance(dve, k, k.e_ln, c.n, te[c.place])
                    order.leave_turn(turn, 7)

            @block.sync
            def _(sp):
                def fetch(c, place):
                    sp.dma_start(n_x[:, place, :], node_rows(k.xb, c, k.NP)).then_inc(k.n_loaded[place].sem, 16)

                for place in range(RING):
                    sp.sem_inc(k.n_stored[place].sem, 32)
                    sp.sem_inc(k.e_stored[place].sem, 16)
                    fetch(place, place)
                for turn in skewed(sp, NC, LATEST):
                    for c in turn.late(1):
                        sp.wait_ge(*k.n_out.at(c.n + 1))
                        sp.dma_start(node_rows(k.t3, c.n, k.NP), n_out[:, c.place, :]).then_inc(k.n_stored[c.place].sem, 16)
                        sp.wait_ge(*k.n_out2.at(c.n + 1))
                        sp.dma_start(node_rows(d["out"], c.n, k.NP), n_final[:, c.place, :]
                                     ).then_inc(k.n_stored[c.place].sem, 16)
                        if c.ahead:
                            fetch(c.n + RING, c.place)
                    for c in turn.late(3):
                        sp.wait_ge(*k.e_out.at(c.n + 1))
                        sp.dma_start(edge_rows(k.t3, k.NP, c.n), out[:, c.place, :]).then_inc(k.e_stored[c.place].sem, 16)
                wait_twice(sp, k.n_stored, NC, 1)
                wait_ring(sp, k.e_stored, NC, 1)
    close_ring(k.gathered, NC)
    close_ring(k.ring_free, NC, 1)
    for signal in (k.index_set, k.rows_ready, k.n_columns, k.n_columns_kept, k.e_columns, k.e_columns_kept, k.n_rows,
                   k.n_out, k.n_out2, k.e_en, k.e_out, k.n_projected, k.e_projected, k.projected):
        signal.close(NC)
    close_sums(k)
    ln_close(k.n_ln, NC)
    ln_close(k.e_ln, NC)
    for _ in range(2):
        close_ring(k.n_stored, NC, 1)
    close_ring(k.n_loaded, NC)
    close_ring(k.e_stored, NC, 1)


def layer3(k):
    nc, d, NC = k.nc, k.d, k.NC
    with ExitStack() as ctx:
        sb = allocator(k, ctx, "l3")
        ring = sb("ring", [P, RING, Q, F])
        index_ring = sb("index_ring", [P, RING, Q], U32)
        store_ring = sb("store_ring", [P, RING, Q], U32)
        own = sb("own", [P, RING, SPAN])
        t = sb("t", [P, Q, F])
        out = sb("out", [P, RING, Q, F])
        s = SumTiles(sb)
        columns, carry, projected = k.bank[0][:, 0:SPAN], k.bank[0][:, SPAN:SPAN + 1], k.bank[1][:, 0:SPAN]

        with nc.Block() as block:
            @block.gpsimd
            def _(pool):
                def gathers(c, place, i):
                    pool.wait_ge(*k.index_set.at(c + 1))
                    pool.wait_ge(*k.ring_free[place].at(i + 1))
                    gather(pool, k, k.t3, ring, index_ring, place)

                def scatters(c, place):
                    pool.wait_ge(*k.e_out.at(c + 1))
                    pool.sem_inc(k.gather_started.sem, 1)
                    for q in range(Q):
                        pool.indirect_dma_start(
                            out=d["out"], out_offset=bass.IndirectOffsetOnAxis(ap=store_ring[:, place, q:q + 1], axis=0),
                            in_=out[:, place, q, :], in_offset=None, bounds_check=k.NP - 1, oob_is_err=False
                        ).then_inc(k.scattered[place].sem, 16)

                gathers(0, 0, 0)
                turns = (NC - 1) // RING
                assert turns * RING == NC - 1
                with pool.Fori(0, turns) as i:
                    for n in range(RING):
                        c = i * RING + n + 1
                        gathers(c, (n + 1) % RING, i + (n + 1) // RING)
                        scatters(c - 1, n)
                scatters(NC - 1, 0)
                wait_ring(pool, k.scattered, NC)

            @block.scalar
            def _(act):
                start_ring(act, k, k.table_index, index_ring)
                for place in range(RING):
                    act.sem_inc(k.ring_free[place].sem, 1)

                def turn(c, place, i, ahead, first=False):
                    act_next_index(act, k, k.table_index, index_ring, c, place, i, ahead)
                    act.wait_ge(*k.columns_ready.at(c + 1))
                    act.sem_inc(k.ring_free[place].sem, 1)
                    if not first:
                        act.wait_ge(*k.scattered[place].at(i))
                    act.activation(store_ring[:, place, :], flat(k.store_rows[:, bass.ds(c, 1), :]), ACT.Copy
                                   ).then_inc(k.e_state.sem, 1)

                for c in range(RING):
                    turn(c, c, 0, True, first=True)
                for c, place, i in chunks(act, NC - RING, RING):
                    turn(c, place, i + 1, True)
                for c in range(NC - RING, NC):
                    turn(c, c % RING, c // RING, False)

            @block.tensor
            def _(pe):
                for c, place, i in chunks(pe, NC):
                    pe.wait_ge(*k.gathered[place].at(i + 1))
                    pe_turn(pe, k, ring[:, place, :, :].rearrange("p q f -> p (q f)"), columns
                            ).then_inc(k.columns_ready.sem, 1)
                    pe_carry(pe, k, s, c, s.sums[:, SPAN - 1:SPAN], carry)
                    pe.wait_ge(*k.e_loaded[place].at(i + 1))
                    pe.wait_ge(*k.scanned.at(c + 1))
                    for h in range(HALVES):
                        at = slice(h * P, (h + 1) * P)
                        pe.matmul(projected[:, at], s.sums[:, at], k.ident[:], start=True, stop=False)
                        last = pe.matmul(projected[:, at], k.ident[:], own[:, place, at], start=False, stop=True)
                    last.then_inc(k.projected.sem, 1)

            @block.vector
            def _(dve):
                order = k.dve
                order.enter(dve)
                order.settle(dve.memset(s.sums[:], 0.0))
                order.close()
                for c, place, i in chunks(dve, NC):
                    order.enter(dve, c, 2)
                    dve_scan_alone(dve, k, s, c, columns)
                    dve_scan(dve, k, c, columns, carry, s.sums[:])
                    dve.wait_ge(*k.projected.at(c + 1))
                    order.settle(dve.tensor_tensor(t[:], projected.rearrange("p (q f) -> p q f", f=F),
                                                   spread(flat(k.inv_sqrt_deg[:, bass.ds(c, 1), :]), Q, F), ALU.mult))
                    order.settle(dve.tensor_tensor(t[:], t[:], k.b3[:].unsqueeze(1).to_broadcast([P, Q, F]), ALU.add))
                    dve.wait_ge(*k.e_state.at(c + 1))
                    dve.scalar_tensor_tensor(out[:, place, :, :].rearrange("p q f -> p (q f)"),
                                             t[:].rearrange("p q f -> p (q f)"), 0.0, flat(k.state[:, bass.ds(c, 1), :]),
                                             ALU.max, ALU.add).then_inc(k.e_out.sem, 1)
                    order.leave()
                order.close(NC)

            @block.sync
            def _(sp):
                def fetch(c, place):
                    sp.dma_start(own[:, place, :], edge_rows(k.t3, k.NP, c)).then_inc(k.e_loaded[place].sem, 16)

                for place in range(RING):
                    fetch(place, place)
                for c, place, i, ahead in chunks_ahead(sp, NC):
                    if ahead:
                        sp.wait_ge(*k.projected.at(c + 1))
                        fetch(c + RING, place)



def layout(inputs):
    x = np.asarray(inputs["x"])
    src, dst = np.asarray(inputs["src"]), np.asarray(inputs["dst"])
    gaps = np.asarray(inputs["edge_attr3_2x32"])
    nodes, edges = x.shape[0], src.shape[0]
    NC = max(-(-edges // CHUNK), -(-(nodes + 1) // (NODE_COLS * P)), 3)
    NP, EP, JN = NC * NODE_COLS * P, NC * CHUNK, NC * NODE_COLS
    a = {}
    a["x"] = np.concatenate([x, np.zeros((NP - nodes, F), x.dtype)])
    a["dst_line"] = np.concatenate([np.full(1, -1, dst.dtype), dst, np.full(EP - edges, nodes, dst.dtype),
                                    np.full(1, -2, dst.dtype)])
    a["src_line"] = np.concatenate([src, np.zeros(EP - edges, src.dtype)])
    gaps = np.concatenate([gaps.reshape(edges, 2 * F), np.zeros((EP - edges, 2 * F), gaps.dtype)])
    a["edge_attr"] = np.ascontiguousarray(
        gaps.reshape(NC, GROUPS, HALVES, P, 2 * F).transpose(0, 3, 2, 1, 4).reshape(EP, 2 * F))
    for name in ("L0_gnn_W", "L1_gnn_W1", "L1_gnn_b1", "L1_gnn_W2s", "L1_gnn_b2s", "L1_gnn_W2d", "L1_gnn_b2d",
                 "L1_gnn_attn", "L2_gnn_W1_l", "L2_gnn_b1", "L2_gnn_W1_r", "L2_gnn_W2_l", "L2_gnn_b2",
                 "L2_gnn_W2_r", "L3_gnn_bias"):
        a[name] = np.ascontiguousarray(np.asarray(inputs[name]))
    a["L3_gnn_W_turned"] = np.ascontiguousarray(np.asarray(inputs["L3_gnn_W"]).T)
    f, g = np.arange(P) % F, np.arange(P) // F
    same_f = f[:, None] == f[None, :]
    a["identity"] = np.eye(P, dtype=np.float32)
    a["carry_patterns"] = np.stack([same_f & (g[:, None] < g[None, :]), same_f & (g[:, None] == GROUPS - 1),
                                    same_f & (g[:, None] > g[None, :]), same_f & (g[:, None] == 0)],
                                   axis=1).astype(np.float32)
    a["below"] = (np.arange(P)[:, None] < np.arange(P)[None, :]).astype(np.float32)
    a["above"] = (np.arange(P)[:, None] > np.arange(P)[None, :]).astype(np.float32)
    pick = np.zeros((P, GROUPS, P), np.float32)
    for group in range(GROUPS):
        pick[F * group, group, :] = 1.0
    a["pick_group"] = pick
    assert JN <= 2048
    a["count_up"] = np.arange(max(JN, P), dtype=np.float16)
    a["edge_number"] = np.arange(EP, dtype=np.float32)
    a["edge_number_rows"] = np.ascontiguousarray(
        a["edge_number"].reshape(NC, GROUPS, HALVES, P).transpose(3, 0, 2, 1).reshape(P, NC * Q))
    a["node_number"] = np.arange(NP, dtype=np.float32).reshape(P, JN)
    return a, NC, nodes


def kernel(**inputs):
    import concourse.bacc as _bacc
    from concourse.bass_utils import run_bass_kernel_spmd as _run

    arrays, NC, nodes = layout(inputs)
    nc = _bacc.Bacc("TRN2", target_bir_lowering=False, num_devices=1)
    d = {name: nc.dram_tensor(name, a.shape, mybir.dt.from_np(a.dtype), kind="ExternalInput").ap()
         for name, a in arrays.items()}
    d["out"] = nc.dram_tensor("out", (NC * NODE_COLS * P, F), F32, kind="ExternalOutput").ap()
    build(nc, d, NC)
    result = _run(nc, [arrays], core_ids=[0])
    return result.results[0]["out"][:nodes]
```

```python
import numpy as np
from contextlib import ExitStack

import concourse.bass as bass
from concourse import mybir

F32 = mybir.dt.float32
BF16 = mybir.dt.bfloat16
F16 = mybir.dt.float16
I32 = mybir.dt.int32
U32 = mybir.dt.uint32
ALU = mybir.AluOpType
ACT = mybir.ActivationFunctionType
AX = mybir.AxisListType.X

P = 128
F = 32
GROUPS = 4
HALVES = 2
Q = GROUPS * HALVES
SPAN = HALVES * P
CHUNK = GROUPS * SPAN
LINE = 512
NODE_COLS = 16
RING = 2
SLOTS = 4
FAR = 1.0e30
EPS = 1e-5
SLOPE = 0.2


class Kernel:
    pass


class NormSignals:

    def __init__(self, signal, name):
        self.centred, self.squared = signal(name + "_centred"), signal(name + "_squared")
        self.varied, self.rooted = signal(name + "_varied"), signal(name + "_rooted")


class NormTiles:
    def __init__(self, sb, name, n, squares=None):
        self.total, self.centred = sb(name + "_total", [P, n])[:], sb(name + "_centred", [P, n, F])[:]
        self.squares = sb(name + "_squares", [P, n, F])[:] if squares is None else squares
        self.var, self.dev, self.inv = sb(name + "_var", [P, n])[:], sb(name + "_dev", [P, n])[:], sb(name + "_inv", [P, n])[:]


def norm_ring(sb, name, n):
    first = NormTiles(sb, name + "0", n)
    return [first] + [NormTiles(sb, f"{name}{place}", n, first.squares) for place in range(1, RING)]


class SumTiles:
    def __init__(self, sb):
        self.carry, self.alone, self.sums = sb("carry", [P, 2, P]), sb("alone", [P, SPAN]), sb("sums", [P, SPAN])


class SumRing:
    def __init__(self, sb):
        self.carry, self.alone, self.sums = sb("carry", [P, 2, P]), sb("alone", [P, SPAN]), sb("sums", [P, RING, SPAN])

    def last(self, place):
        return self.sums[:, 1 - place, SPAN - 1:SPAN]


class SortSemaphores:
    def __init__(self, sem):
        self.loaded, self.flags, self.counted = sem("sort_loaded"), sem("sort_flags"), sem("sort_counted")
        self.known, self.piece, self.piece_used = sem("sort_known"), sem("sort_piece"), sem("sort_piece_used")
        self.rows, self.set, self.free = sem("sort_rows"), sem("sort_set"), sem("sort_free")
        self.stored, self.ends = sem("sort_stored"), sem("sort_ends")


class Signal:

    def __init__(self, sem, unit=1):
        self.sem, self.unit, self.before = sem, unit, 0

    def at(self, n):
        return self.sem, self.before + n * self.unit

    def close(self, n):
        self.before += n * self.unit


class Order:

    def __init__(self, sem):
        self.sem, self.before, self.base, self.k = sem, 0, 0, 0

    def enter(self, eng, turn=0, per_turn=None):
        self.eng, self.k, self.per_turn = eng, 0, per_turn
        self.base = self.before + turn * (per_turn or 0)

    def settle(self, instruction):
        instruction.then_inc(self.sem, 1)
        self.k += 1
        self.eng.wait_ge(self.sem, self.base + self.k)

    def note(self, instruction):
        instruction.then_inc(self.sem, 1)
        self.k += 1

    def leave(self):
        assert self.per_turn is None or self.k == self.per_turn, f"a turn has {self.k} steps"

    def close(self, turns=1):
        self.before += self.k * turns

    def enter_turn(self, eng, turn, per_turn):
        self.eng, self.k = eng, 0
        self.base = self.before if turn.i is None else self.before + (turn.i * turn.unroll + turn.n) * per_turn

    def leave_turn(self, turn, per_turn):
        if turn.i is None:
            self.before += self.k
        else:
            assert self.k == per_turn, f"a turn has {self.k} steps"
            if turn.n == turn.unroll - 1:
                self.before += turn.turns * turn.unroll * per_turn


def chunks(eng, n, start=0, ring=RING):
    turns = (n - start) // ring
    if turns:
        with eng.Fori(0, turns) as i:
            for place in range(ring):
                yield i * ring + place + start, place, i
    for rest in range(turns * ring, n - start):
        yield rest + start, rest % ring, turns


def chunks_ahead(eng, n):
    for c, place, i in chunks(eng, n - RING):
        yield c, place, i, True
    for c in range(n - RING, n):
        yield c, c % RING, c // RING, False


class Chunk:

    def __init__(self, at, base=0, again=True, ahead=True, gather_ahead=True):
        self.n = base + at
        self.place, self.uses = at % RING, at // RING
        self.slot, self.slot_uses = at % SLOTS, at // SLOTS
        self.first, self.again, self.ahead, self.gather_ahead = False, again, ahead, gather_ahead
        self.slot_again = True

    @staticmethod
    def alone(at, NC):
        c = Chunk(at, 0, at >= RING, at + RING < NC, at + SLOTS < NC)
        c.first, c.slot_again = at == 0, at >= SLOTS
        return c

    @staticmethod
    def looped(at, i, unroll):
        c = Chunk(at)
        c.n = i * unroll + at
        c.uses = (i * (unroll // RING) if unroll > RING else i) + at // RING
        if unroll % SLOTS == 0:
            c.slot_uses = (i * (unroll // SLOTS) if unroll > SLOTS else i) + at // SLOTS
        else:
            c.slot = c.slot_uses = None
        return c


class Turn:

    def __init__(self, NC, at, i=None, turns=0, n=0, unroll=RING):
        self.NC, self.at, self.i, self.turns, self.n, self.unroll = NC, at, i, turns, n, unroll

    def late(self, by=0):
        at = self.at - by
        if self.i is None:
            return [Chunk.alone(at, self.NC)] if 0 <= at < self.NC else []
        return [Chunk.looped(at, self.i, self.unroll)]


def skewed(eng, NC, depth, unroll=RING, tail=SLOTS):
    head = min(depth + SLOTS if unroll >= SLOTS else depth + RING, NC - RING)
    turns = max(0, NC - tail - head) // unroll
    for t in range(head):
        yield Turn(NC, t)
    if turns:
        with eng.Fori(0, turns) as i:
            for n in range(unroll):
                yield Turn(NC, head + n, i, turns, n, unroll)
    for t in range(head + turns * unroll, NC + depth):
        yield Turn(NC, t)


def close_ring(signals, n, more=0):
    for place, s in enumerate(signals):
        s.close(len(range(place, n, len(signals))) + more)


def wait_ring(eng, signals, n, more=0):
    for place, s in enumerate(signals):
        eng.wait_ge(*s.at(len(range(place, n, len(signals))) + more))


def spread(ap, n, width):
    return ap.unsqueeze(2).to_broadcast([ap.shape[0], n, width])


def build(nc, d, NC):
    k = Kernel()
    k.nc, k.d, k.NC = nc, d, NC
    k.NP, k.EP, k.JN, k.SP = NC * NODE_COLS * P, NC * CHUNK, NC * NODE_COLS, NC * CHUNK // LINE
    with ExitStack() as ctx:
        def sb(name, shape, dt=F32):
            return ctx.enter_context(nc.sbuf_tensor(name, shape, dt))

        k.bank = [ctx.enter_context(nc.psum_tensor(f"bank{n}", [P, 512], F32)) for n in range(8)]

        k.ident = sb("ident", [P, P])
        k.ones_row = sb("ones_row", [1, P])
        k.carry_base = sb("carry_base", [P, 4, P])
        k.eps = sb("eps", [P, 1])
        k.w0 = sb("w0", [P, P])
        k.w1 = sb("w1", [P, P])
        k.w2s = sb("w2s", [P, 256])
        k.w2d = sb("w2d", [P, 256])
        k.w1l = sb("w1l", [P, 256])
        k.w1r = sb("w1r", [P, 256])
        k.w2lr = sb("w2lr", [P, P])
        k.w3 = sb("w3", [P, P])
        k.attn = sb("attn", [P, 4])
        k.attn_parts = sb("attn_parts", [P, 2, 4])
        k.bz = sb("bz", [P, 1])
        k.columns = sb("columns", [P, 3])
        k.b1_col = k.columns[:, 0:1]
        k.b1_row = sb("b1_row", [1, P])
        k.b2s_row = sb("b2s_row", [1, 2 * P])
        k.b3_row = sb("b3_row", [1, P])
        k.b2 = sb("b2", [P, F])
        k.b3 = sb("b3", [P, F])
        k.unsorted = sb("unsorted", [1, 1], I32)
        k.dst_rows = sb("dst_rows", [P, NC, Q])
        k.dst_index = sb("dst_index", [P, NC * Q], U32)
        k.src_index = sb("src_index", [P, NC * Q], U32)
        k.table_index = sb("table_index", [P, NC * Q], U32)
        k.store_rows = sb("store_rows", [P, NC, Q])
        k.inv_deg = sb("inv_deg", [P, NC, Q])
        k.inv_sqrt_deg = sb("inv_sqrt_deg", [P, NC, Q])
        k.same = sb("same", [P, NC, SPAN + 1], BF16)
        k.first_col = sb("first_col", [P, NC + 1])
        k.last_col = sb("last_col", [P, NC + 1])
        k.first_all = sb("first_all", [P, NC, GROUPS])
        k.last_all = sb("last_all", [P, NC, GROUPS])
        k.line_same = sb("line_same", [k.SP, LINE + 1])
        k.line_far = sb("line_far", [k.SP, LINE + 1])
        k.line_fwd = sb("line_fwd", [k.SP, k.SP])
        k.line_bwd = sb("line_bwd", [k.SP, k.SP])
        k.line_far_fwd = sb("line_far_fwd", [k.SP, k.SP])
        k.line_far_bwd = sb("line_far_bwd", [k.SP, k.SP])
        k.line_ones = sb("line_ones", [k.SP, k.SP])
        k.carry_col = sb("carry_col", [k.SP, 1])
        k.line_a = sb("line_a", [k.SP, LINE])
        k.line_f = sb("line_f", [k.SP, LINE])
        k.line_b = sb("line_b", [k.SP, LINE])
        k.line_diag = sb("line_diag", [k.SP, k.SP])
        k.logits = sb("logits", [P, 8, NC * 2])
        k.alpha = sb("alpha", [P, NC, 2 * Q])

        def sem(name):
            return ctx.enter_context(nc.semaphore(name))

        k.dve, k.act, k.pool = Order(sem("dve_done")), Order(sem("act_done")), Order(sem("pool_done"))

        def signal(name, unit=1):
            return Signal(sem(name), unit)

        k.loaded = signal("loaded", 16)
        k.prepared = signal("prepared")
        k.dst_set = signal("dst_set")
        k.line_carried = signal("line_carried")
        k.line_scanned = signal("line_scanned")
        k.turned = signal("turned")
        k.turned_used = signal("turned_used")
        k.gathered = [signal(f"gathered{n}", 16 * Q) for n in range(SLOTS)]
        k.index_set = signal("index_set")
        k.gather_started = signal("gather_started")
        k.ring_free = [signal(f"ring_free{n}") for n in range(SLOTS)]
        k.rows_ready = signal("rows_ready")
        k.columns_ready = signal("columns_ready")
        k.scanned_alone = signal("scanned_alone")
        k.carried = signal("carried")
        k.scanned = signal("scanned")
        k.projected = signal("projected")
        k.e_ln, k.n_ln = NormSignals(signal, "e"), NormSignals(signal, "n")
        k.e_out = signal("e_out")
        k.e_stored = [signal(f"e_stored{n}", 16) for n in range(RING)]
        k.e_loaded = [signal(f"e_loaded{n}", 16) for n in range(RING)]
        k.n_loaded = [signal(f"n_loaded{n}", 16) for n in range(RING)]
        k.h_loaded = [signal(f"h_loaded{n}", 16) for n in range(RING)]
        k.x_loaded = [signal(f"x_loaded{n}", 16) for n in range(SLOTS)]
        k.x_stored = [signal(f"x_stored{n}", 16) for n in range(RING)]
        k.n_out = signal("n_out")
        k.n_out2 = signal("n_out2")
        k.n_read = signal("n_read")
        k.n_stored = [signal(f"n_stored{n}", 16) for n in range(RING)]
        k.n_rows = signal("n_rows")
        k.n_columns = signal("n_columns")
        k.n_columns_kept = signal("n_columns_kept")
        k.n_hidden = signal("n_hidden")
        k.n_hidden_kept = signal("n_hidden_kept")
        k.n_projected = signal("n_projected")
        k.e_columns = signal("e_columns")
        k.e_columns_kept = signal("e_columns_kept")
        k.e_hidden = signal("e_hidden")
        k.e_hidden_kept = signal("e_hidden_kept")
        k.e_projected = signal("e_projected")
        k.e_gap = signal("e_gap")
        k.e_en = signal("e_en")
        k.e_state = signal("e_state")
        k.e_logits = signal("e_logits")
        k.e_logits_kept = signal("e_logits_kept")
        k.weighted = signal("weighted")
        k.raised = signal("raised")
        k.summed = signal("summed")
        k.counted = signal("counted")
        k.onehot = signal("onehot")
        k.scattered = [signal(f"scattered{n}", 16 * Q) for n in range(SLOTS)]

        k.sort_dve = Order(sem("sort_dve_done"))
        k.sort = SortSemaphores(sem)
        k.dst_sorted = nc.dram_tensor("dst_sorted", (k.EP + 2,), I32).ap()
        k.src_sorted = nc.dram_tensor("src_sorted", (k.EP,), I32).ap()
        k.attr_sorted = nc.dram_tensor("attr_sorted", (k.EP, 2 * F), F32).ap()
        k.t01 = nc.dram_tensor("table01", (k.NP + k.EP, F + 1), F32).ap()
        k.t2 = nc.dram_tensor("table2", (k.NP + k.EP, F), F32).ap()
        k.t2b = nc.dram_tensor("table2b", (k.NP + k.EP, F), F32).ap()
        k.t3 = nc.dram_tensor("table3", (k.NP + k.EP, F), F32).ap()
        k.xa = nc.dram_tensor("nodes_after1", (k.NP, F), F32).ap()
        k.xb = nc.dram_tensor("nodes_after2", (k.NP, F), F32).ap()
        k.gap_rows = nc.dram_tensor("edge_gaps", (k.EP, 2 * F), F32).ap()

        load_constants(k)
        sort_edges(k)
        k.state = sb("state", [P, NC, Q * F])
        with ExitStack() as inner:
            ring = inner.enter_context(nc.sbuf_tensor("dest_ring", [P, SLOTS, Q, F], F32))
            index_ring = inner.enter_context(nc.sbuf_tensor("dest_index_ring", [P, SLOTS, Q], U32))
            prepare_edges(k, ring, index_ring)
            gather_destinations(k, ring, index_ring)
        with ExitStack() as inner:
            k.sums0 = inner.enter_context(nc.sbuf_tensor("sums0", [P, NC * SPAN], F32))
            layer0(k)
            layer1_logits(k)
        layer1_softmax(k)
        layer1_sums(k)
        layer2_first(k)
        layer2_second(k)
        layer3(k)



def allocator(k, ctx, phase):
    def sb(name, shape, dt=F32):
        return ctx.enter_context(k.nc.sbuf_tensor(f"{phase}_{name}", shape, dt))
    return sb


def edge_rows(table, base, c):
    width = table.shape[1]
    return table[bass.ds(base + c * CHUNK, CHUNK), :].rearrange("(p q) f -> p (q f)", p=P)


def node_rows(table, c, nodes):
    whole = table[0:nodes, :].rearrange("(p j) f -> p (j f)", p=P)
    width = NODE_COLS * table.shape[1]
    return whole[:, bass.ds(c * width, width)]


def gather(pool, k, table, ring, index_ring, slot):
    pool.sem_inc(k.gather_started.sem, 1)
    for q in range(Q):
        pool.indirect_dma_start(out=ring[:, slot, q, :], out_offset=None, in_=table,
                                in_offset=bass.IndirectOffsetOnAxis(ap=index_ring[:, slot, q:q + 1], axis=0)
                                ).then_inc(k.gathered[slot].sem, 16)


def ln_centre(dve, k, ln, x, n, s):
    k.dve.settle(dve.tensor_reduce(s.total, x, AX, ALU.add))
    dve.scalar_tensor_tensor(s.centred, spread(s.total, n, F), -1.0 / F, x, ALU.mult, ALU.add
                             ).then_inc(ln.centred.sem, 1)


def ln_square(act, k, ln, c, s):
    act.wait_ge(*ln.centred.at(c + 1))
    act.activation(s.squares, s.centred, ACT.Square).then_inc(ln.squared.sem, 1)


def ln_variance(dve, k, ln, c, s):
    dve.wait_ge(*ln.squared.at(c + 1))
    dve.tensor_reduce(s.var, s.squares, AX, ALU.add).then_inc(ln.varied.sem, 1)


def ln_root(act, k, ln, c, s):
    act.wait_ge(*ln.varied.at(c + 1))
    act.activation(s.dev, s.var, ACT.Sqrt, bias=k.eps[:], scale=1.0 / F).then_inc(ln.rooted.sem, 1)


def ln_scale(dve, k, ln, c, n, s, out):
    dve.wait_ge(*ln.rooted.at(c + 1))
    k.dve.settle(dve.reciprocal(s.inv, s.dev))
    return dve.scalar_tensor_tensor(out, s.centred, 0.0, spread(s.inv, n, F), ALU.max, ALU.mult)


def ln_close(ln, n):
    for s in (ln.centred, ln.squared, ln.varied, ln.rooted):
        s.close(n)


FORWARD, FORWARD_BEFORE, BACKWARD, BACKWARD_AFTER = range(4)


def pe_turn(pe, k, rows, columns):
    for h in range(HALVES):
        last = pe.transpose(columns[:, h * P:(h + 1) * P], rows[:, h * P:(h + 1) * P], k.ident[:])
    return last


def dve_scan_alone(dve, k, t, c, columns):
    dve.scalar_tensor_tensor(t.carry[:, 0, :].rearrange("p (g f) -> p g f", g=GROUPS),
                             spread(k.first_all[:, bass.ds(c, 1), :].rearrange("p o g -> p (o g)"), GROUPS, F),
                             k.last_col[:, bass.ds(c + 1, 1)],
                             k.carry_base[:, FORWARD, :].rearrange("p (g f) -> p g f", g=GROUPS),
                             ALU.is_equal, ALU.mult)
    dve.scalar_tensor_tensor(t.carry[:, 1, :].rearrange("p (g f) -> p g f", g=GROUPS),
                             spread(k.first_all[:, bass.ds(c, 1), :].rearrange("p o g -> p (o g)"), GROUPS, F),
                             k.last_col[:, bass.ds(c, 1)],
                             k.carry_base[:, FORWARD_BEFORE, :].rearrange("p (g f) -> p g f", g=GROUPS),
                             ALU.is_equal, ALU.mult)
    dve.wait_ge(*k.columns_ready.at(c + 1))
    dve.tensor_tensor_scan(t.alone[:], flat(k.same[:, bass.ds(c, 1), 0:SPAN]), columns, 0.0, ALU.mult, ALU.add
                           ).then_inc(k.scanned_alone.sem, 1)


def flat(ap):
    return ap.rearrange("p o n -> p (o n)")


def pe_carry(pe, k, t, c, before, out):
    pe.wait_ge(*k.scanned_alone.at(c + 1))
    pe.matmul(out, t.carry[:, 0, :], t.alone[:, SPAN - 1:SPAN], start=True, stop=False)
    pe.matmul(out, t.carry[:, 1, :], before, start=False, stop=True).then_inc(k.carried.sem, 1)


def dve_scan(dve, k, c, columns, carry, sums):
    dve.wait_ge(*k.carried.at(c + 1))
    dve.tensor_tensor_scan(sums, flat(k.same[:, bass.ds(c, 1), 0:SPAN]), columns, carry, ALU.mult, ALU.add
                           ).then_inc(k.scanned.sem, 1)


def act_index(act, k, index, index_ring, c, slot, reverse=None):
    col = c * Q if reverse is None else (reverse - c) * Q
    return act.activation(index_ring[:, slot, :], index[:, bass.ds(col, Q)], ACT.Copy)


def start_ring(act, k, index, index_ring, reverse=None):
    for slot in range(SLOTS):
        act_index(act, k, index, index_ring, slot, slot, reverse).then_inc(k.index_set.sem, 1)
        act.sem_inc(k.ring_free[slot].sem, 1)



def load_constants(k):
    nc, d = k.nc, k.d
    loads = [(k.ident[:], d["identity"]), (k.carry_base[:], d["carry_patterns"]),
             (k.w0[:], d["L0_gnn_W"]), (k.w1[:], d["L1_gnn_W1"]), (k.w2s[:], d["L1_gnn_W2s"]), (k.w2d[:], d["L1_gnn_W2d"]),
             (k.w1l[:], d["L2_gnn_W1_l"]), (k.w1r[:], d["L2_gnn_W1_r"]), (k.w2lr[:], d["L2_gnn_W2_lr"]),
             (k.w3[:], d["L3_gnn_W_turned"]), (k.attn[:], d["L1_gnn_attn"]), (k.columns[:], d["bias_columns"]),
             (k.b1_row[:], d["L1_gnn_b1_row"]), (k.b2s_row[:], d["L1_gnn_b2s_row"]),
             (k.b3_row[:], d["L3_gnn_bias_row"]),
             (k.b3[:], d["L3_gnn_bias"].partition_broadcast(P)), (k.b2[:], d["L2_gnn_b2"].partition_broadcast(P))]
    with nc.Block() as block:
        @block.vector
        def _(dve):
            dve.memset(k.ones_row[:], 1.0)
            dve.memset(k.eps[:], EPS)
            dve.memset(k.line_ones[:], 1.0)
            dve.wait_ge(*k.loaded.at(len(loads)))
            dve.tensor_scalar(k.attn_parts[:, 0, :], k.attn[:], SLOPE, None, ALU.mult)
            dve.tensor_scalar(k.attn_parts[:, 1, :], k.attn[:], 1.0 - SLOPE, None, ALU.mult)
            dve.tensor_tensor(k.bz[:], k.columns[:, 1:2], k.columns[:, 2:3], ALU.add).then_inc(k.prepared.sem, 1)
            dve.wait_ge(*k.prepared.at(1))

        @block.sync
        def _(sp):
            for out, data in loads:
                sp.dma_start(out, data).then_inc(k.loaded.sem, 16)
            sp.wait_ge(*k.loaded.at(len(loads)))
    k.loaded.close(len(loads))
    k.prepared.close(1)


def sort_edges(k):
    nc, d, NC, SP, EP = k.nc, k.d, k.NC, k.SP, k.EP
    pieces = next(n for n in range(1, NC + 1) if NC % n == 0 and EP // n <= 8 * CHUNK)
    width = EP // pieces
    s, order = k.sort, k.sort_dve
    with ExitStack() as ctx:
        sb = allocator(k, ctx, "sort")
        line = sb("line", [SP, LINE + 2], I32)
        falls = sb("falls", [SP, LINE])
        fall_count = sb("fall_count", [SP, 1])
        dst_all = sb("dst_all", [P, width], I32)
        number_all = sb("number_all", [P, width])
        ahead = sb("ahead", [P, width])
        dst_own = sb("dst_own", [P, NC, Q], I32)
        src_own = sb("src_own", [P, NC, Q], I32)
        dst_f = sb("dst_f", [P, NC * Q])
        number_own = sb("number_own", [P, NC * Q])
        found = sb("found", [P, 1])
        rank = sb("rank", [P, NC * Q])
        row = sb("row", [P, 4, NC * Q], I32)
        targets = sb("targets", [P, 3, Q], U32)
        own = sb("own", [P, 2, Q], I32)
        attr = sb("attr", [P, Q, 2 * F])
        count = k.bank[0][0:1, 0:1]

        with nc.Block() as block:
            @block.sync
            def _(sp):
                sp.dma_start(line[:], bass.AP(tensor=d["dst_line"].tensor, offset=0, ap=[[LINE, SP], [1, LINE + 2]])
                             ).then_inc(s.loaded, 16)
                sp.wait_ge(s.known, 1)
                falling = sp.value_load(k.unsorted[0:1, 0:1])
                with sp.If(falling == 0):
                    sp.dma_start(k.dst_sorted, d["dst_line"]).then_inc(s.ends, 16)
                    sp.dma_start(k.src_sorted, d["src_line"]).then_inc(s.ends, 16)
                    sp.wait_ge(s.ends, 32)
                with sp.Else():
                    for b in range(HALVES):
                        for c in range(NC):
                            at = c * CHUNK + b * P
                            with nc.allow_non_contiguous_dma("the edges of a lane lie apart"):
                                sp.dma_start(dst_own[:, c, b * GROUPS:(b + 1) * GROUPS],
                                             bass.AP(tensor=d["dst_line"].tensor, offset=1 + at, ap=[[1, P], [SPAN, GROUPS]])
                                             ).then_inc(s.rows, 16)
                                sp.dma_start(src_own[:, c, b * GROUPS:(b + 1) * GROUPS],
                                             bass.AP(tensor=d["src_line"].tensor, offset=at, ap=[[1, P], [SPAN, GROUPS]])
                                             ).then_inc(s.rows, 16)
                    sp.dma_start(number_own[:], d["edge_number_rows"]).then_inc(s.rows, 16)
                    for n in range(pieces):
                        if n:
                            sp.wait_ge(s.piece_used, n)
                        at = slice(n * width, (n + 1) * width)
                        sp.dma_start(dst_all[:], d["dst_line"][1 + n * width:1 + (n + 1) * width].partition_broadcast(P)
                                     ).then_inc(s.piece, 16)
                        sp.dma_start(number_all[:], d["edge_number"][at].partition_broadcast(P)).then_inc(s.piece, 16)
                    for at in (0, EP + 1):
                        sp.dma_start(k.dst_sorted[at:at + 1], d["dst_line"][at:at + 1]).then_inc(s.ends, 16)
                    with sp.Fori(0, NC) as c:
                        sp.wait_ge(s.free, c + 1)
                        sp.dma_start(attr[:].rearrange("p q f -> p (q f)"), edge_rows(d["edge_attr"], 0, c)).then_inc(s.loaded, 16)
                    sp.wait_ge(s.ends, 32)
                    sp.wait_ge(s.free, NC + 1)

            @block.tensor
            def _(pe):
                pe.wait_ge(s.flags, 1)
                pe.matmul(count, fall_count[:], k.line_ones[:, 0:1], start=True, stop=True).then_inc(s.counted, 1)

            @block.vector
            def _(dve):
                order.enter(dve)
                dve.wait_ge(s.loaded, 16)
                order.settle(dve.tensor_tensor(falls[:], line[:, 0:LINE], line[:, 1:LINE + 1], ALU.is_gt))
                dve.tensor_reduce(fall_count[:], falls[:], AX, ALU.add).then_inc(s.flags, 1)
                dve.wait_ge(s.counted, 1)
                dve.tensor_copy(k.unsorted[:], count).then_inc(s.known, 1)
                dve.wait_ge(s.known, 1)
                falling = dve.value_load(k.unsorted[0:1, 0:1])
                with dve.If(falling == 0):
                    dve.sem_inc(s.flags, 1)
                with dve.Else():
                    dve.wait_ge(s.rows, 16 * (4 * NC + 1))
                    order.settle(dve.tensor_copy(dst_f[:], dst_own[:].rearrange("p c q -> p (c q)")))
                    order.settle(dve.memset(rank[:], 0.0))
                    order.close()
                    for n in range(pieces):
                        dve.wait_ge(s.piece, 32 * (n + 1))
                        with dve.Fori(0, NC * Q) as t:
                            order.enter(dve, t, 5)
                            order.settle(dve.tensor_scalar(ahead[:], number_all[:], number_own[:, bass.ds(t, 1)], None, ALU.is_lt))
                            order.settle(dve.scalar_tensor_tensor(ahead[:], dst_all[:], dst_f[:, bass.ds(t, 1)], ahead[:],
                                                                  ALU.is_equal, ALU.mult))
                            order.settle(dve.scalar_tensor_tensor(ahead[:], dst_all[:], dst_f[:, bass.ds(t, 1)], ahead[:],
                                                                  ALU.is_lt, ALU.add))
                            order.settle(dve.tensor_reduce(found[:], ahead[:], AX, ALU.add))
                            order.note(dve.tensor_tensor(rank[:, bass.ds(t, 1)], rank[:, bass.ds(t, 1)], found[:], ALU.add))
                            order.leave()
                        order.close(NC * Q)
                        order.enter(dve)
                        dve.wait_ge(order.sem, order.base)
                        dve.sem_inc(s.piece_used, 1)
                    order.enter(dve)
                    order.settle(dve.tensor_copy(row[:, 0, :], rank[:]))
                    row_of_edge(dve, order, row)
                    order.close()
                    with dve.Fori(0, NC) as c:
                        order.enter(dve, c, 4)
                        dve.wait_ge(s.free, c + 1)
                        order.note(dve.tensor_scalar(targets[:, 0, :], rank[:, bass.ds(c * Q, Q)], 1.0, None, ALU.add))
                        order.note(dve.tensor_copy(targets[:, 1, :], rank[:, bass.ds(c * Q, Q)]))
                        order.note(dve.tensor_copy(targets[:, 2, :], row[:, 0, bass.ds(c * Q, Q)]))
                        order.note(dve.tensor_copy(own[:, 0, :], flat(dst_own[:, bass.ds(c, 1), :])))
                        dve.tensor_copy(own[:, 1, :], flat(src_own[:, bass.ds(c, 1), :])).then_inc(s.set, 1)
                        order.leave()
                    order.close(NC)

            @block.gpsimd
            def _(pool):
                pool.wait_ge(s.known, 1)
                falling = pool.value_load(k.unsorted[0:1, 0:1])
                with pool.If(falling == 0):
                    pool.sem_inc(s.flags, 1)
                with pool.Else():
                    pool.sem_inc(s.free, 1)
                    with pool.Fori(0, NC) as c:
                        pool.wait_ge(s.set, c + 1)
                        pool.wait_ge(s.loaded, 16 * (c + 2))
                        pool.sem_inc(s.flags, 1)
                        for q in range(Q):
                            for n, (out, data) in enumerate(((k.dst_sorted, own[:, 0, q:q + 1]), (k.src_sorted, own[:, 1, q:q + 1]),
                                                             (k.attr_sorted, attr[:, q, :]))):
                                pool.indirect_dma_start(
                                    out=out.unsqueeze(1) if n < 2 else out,
                                    out_offset=bass.IndirectOffsetOnAxis(ap=targets[:, n, q:q + 1], axis=0),
                                    in_=data, in_offset=None).then_inc(s.stored, 16)
                        pool.wait_ge(s.stored, (c + 1) * (16 * 3 * Q))
                        pool.sem_inc(s.free, 1)


def line_carry(k):
    return k.bank[0][0:k.SP, 0:1], k.bank[0][0:k.SP, 0:k.SP]


def dve_line_total(dve, k, values, op, out, turn):
    same, op0, start = (k.line_same, ALU.mult, 0.0) if op == ALU.add else (k.line_far, ALU.add, -FAR)
    carry, everyone = line_carry(k)
    for way in range(2):
        if way == 0:
            flags, data, result = same[:, 0:LINE], values, k.line_f[:]
            alone, tail, far = k.line_a[:], k.line_a[:, LINE - 1:LINE], k.line_far_fwd
        else:
            flags, data, result = same[:, 1:LINE + 1][:, ::-1], values[:, ::-1], k.line_b[:, ::-1]
            alone, tail, far = k.line_a[:, ::-1], k.line_a[:, 0:1], k.line_far_bwd
        if op == ALU.add:
            dve.tensor_tensor_scan(alone, flags, data, start, op0, op).then_inc(k.line_scanned.sem, 1)
            dve.wait_ge(*k.line_carried.at(turn + way + 1))
            k.dve.settle(dve.tensor_tensor_scan(result, flags, data, carry, op0, op))
        else:
            k.dve.settle(dve.tensor_tensor_scan(alone, flags, data, start, op0, op))
            dve.tensor_scalar(k.line_diag[:], k.ident[0:k.SP, 0:k.SP], tail, None, ALU.mult
                              ).then_inc(k.line_scanned.sem, 1)
            dve.wait_ge(*k.line_carried.at(turn + way + 1))
            k.dve.settle(dve.tensor_tensor(k.line_diag[:], everyone, far[:], ALU.add))
            k.dve.settle(dve.tensor_reduce(k.carry_col[:], k.line_diag[:], AX, ALU.max))
            k.dve.settle(dve.tensor_tensor_scan(result, flags, data, k.carry_col[:], op0, op))
    if op == ALU.add:
        k.dve.settle(dve.tensor_tensor(out, k.line_f[:], k.line_b[:], ALU.add))
        k.dve.settle(dve.tensor_tensor(out, out, values, ALU.subtract))
    else:
        k.dve.settle(dve.tensor_tensor(out, k.line_f[:], k.line_b[:], ALU.max))


def pe_line_total(pe, k, op, turn):
    carry, everyone = line_carry(k)
    for way in range(2):
        pe.wait_ge(*k.line_scanned.at(turn + way + 1))
        if op == ALU.add:
            reach, tail = ((k.line_fwd, k.line_a[:, LINE - 1:LINE]), (k.line_bwd, k.line_a[:, 0:1]))[way]
            pe.matmul(carry, reach[:], tail, start=True, stop=True).then_inc(k.line_carried.sem, 1)
        else:
            pe.matmul(everyone, k.line_ones[:], k.line_diag[:], start=True, stop=True).then_inc(k.line_carried.sem, 1)


def prepare_edges(k, ring, index_ring):
    nc, d, NC, SP = k.nc, k.d, k.NC, k.SP
    dst, src = k.dst_sorted, k.src_sorted
    with ExitStack() as ctx:
        sb = allocator(k, ctx, "prep")
        dst_int = sb("dst_int", [SP, LINE + 2], I32)
        src_int = sb("src_int", [SP, LINE], I32)
        dstf = sb("dstf", [SP, LINE + 2])
        srcf = sb("srcf", [SP, LINE])
        tmp = sb("tmp", [SP, LINE])
        ones = sb("ones", [SP, LINE])
        deg = sb("deg", [SP, LINE])
        inv = sb("inv", [SP, LINE])
        isd = sb("isd", [SP, LINE])
        store = sb("store", [SP, LINE])
        lt = sb("lt", [P, P])
        gt = sb("gt", [P, P])
        dcols = sb("dcols", [P, NC, SPAN + 2], I32)
        pick = sb("pick", [P, GROUPS, P])

        with nc.Block() as block:
            @block.sync
            def _(sp):
                sp.dma_start(dst_int[:], bass.AP(tensor=dst.tensor, offset=0, ap=[[LINE, SP], [1, LINE + 2]])
                             ).then_inc(k.loaded.sem, 16)
                sp.dma_start(src_int[:], src.rearrange("(p n) -> p n", n=LINE)).then_inc(k.loaded.sem, 16)
                sp.dma_start(lt[:], d["below"]).then_inc(k.loaded.sem, 16)
                sp.dma_start(gt[:], d["above"]).then_inc(k.loaded.sem, 16)
                sp.dma_start(pick[:], d["pick_group"]).then_inc(k.loaded.sem, 16)
                sp.wait_ge(*k.loaded.at(5))
                for g in range(GROUPS):
                    sp.dma_start(dcols[F * g:F * g + F, :, :],
                                 bass.AP(tensor=dst.tensor, offset=g * SPAN,
                                         ap=[[0, F], [CHUNK, NC], [1, SPAN + 2]])).then_inc(k.loaded.sem, 16)
                sp.wait_ge(*k.loaded.at(9))

            @block.vector
            def _(dve):
                order = k.dve
                order.enter(dve)
                dve.wait_ge(*k.loaded.at(5))
                dve.memset(ones[:], 1.0)
                dve.tensor_copy(srcf[:], src_int[:])
                dve.tensor_copy(dstf[:], dst_int[:]).then_inc(k.prepared.sem, 1)
                dve.wait_ge(*k.prepared.at(1))
                order.settle(dve.tensor_tensor(k.line_same[:], dstf[:, 1:LINE + 2], dstf[:, 0:LINE + 1], ALU.is_equal))
                order.settle(dve.tensor_scalar(k.line_far[:], k.line_same[:], 1.0, FAR, ALU.subtract, ALU.mult))
                order.settle(dve.tensor_scalar(k.line_diag[:], k.ident[0:SP, 0:SP], dstf[:, 1:2], None, ALU.mult))
                order.settle(dve.tensor_scalar(tmp[:, 0:SP], k.ident[0:SP, 0:SP], dstf[:, LINE:LINE + 1], None, ALU.mult))
                dve.sem_inc(k.line_scanned.sem, 2)
                dve.wait_ge(*k.line_carried.at(2))
                first, last = k.bank[1][0:SP, 0:SP], k.bank[2][0:SP, 0:SP]
                dve.scalar_tensor_tensor(k.line_fwd[:], first, dstf[:, LINE:LINE + 1], lt[0:SP, 0:SP], ALU.is_equal, ALU.mult)
                dve.scalar_tensor_tensor(k.line_bwd[:], last, dstf[:, 1:2], gt[0:SP, 0:SP], ALU.is_equal, ALU.mult)
                dve.scalar_tensor_tensor(k.line_far_fwd[:], last, dstf[:, 1:2], gt[0:SP, 0:SP], ALU.is_equal, ALU.mult)
                order.settle(dve.scalar_tensor_tensor(k.line_far_bwd[:], first, dstf[:, LINE:LINE + 1], lt[0:SP, 0:SP], ALU.is_equal, ALU.mult))
                dve.tensor_scalar(k.line_far_fwd[:], k.line_far_fwd[:], 1.0, FAR, ALU.subtract, ALU.mult)
                order.settle(dve.tensor_scalar(k.line_far_bwd[:], k.line_far_bwd[:], 1.0, FAR, ALU.subtract, ALU.mult))
                dve_line_total(dve, k, ones[:], ALU.add, deg[:], 2)
                order.settle(dve.tensor_scalar(tmp[:], deg[:], 1.0, None, ALU.max))
                order.settle(dve.reciprocal(inv[:], tmp[:]))
                order.settle(dve.tensor_scalar(tmp[:], deg[:], 1.0, 1.0, ALU.add, ALU.max))
                dve.sem_inc(k.prepared.sem, 1)
                dve.wait_ge(*k.prepared.at(3))
                order.settle(dve.reciprocal(isd[:], tmp[:]))
                order.settle(dve.tensor_scalar(store[:], dstf[:, 1:LINE + 1], float(2 * k.NP), None, ALU.subtract))
                order.settle(dve.scalar_tensor_tensor(store[:], k.line_same[:, 1:LINE + 1], 0.0, store[:], ALU.is_equal, ALU.mult))
                order.settle(dve.tensor_scalar(store[:], store[:], float(2 * k.NP), None, ALU.add))
                dve.sem_inc(k.prepared.sem, 1)
                dve.wait_ge(*k.loaded.at(9))
                order.settle(dve.tensor_tensor(k.same[:], dcols[:, :, 1:SPAN + 2], dcols[:, :, 0:SPAN + 1], ALU.is_equal))
                dve.memset(k.first_col[:, NC:NC + 1], -2.0)
                dve.memset(k.last_col[:, 0:1], -1.0)
                dve.tensor_copy(k.first_col[:, 0:NC], dcols[:, :, 1])
                order.settle(dve.tensor_copy(k.last_col[:, 1:NC + 1], dcols[:, :, SPAN]))
                dve.sem_inc(k.prepared.sem, 1)
                for g in range(GROUPS):
                    for way, out in enumerate((k.first_all, k.last_all)):
                        n = 2 * g + way
                        dve.wait_ge(*k.counted.at(n + 1))
                        order.settle(dve.tensor_copy(out[:, :, g], k.bank[6 + n % 2][:, 0:NC]))
                        dve.sem_inc(k.onehot.sem, 1)

            @block.tensor
            def _(pe):
                def turn_line(line, n):
                    for part in range(4):
                        if n >= 2:
                            pe.wait_ge(*k.turned_used.at(n - 1))
                        pe.transpose(k.bank[3 + n % 2][:, 0:SP], line[:, part * P:(part + 1) * P],
                                     k.ident[0:SP, 0:SP]).then_inc(k.turned.sem, 1)
                        n += 1

                pe.wait_ge(*k.prepared.at(1))
                turn_line(dstf[:, 1:LINE + 1], 0)
                pe.wait_ge(*k.line_scanned.at(2))
                pe.matmul(k.bank[1][0:SP, 0:SP], k.line_ones[:], k.line_diag[:], start=True, stop=True
                          ).then_inc(k.line_carried.sem, 1)
                pe.matmul(k.bank[2][0:SP, 0:SP], k.line_ones[:], tmp[:, 0:SP], start=True, stop=True
                          ).then_inc(k.line_carried.sem, 1)
                pe_line_total(pe, k, ALU.add, 2)
                pe.wait_ge(*k.prepared.at(4))
                for n, line in enumerate((srcf[:], inv[:], isd[:], store[:])):
                    turn_line(line, 4 * (n + 1))
                pe.wait_ge(*k.prepared.at(5))
                for g in range(GROUPS):
                    for way, col in enumerate((k.first_col[:, 0:NC], k.last_col[:, 1:NC + 1])):
                        n = 2 * g + way
                        if n >= 2:
                            pe.wait_ge(*k.onehot.at(n - 1))
                        pe.matmul(k.bank[6 + n % 2][:, 0:NC], pick[:, g, :], col, start=True, stop=True
                                  ).then_inc(k.counted.sem, 1)

            @block.scalar
            def _(act):
                def keep_rows(out, n):
                    for part in range(4):
                        gl, half = part // 2, part % 2
                        view = out[:] if len(out.shape) == 3 else out[:].rearrange("p (c q) -> p c q", q=Q)
                        view = view.rearrange("p c (b j l) -> p c b j l", b=2, j=2)[:, :, half, :, gl]
                        act.wait_ge(*k.turned.at(n + 1))
                        act.activation(view, k.bank[3 + n % 2][:, 0:SP].rearrange("p (c j) -> p c j", j=2),
                                       ACT.Copy).then_inc(k.turned_used.sem, 1)
                        n += 1

                keep_rows(k.dst_rows, 0)
                act.wait_ge(*k.turned_used.at(4))
                act.activation(k.dst_index[:], k.dst_rows[:].rearrange("p c q -> p (c q)"), ACT.Copy
                               ).then_inc(k.dst_set.sem, 1)
                act.wait_ge(*k.dst_set.at(1))
                start_ring(act, k, k.dst_index, index_ring)
                act.wait_ge(*k.prepared.at(2))
                act.activation(tmp[:], tmp[:], ACT.Sqrt).then_inc(k.prepared.sem, 1)
                for n, out in enumerate((k.src_index, k.inv_deg, k.inv_sqrt_deg, k.store_rows)):
                    keep_rows(out, 4 * (n + 1))

            @block.gpsimd
            def _(pool):
                for slot in range(SLOTS):
                    pool.wait_ge(*k.index_set.at(slot + 1))
                    gather(pool, k, d["x"], ring, index_ring, slot)
    k.loaded.close(9)
    k.prepared.close(5)
    k.line_scanned.close(4)
    k.line_carried.close(4)
    k.turned.close(20)
    k.turned_used.close(20)
    k.dst_set.close(1)
    k.counted.close(8)
    k.onehot.close(8)
    k.dve.close()


def row_of_edge(dve, order, e):
    dve.tensor_scalar(e[:, 1, :], e[:, 0, :], 127, 3, ALU.bitwise_and, ALU.logical_shift_left)
    dve.tensor_scalar(e[:, 2, :], e[:, 0, :], 128, 5, ALU.bitwise_and, ALU.logical_shift_right)
    dve.tensor_scalar(e[:, 3, :], e[:, 0, :], 768, 8, ALU.bitwise_and, ALU.logical_shift_right)
    order.settle(dve.tensor_scalar(e[:, 0, :], e[:, 0, :], 10, 10, ALU.arith_shift_right, ALU.logical_shift_left))
    for part in (1, 2, 3):
        order.settle(dve.tensor_tensor(e[:, 0, :], e[:, 0, :], e[:, part, :], ALU.bitwise_or))


def gather_destinations(k, ring, index_ring):
    nc, d, NC, JN = k.nc, k.d, k.NC, k.JN
    half = JN // 2
    with ExitStack() as ctx:
        sb = allocator(k, ctx, "dest")
        iota_lo = sb("iota_lo", [P, JN], F16)
        iota_hi = sb("iota_hi", [P, P], F16)
        before = sb("before", [P, P])
        node = sb("node", [P, JN])
        hi = sb("hi", [P, NC * Q])
        lo = sb("lo", [P, NC * Q])
        fix = sb("fix", [P, NC * Q])
        hi_int = sb("hi_int", [P, NC * Q], I32)
        hot_lo = sb("hot_lo", [P, Q, JN], BF16)
        hot_hi = sb("hot_hi", [P, Q, P], BF16)
        zeros = sb("zeros", [P, max(half, P)], BF16)
        degree = sb("degree", [P, JN])
        upto = sb("upto", [P, JN])
        ones = sb("ones_jn", [P, JN], BF16)
        carry = sb("carry", [P, 1])
        e_int = sb("e_int", [P, 4, JN], I32)
        pos = sb("pos", [P, JN], I32)
        xin = sb("xin", [P, RING, NODE_COLS, F])
        table = sb("table", [P, RING, NODE_COLS, F + 1])
        t = norm_ring(sb, "ln", NODE_COLS)
        LATEST, EARLIER = 1, 4
        kept_alone = max(NC - (NC + LATEST) // 2 + EARLIER, SLOTS)
        counts = [k.bank[0][:, 0:half], k.bank[1][:, 0:half]]
        with nc.Block() as block:
            @block.gpsimd
            def _(pool):
                for n, slot, i in chunks(pool, NC, SLOTS, ring=SLOTS):
                    pool.wait_ge(*k.index_set.at(n + 1))
                    pool.wait_ge(*k.ring_free[slot].at(i + 2))
                    gather(pool, k, d["x"], ring, index_ring, slot)

            @block.scalar
            def _(act):

                def keep(c):
                    act_next_index(act, k, k.dst_index, index_ring, c)
                    act.activation(flat(k.state[:, bass.ds(c.n, 1), :]),
                                   ring[:, c.slot, :, :].rearrange("p q f -> p (q f)"), ACT.Copy
                                   ).then_inc(k.ring_free[c.slot].sem, 1)

                turns = kept_alone // SLOTS
                with act.Fori(0, turns) as i:
                    for n in range(SLOTS):
                        keep(Chunk.looped(n, i, SLOTS))
                for at in range(turns * SLOTS, kept_alone):
                    keep(Chunk.alone(at, NC))
                for turn in skewed(act, NC, LATEST, 2 * SLOTS, 2 * (SLOTS + EARLIER)):
                    for c in turn.late(1):
                        ln_root(act, k, k.n_ln, c.n, t[c.place])
                    for c in turn.late(0):
                        ln_square(act, k, k.n_ln, c.n, t[c.place])
                    at = kept_alone + turn.at // 2
                    if turn.at % 2 and (turn.i is not None or at < NC):
                        keep(Chunk.alone(at, NC) if turn.i is None else Chunk.looped(at, turn.i, SLOTS))

            @block.vector
            def _(dve):
                order = k.dve
                order.enter(dve)
                dve.memset(zeros[:], 0.0)
                dve.memset(ones[:], 1.0)
                dst = k.dst_rows[:].rearrange("p c q -> p (c q)")
                order.settle(dve.tensor_scalar(hi[:], dst, 1.0 / JN, 0.5, ALU.mult, ALU.subtract))
                order.settle(dve.tensor_copy(hi_int[:], hi[:]))
                order.settle(dve.tensor_copy(hi[:], hi_int[:]))
                for _ in range(2):
                    order.settle(dve.scalar_tensor_tensor(lo[:], hi[:], -float(JN), dst, ALU.mult, ALU.add))
                    order.settle(dve.tensor_scalar(fix[:], lo[:], 0.0, None, ALU.is_lt))
                    order.settle(dve.tensor_tensor(hi[:], hi[:], fix[:], ALU.subtract))
                    order.settle(dve.tensor_scalar(fix[:], lo[:], float(JN), None, ALU.is_ge))
                    order.settle(dve.tensor_tensor(hi[:], hi[:], fix[:], ALU.add))
                order.settle(dve.scalar_tensor_tensor(lo[:], hi[:], -float(JN), dst, ALU.mult, ALU.add))
                dve.wait_ge(*k.loaded.at(4))
                dve.sem_inc(k.prepared.sem, 1)

                def one_hot(c, q, wait):
                    if wait:
                        dve.wait_ge(*k.counted.at((c - 1) * Q + q + 3))
                    at = bass.ds(c * Q + q, 1)
                    dve.tensor_scalar(hot_hi[:, q, :], iota_hi[:], hi[:, at], None, ALU.is_equal)
                    dve.tensor_scalar(hot_lo[:, q, :], iota_lo[:], lo[:, at], None, ALU.is_equal).then_inc(k.onehot.sem, 1)

                for q in range(Q):
                    one_hot(0, q, False)
                with dve.Fori(0, NC - 1) as c:
                    for q in range(Q):
                        one_hot(c + 1, q, True)
                dve.wait_ge(*k.counted.at(NC * Q + 3))
                for part in range(2):
                    order.settle(dve.tensor_copy(degree[:, part * half:(part + 1) * half], counts[part]))
                order.settle(dve.tensor_tensor_scan(upto[:], ones[:], degree[:], 0.0, ALU.mult, ALU.add))
                dve.sem_inc(k.onehot.sem, 1)
                dve.wait_ge(*k.counted.at(NC * Q + 4))
                order.settle(dve.tensor_scalar(carry[:], k.bank[2][:, 0:1], 1.0, None, ALU.subtract))
                order.settle(dve.tensor_scalar(upto[:], upto[:], carry[:], None, ALU.add))
                order.settle(dve.tensor_copy(e_int[:, 0, :], upto[:]))
                row_of_edge(dve, order, e_int)
                order.settle(dve.tensor_copy(upto[:], e_int[:, 0, :]))
                order.settle(dve.scalar_tensor_tensor(upto[:], upto[:], float(k.NP), node[:], ALU.add, ALU.subtract))
                order.settle(dve.scalar_tensor_tensor(upto[:], degree[:], 0.0, upto[:], ALU.is_gt, ALU.mult))
                order.settle(dve.tensor_tensor(pos[:], upto[:], node[:], ALU.add))
                order.close()
                for turn in skewed(dve, NC, LATEST):
                    order.enter_turn(dve, turn, 2)
                    for c in turn.late(0):
                        dve.wait_ge(*k.n_loaded[c.place].at(c.uses + 1))
                        ln_centre(dve, k, k.n_ln, xin[:, c.place, :, :], NODE_COLS, t[c.place])
                    for c in turn.late(1):
                        dve.wait_ge(*k.n_stored[c.place].at(c.uses + 1))
                        dve.tensor_copy(table[:, c.place, :, F].bitcast(I32), pos[:, bass.ds(c.n * NODE_COLS, NODE_COLS)])
                        ln_scale(dve, k, k.n_ln, c.n, NODE_COLS, t[c.place], table[:, c.place, :, 0:F]
                                 ).then_inc(k.n_out.sem, 1)
                    for c in turn.late(0):
                        ln_variance(dve, k, k.n_ln, c.n, t[c.place])
                    order.leave_turn(turn, 2)

            @block.tensor
            def _(pe):
                pe.wait_ge(*k.prepared.at(1))
                for part in range(2):
                    pe.matmul(counts[part], zeros[:, 0:P], zeros[:, 0:half], start=True, stop=False
                              ).then_inc(k.counted.sem, 1)
                with pe.Fori(0, NC) as c:
                    for q in range(Q):
                        pe.wait_ge(*k.onehot.at(c * Q + q + 1))
                        pe.matmul(counts[0], hot_hi[:, q, :], hot_lo[:, q, 0:half], start=False, stop=False)
                        pe.matmul(counts[1], hot_hi[:, q, :], hot_lo[:, q, half:JN], start=False, stop=False
                                  ).then_inc(k.counted.sem, 1)
                for part in range(2):
                    last = pe.matmul(counts[part], zeros[:, 0:P], zeros[:, 0:half], start=False, stop=True)
                last.then_inc(k.counted.sem, 1)
                pe.wait_ge(*k.onehot.at(NC * Q + 1))
                pe.matmul(k.bank[2][:, 0:1], before[:], upto[:, JN - 1:JN], start=True, stop=True
                          ).then_inc(k.counted.sem, 1)

            @block.sync
            def _(sp):
                sp.dma_start(iota_lo[:], d["count_up"][0:JN].partition_broadcast(P)).then_inc(k.loaded.sem, 16)
                sp.dma_start(iota_hi[:], d["count_up"][0:P].partition_broadcast(P)).then_inc(k.loaded.sem, 16)
                sp.dma_start(before[:], d["below"]).then_inc(k.loaded.sem, 16)
                sp.dma_start(node[:], d["node_number"]).then_inc(k.loaded.sem, 16)
                def fetch(c, place):
                    sp.dma_start(xin[:, place, :, :].rearrange("p n f -> p (n f)"), node_rows(d["x"], c, k.NP)
                                 ).then_inc(k.n_loaded[place].sem, 16)

                for place in range(RING):
                    sp.sem_inc(k.n_stored[place].sem, 16)
                    fetch(place, place)
                for turn in skewed(sp, NC, LATEST):
                    for c in turn.late(0):
                        if c.ahead:
                            sp.wait_ge(*k.n_ln.centred.at(c.n + 1))
                            fetch(c.n + RING, c.place)
                    for c in turn.late(1):
                        sp.wait_ge(*k.n_out.at(c.n + 1))
                        sp.dma_start(node_rows(k.t01, c.n, k.NP), table[:, c.place, :, :].rearrange("p n f -> p (n f)")
                                     ).then_inc(k.n_stored[c.place].sem, 16)
                wait_ring(sp, k.n_stored, NC, 1)
    close_ring(k.gathered, NC)
    close_ring(k.ring_free, NC, 1)
    k.index_set.close(NC)
    k.loaded.close(4)
    k.prepared.close(1)
    k.counted.close(NC * Q + 4)
    k.onehot.close(NC * Q + 1)
    ln_close(k.n_ln, NC)
    k.n_out.close(NC)
    close_ring(k.n_stored, NC, 1)
    close_ring(k.n_loaded, NC)


def layer0(k):
    nc, d, NC = k.nc, k.d, k.NC
    with ExitStack() as ctx:
        sb = allocator(k, ctx, "l0")
        ring = sb("ring", [P, SLOTS, Q, F + 1])
        index_ring = sb("index_ring", [P, SLOTS, Q], U32)
        rows = sb("rows", [P, SPAN])
        x1 = sb("x1", [P, Q, F])
        out = sb("out", [P, RING, Q, F + 1])
        s = SumRing(sb)
        te = norm_ring(sb, "lne", Q)
        n_h = sb("n_h", [P, RING, NODE_COLS, F + 1])
        n_rows = sb("n_rows", [P, NODE_COLS, F])
        n_kept = sb("n_kept", [P, RING, 4 * P])
        n_x = sb("n_x", [P, RING, NODE_COLS * F])
        n_out = sb("n_out", [P, RING, NODE_COLS, F])
        tn = norm_ring(sb, "lnn", NODE_COLS)
        columns, carry, projected = k.bank[0][:, 0:SPAN], k.bank[0][:, SPAN:SPAN + 1], k.bank[1][:, 0:SPAN]
        n_columns, n_projected = k.bank[2], k.bank[3]
        LATEST = 3

        with nc.Block() as block:
            @block.gpsimd
            def _(pool):
                for c, slot, i in chunks(pool, NC, ring=SLOTS):
                    pool.wait_ge(*k.index_set.at(c + 1))
                    pool.wait_ge(*k.ring_free[slot].at(i + 1))
                    gather(pool, k, k.t01[0:k.NP, :], ring, index_ring, slot)

            @block.scalar
            def _(act):
                start_ring(act, k, k.src_index, index_ring)
                for turn in skewed(act, NC, LATEST, SLOTS):
                    for c in turn.late(1):
                        act.wait_ge(*k.scanned.at(c.n + 1))
                        act.activation(k.sums0[:, bass.ds(c.n * SPAN, SPAN)], s.sums[:, c.place, :], ACT.Copy)
                    for c in turn.late(0):
                        act_next_index(act, k, k.src_index, index_ring, c)
                        act.activation(rows[:].rearrange("p (q f) -> p q f", f=F), ring[:, c.slot, :, 0:F], ACT.Copy
                                       ).then_inc(k.rows_ready.sem, 1)
                        act.activation(k.table_index[:, bass.ds(c.n * Q, Q)], ring[:, c.slot, :, F].bitcast(I32), ACT.Copy
                                       ).then_inc(k.ring_free[c.slot].sem, 1)
                    for c in turn.late(2):
                        ln_root(act, k, k.e_ln, c.n, te[c.place])
                    for c in turn.late(3):
                        ln_root(act, k, k.n_ln, c.n, tn[c.place])
                    for c in turn.late(0):
                        act.wait_ge(*k.h_loaded[c.place].at(c.uses + 1))
                        act.activation(n_rows[:], n_h[:, c.place, :, 0:F], ACT.Copy).then_inc(k.n_rows.sem, 1)
                    for c in turn.late(2):
                        ln_square(act, k, k.n_ln, c.n, tn[c.place])
                    for c in turn.late(1):
                        ln_square(act, k, k.e_ln, c.n, te[c.place])
                    for c in turn.late(0):
                        act.wait_ge(*k.n_columns.at(c.n + 1))
                        act.activation(n_kept[:, c.place, :], n_columns[:], ACT.Copy).then_inc(k.n_columns_kept.sem, 1)

            @block.tensor
            def _(pe):
                for turn in skewed(pe, NC, LATEST):
                    for c in turn.late(1):
                        pe.wait_ge(*k.scanned.at(c.n + 1))
                        pe_project(pe, s.sums[:, c.place, :], k.w0, projected).then_inc(k.projected.sem, 1)
                    for c in turn.late(0):
                        pe.wait_ge(*k.rows_ready.at(c.n + 1))
                        pe_turn(pe, k, rows, columns).then_inc(k.columns_ready.sem, 1)
                    for c in turn.late(1):
                        pe.wait_ge(*k.n_columns_kept.at(c.n + 1))
                        if not c.first:
                            pe.wait_ge(*k.n_ln.centred.at(c.n))
                        for part in range(4):
                            at = slice(part * P, (part + 1) * P)
                            pe.matmul(n_projected[:, at], n_kept[:, c.place, at], k.w1[:], start=True, stop=False)
                            last = pe.matmul(n_projected[:, at], k.ones_row[:], k.b1_row[:], start=False, stop=True)
                        last.then_inc(k.n_projected.sem, 1)
                    for c in turn.late(0):
                        pe_carry(pe, k, s, c.n, s.last(c.place), carry)
                        pe.wait_ge(*k.n_rows.at(c.n + 1))
                        for part in range(4):
                            last = pe.transpose(n_columns[:, part * P:(part + 1) * P],
                                                n_rows[:].rearrange("p n f -> p (n f)")[:, part * P:(part + 1) * P], k.ident[:])
                        last.then_inc(k.n_columns.sem, 1)

            @block.vector
            def _(dve):
                order = k.dve
                order.enter(dve)
                order.settle(dve.memset(s.sums[:], 0.0))
                for place in range(RING):
                    order.settle(dve.memset(out[:, place, :, F], 0.0))
                order.close()
                for turn in skewed(dve, NC, LATEST):
                    order.enter_turn(dve, turn, 6)
                    for c in turn.late(2):
                        dve.wait_ge(*k.n_loaded[c.place].at(c.uses + 1))
                        dve.wait_ge(*k.n_projected.at(c.n + 1))
                        order.settle(dve.tensor_tensor(n_x[:, c.place, :], n_x[:, c.place, :], n_projected[:], ALU.add))
                        ln_centre(dve, k, k.n_ln, n_x[:, c.place, :].rearrange("p (n f) -> p n f", f=F), NODE_COLS,
                                  tn[c.place])
                        dve.wait_ge(*k.e_stored[c.place].at(c.uses + 1))
                        ln_scale(dve, k, k.e_ln, c.n, Q, te[c.place], out[:, c.place, :, 0:F]).then_inc(k.e_out.sem, 1)
                    for c in turn.late(1):
                        dve.wait_ge(*k.projected.at(c.n + 1))
                        order.settle(dve.tensor_tensor(x1[:].rearrange("p q f -> p (q f)"),
                                                       flat(k.state[:, bass.ds(c.n, 1), :]), projected, ALU.add))
                        ln_centre(dve, k, k.e_ln, x1[:], Q, te[c.place])
                    for c in turn.late(0):
                        dve_scan_alone(dve, k, s, c.n, columns)
                    for c in turn.late(3):
                        dve.wait_ge(*k.n_stored[c.place].at(c.uses + 1))
                        ln_scale(dve, k, k.n_ln, c.n, NODE_COLS, tn[c.place], n_out[:, c.place, :, :]).then_inc(k.n_out.sem, 1)
                    for c in turn.late(0):
                        dve_scan(dve, k, c.n, columns, carry, s.sums[:, c.place, :])
                    for c in turn.late(2):
                        ln_variance(dve, k, k.n_ln, c.n, tn[c.place])
                    for c in turn.late(1):
                        ln_variance(dve, k, k.e_ln, c.n, te[c.place])
                    order.leave_turn(turn, 6)

            @block.sync
            def _(sp):
                def fetch_x(c, place):
                    sp.dma_start(n_x[:, place, :], node_rows(d["x"], c, k.NP)).then_inc(k.n_loaded[place].sem, 16)

                def fetch_h(c, place):
                    sp.dma_start(n_h[:, place, :, :].rearrange("p n f -> p (n f)"), node_rows(k.t01, c, k.NP)
                                 ).then_inc(k.h_loaded[place].sem, 16)

                for place in range(RING):
                    sp.sem_inc(k.n_stored[place].sem, 16)
                    sp.sem_inc(k.e_stored[place].sem, 16)
                    fetch_h(place, place)
                    fetch_x(place, place)
                for turn in skewed(sp, NC, LATEST):
                    for c in turn.late(0):
                        if c.ahead:
                            sp.wait_ge(*k.n_rows.at(c.n + 1))
                            fetch_h(c.n + RING, c.place)
                    for c in turn.late(2):
                        sp.wait_ge(*k.n_ln.centred.at(c.n + 1))
                        sp.dma_start(node_rows(k.xa, c.n, k.NP), n_x[:, c.place, :]).then_inc(k.x_stored[c.place].sem, 16)
                        sp.wait_ge(*k.e_out.at(c.n + 1))
                        sp.dma_start(edge_rows(k.t01, k.NP, c.n), out[:, c.place, :, :].rearrange("p q f -> p (q f)")
                                     ).then_inc(k.e_stored[c.place].sem, 16)
                    for c in turn.late(3):
                        if c.ahead:
                            sp.wait_ge(*k.x_stored[c.place].at(c.uses + 1))
                            fetch_x(c.n + RING, c.place)
                        sp.wait_ge(*k.n_out.at(c.n + 1))
                        sp.dma_start(node_rows(k.t2, c.n, k.NP), n_out[:, c.place, :, :].rearrange("p n f -> p (n f)")
                                     ).then_inc(k.n_stored[c.place].sem, 16)
                wait_ring(sp, k.x_stored, NC)
                wait_ring(sp, k.n_stored, NC, 1)
                wait_ring(sp, k.e_stored, NC, 1)
    close_ring(k.gathered, NC)
    close_ring(k.ring_free, NC, 1)
    for signal in (k.index_set, k.n_rows, k.rows_ready, k.n_columns, k.n_columns_kept, k.n_projected, k.n_out, k.e_out,
                   k.projected):
        signal.close(NC)
    close_sums(k)
    ln_close(k.n_ln, NC)
    ln_close(k.e_ln, NC)
    close_ring(k.n_loaded, NC)
    close_ring(k.h_loaded, NC)
    close_ring(k.x_stored, NC)
    close_ring(k.n_stored, NC, 1)
    close_ring(k.e_stored, NC, 1)


def wait_twice(eng, signals, n, more=0):
    for place, s in enumerate(signals):
        eng.wait_ge(*s.at(2 * (len(range(place, n, len(signals))) + more)))


def close_sums(k):
    for signal in (k.columns_ready, k.scanned_alone, k.carried, k.scanned):
        signal.close(k.NC)


def pe_project(pe, sums, weight, out):
    for h in range(HALVES):
        last = pe.matmul(out[:, h * P:(h + 1) * P], sums[:, h * P:(h + 1) * P], weight[:], start=True, stop=True)
    return last


def layer1_logits(k):
    nc, d, NC = k.nc, k.d, k.NC
    with ExitStack() as ctx:
        sb = allocator(k, ctx, "l1a")
        ring = sb("ring", [P, SLOTS, Q, F + 1])
        index_ring = sb("index_ring", [P, SLOTS, Q], U32)
        rows = sb("rows", [P, SPAN])
        goes_on = sb("goes_on", [P, SPAN], BF16)
        ends = sb("ends", [P, SPAN])
        x1 = sb("x1", [P, RING, Q, F])
        h1 = sb("h1", [P, RING, Q, F])
        kept = sb("kept", [P, RING, 2 * SPAN])
        hidden = sb("hidden", [P, RING, 2, 2 * SPAN])
        attr = sb("attr", [P, RING, 2 * Q, F])
        gap = sb("gap", [P, RING, 2 * Q, F])
        top = sb("top", [P, 2 * Q])
        s = SumRing(sb)
        t = norm_ring(sb, "ln", Q)
        carry, projected, both = k.bank[0][:, 0:1], k.bank[1][:, 0:SPAN], k.bank[2]
        en, z, own, logit = k.bank[3], k.bank[4], k.bank[5][:, 0:SPAN], k.bank[6][:, 0:2 * Q]
        REV = NC - 1
        LATEST = 4

        with nc.Block() as block:
            @block.gpsimd
            def _(pool):
                for m, slot, i in chunks(pool, NC, ring=SLOTS):
                    pool.wait_ge(*k.index_set.at(m + 1))
                    pool.wait_ge(*k.ring_free[slot].at(i + 1))
                    gather(pool, k, k.t01, ring, index_ring, slot)

            @block.scalar
            def _(act):
                start_ring(act, k, k.table_index, index_ring, REV)
                for turn in skewed(act, NC, LATEST, SLOTS):
                    for m in turn.late(2):
                        ln_root(act, k, k.e_ln, m.n, t[m.place])
                        act.wait_ge(*k.gathered[m.slot].at(m.slot_uses + 1))
                        if m.gather_ahead:
                            act_index(act, k, k.table_index, index_ring, m.n + SLOTS, m.slot, REV
                                      ).then_inc(k.index_set.sem, 1)
                        act.activation(rows[:].rearrange("p (q f) -> p q f", f=F), ring[:, m.slot, :, 0:F], ACT.Copy
                                       ).then_inc(k.rows_ready.sem, 1)
                        act.wait_ge(*k.rows_ready.at(m.n + 1))
                        act.sem_inc(k.ring_free[m.slot].sem, 1)
                    for m in turn.late(4):
                        act.wait_ge(*k.e_logits.at(m.n + 1))
                        planes = k.logits[:].rearrange("p (l b h) n -> p l b h n", l=2, b=2)
                        for b in range(HALVES):
                            last = act.activation(
                                planes[:, :, b, :, bass.ds((m.n * -1 + REV) * 2, 2)].rearrange("p l h j -> p j l h"),
                                logit[:, b * Q:(b + 1) * Q].rearrange("p (j l h) -> p j l h", j=2, l=2), ACT.Copy)
                        last.then_inc(k.e_logits_kept.sem, 1)
                    for m in turn.late(3):
                        act.wait_ge(*k.e_hidden.at(m.n + 1))
                        act.activation(hidden[:, m.place, 0, :], z[:], ACT.Identity, bias=k.bz[:, 0:1])
                        act.activation(hidden[:, m.place, 1, :], z[:], ACT.Relu, bias=k.bz[:, 0:1]
                                       ).then_inc(k.e_hidden_kept.sem, 1)
                    for m in turn.late(1):
                        act.wait_ge(*k.e_ln.centred.at(m.n + 1))
                        act.activation(flat(k.state[:, bass.ds(m.n * -1 + REV, 1), :]),
                                       x1[:, m.place, :, :].rearrange("p q f -> p (q f)"), ACT.Copy)
                        ln_square(act, k, k.e_ln, m.n, t[m.place])
                    for m in turn.late(2):
                        act.wait_ge(*k.e_columns.at(m.n + 1))
                        act.activation(kept[:, m.place, :], both[:], ACT.Copy).then_inc(k.e_columns_kept.sem, 1)

            @block.tensor
            def _(pe):
                for turn in skewed(pe, NC, LATEST):
                    for m in turn.late(4):
                        pe.wait_ge(*k.e_hidden_kept.at(m.n + 1))
                        if not m.first:
                            pe.wait_ge(*k.e_logits_kept.at(m.n))
                        for h in range(HALVES):
                            for j in range(2):
                                for part in range(2):
                                    last = pe.matmul(logit[:, h * Q + j * 4:h * Q + j * 4 + 4],
                                                     hidden[:, m.place, part, j * SPAN + h * P:j * SPAN + (h + 1) * P],
                                                     k.attn_parts[:, part, :], start=(part == 0), stop=(part == 1))
                        last.then_inc(k.e_logits.sem, 1)
                    for m in turn.late(1):
                        pe.wait_ge(*k.scanned.at(m.n + 1))
                        pe_project(pe, s.sums[:, m.place, :], k.w0, projected).then_inc(k.projected.sem, 1)
                    for m in turn.late(3):
                        pe.wait_ge(*k.e_columns_kept.at(m.n + 1))
                        for j in range(2):
                            at = slice(j * SPAN, (j + 1) * SPAN)
                            pe.matmul(z[:, at], k.w2s[:, j * P:(j + 1) * P], kept[:, m.place, SPAN:2 * SPAN],
                                      start=True, stop=False)
                            last = pe.matmul(z[:, at], k.w2d[:, j * P:(j + 1) * P], kept[:, m.place, 0:SPAN],
                                             start=False, stop=True)
                        last.then_inc(k.e_hidden.sem, 1)
                        if not m.first:
                            pe.wait_ge(*k.e_gap.at(m.n))
                        for h in range(HALVES):
                            at = slice(h * P, (h + 1) * P)
                            pe.matmul(own[:, at], kept[:, m.place, at], k.w1[:], start=True, stop=False)
                            last = pe.matmul(own[:, at], k.ones_row[:], k.b1_row[:], start=False, stop=True)
                        for h in range(HALVES):
                            at = slice(h * 2 * P, (h + 1) * 2 * P)
                            pe.matmul(en[:, at], kept[:, m.place, SPAN + h * P:SPAN + (h + 1) * P], k.w2s[:],
                                      start=True, stop=False)
                            last = pe.matmul(en[:, at], k.ones_row[:], k.b2s_row[:], start=False, stop=True)
                        last.then_inc(k.e_en.sem, 1)
                    for m in turn.late(0):
                        pe.wait_ge(*k.scanned_alone.at(m.n + 1))
                        pe.matmul(carry, s.carry[:, 0, :], s.alone[:, 0:1], start=True, stop=False)
                        pe.matmul(carry, s.carry[:, 1, :], s.sums[:, 1 - m.place, 0:1], start=False, stop=True
                                  ).then_inc(k.carried.sem, 1)
                    for m in turn.late(2):
                        pe.wait_ge(*k.rows_ready.at(m.n + 1))
                        pe_turn(pe, k, rows, both[:, SPAN:2 * SPAN])
                        pe.wait_ge(*k.e_out.at(m.n + 1))
                        pe_turn(pe, k, h1[:, m.place, :, :].rearrange("p q f -> p (q f)"), both[:, 0:SPAN]
                                ).then_inc(k.e_columns.sem, 1)

            @block.vector
            def _(dve):
                order = k.dve
                order.enter(dve)
                order.settle(dve.memset(s.sums[:], 0.0))
                order.close()
                for turn in skewed(dve, NC, LATEST):
                    order.enter_turn(dve, turn, 8)
                    for m in turn.late(2):
                        ln_scale(dve, k, k.e_ln, m.n, Q, t[m.place], h1[:, m.place, :, :]).then_inc(k.e_out.sem, 1)
                    for m in turn.late(4):
                        dve.wait_ge(*k.e_loaded[m.place].at(m.uses + 1))
                        dve.wait_ge(*k.e_stored[m.place].at(m.uses + 1))
                        dve.wait_ge(*k.e_en.at(m.n + 1))
                        state = flat(k.state[:, bass.ds(m.n * -1 + REV, 1), :])
                        order.note(dve.tensor_tensor(state, state, own, ALU.add))
                        order.settle(dve.tensor_tensor(attr[:, m.place, :, :], attr[:, m.place, :, :],
                                                       en[:].rearrange("p (n f) -> p n f", f=F), ALU.mult))
                        order.settle(dve.tensor_reduce(top[:], attr[:, m.place, :, :], AX, ALU.max))
                        dve.tensor_tensor(gap[:, m.place, :, :], attr[:, m.place, :, :], spread(top[:], 2 * Q, F), ALU.subtract
                                          ).then_inc(k.e_gap.sem, 1)
                    for m in turn.late(1):
                        dve.wait_ge(*k.projected.at(m.n + 1))
                        order.settle(dve.tensor_tensor(x1[:, m.place, :, :].rearrange("p q f -> p (q f)"),
                                                       flat(k.state[:, bass.ds(m.n * -1 + REV, 1), :]), projected, ALU.add))
                        ln_centre(dve, k, k.e_ln, x1[:, m.place, :, :], Q, t[m.place])
                    for m in turn.late(0):
                        c = m.n * -1 + REV
                        groups = spread(k.last_all[:, bass.ds(c, 1), :].rearrange("p o g -> p (o g)"), GROUPS, F)
                        for n, (pattern, col) in enumerate(((BACKWARD, c), (BACKWARD_AFTER, c + 1))):
                            dve.scalar_tensor_tensor(s.carry[:, n, :].rearrange("p (g f) -> p g f", g=GROUPS), groups,
                                                     k.first_col[:, bass.ds(col, 1)],
                                                     k.carry_base[:, pattern, :].rearrange("p (g f) -> p g f", g=GROUPS),
                                                     ALU.is_equal, ALU.mult)
                        after = flat(k.same[:, bass.ds(c, 1), 1:SPAN + 1])
                        order.note(dve.tensor_copy(goes_on[:], after))
                        order.settle(dve.scalar_tensor_tensor(ends[:], after, 0.0, k.sums0[:, bass.ds(c * SPAN, SPAN)],
                                                              ALU.is_equal, ALU.mult))
                        dve.tensor_tensor_scan(s.alone[:, ::-1], goes_on[:, ::-1], ends[:, ::-1], 0.0, ALU.mult, ALU.add
                                               ).then_inc(k.scanned_alone.sem, 1)
                    for m in turn.late(0):
                        dve.wait_ge(*k.carried.at(m.n + 1))
                        dve.tensor_tensor_scan(s.sums[:, m.place, ::-1], goes_on[:, ::-1], ends[:, ::-1], carry, ALU.mult, ALU.add
                                               ).then_inc(k.scanned.sem, 1)
                    for m in turn.late(1):
                        ln_variance(dve, k, k.e_ln, m.n, t[m.place])
                    order.leave_turn(turn, 8)

            @block.sync
            def _(sp):
                def fetch(source, m, place):
                    sp.dma_start(attr[:, place, :, :].rearrange("p n f -> p (n f)"), edge_rows(source, 0, m * -1 + REV)
                                 ).then_inc(k.e_loaded[place].sem, 16)

                def loads_and_stores(source):
                    for place in range(RING):
                        fetch(source, place, place)
                    for m, place, i, ahead in chunks_ahead(sp, NC):
                        sp.wait_ge(*k.e_gap.at(m + 1))
                        sp.dma_start(edge_rows(k.gap_rows, 0, m * -1 + REV), gap[:, place, :, :].rearrange("p n f -> p (n f)")
                                     ).then_inc(k.e_stored[place].sem, 16)
                        if ahead:
                            fetch(source, m + RING, place)

                for place in range(RING):
                    sp.sem_inc(k.e_stored[place].sem, 16)
                falling = sp.value_load(k.unsorted[0:1, 0:1])
                with sp.If(falling == 0):
                    loads_and_stores(d["edge_attr"])
                with sp.Else():
                    loads_and_stores(k.attr_sorted)
                wait_ring(sp, k.e_stored, NC, 1)
    close_ring(k.gathered, NC)
    close_ring(k.ring_free, NC, 1)
    for signal in (k.index_set, k.rows_ready, k.e_columns, k.e_columns_kept, k.e_hidden, k.e_hidden_kept, k.e_logits,
                   k.e_en, k.e_logits_kept, k.e_out, k.e_gap, k.projected, k.scanned_alone, k.carried, k.scanned):
        signal.close(NC)
    ln_close(k.e_ln, NC)
    close_ring(k.e_loaded, NC)
    close_ring(k.e_stored, NC, 1)


def layer1_softmax(k):
    nc, NC, SP = k.nc, k.NC, k.SP
    with ExitStack() as ctx:
        sb = allocator(k, ctx, "l1s")
        logit = sb("logit", [SP, 2, LINE])
        top = sb("top", [SP, LINE])
        guarded = sb("guarded", [SP, LINE])
        finite = sb("finite", [SP, LINE], I32)
        raised = sb("raised", [SP, 2, LINE])
        total = sb("total", [SP, LINE])
        alpha = sb("alpha", [SP, 2, LINE])
        with nc.Block() as block:
            @block.vector
            def _(dve):
                order = k.dve
                order.enter(dve)
                for h in range(2):
                    dve.wait_ge(*k.turned_used.at(h + 1))
                    dve_line_total(dve, k, logit[:, h, :], ALU.max, top[:], 2 * h)
                    order.settle(dve.tensor_scalar(guarded[:], top[:], 0.0, None, ALU.mult))
                    order.settle(dve.tensor_scalar(finite[:], guarded[:], 0.0, None, ALU.is_equal))
                    order.settle(dve.memset(guarded[:], 0.0))
                    order.settle(dve.copy_predicated(guarded[:], finite[:], top[:]))
                    dve.tensor_tensor(logit[:, h, :], logit[:, h, :], guarded[:], ALU.subtract).then_inc(k.weighted.sem, 1)
                for h in range(2):
                    dve.wait_ge(*k.raised.at(h + 1))
                    dve_line_total(dve, k, raised[:, h, :], ALU.add, total[:], 4 + 2 * h)
                    order.settle(dve.tensor_scalar(total[:], total[:], 1e-9, None, ALU.max))
                    order.settle(dve.reciprocal(total[:], total[:]))
                    dve.tensor_tensor(alpha[:, h, :], raised[:, h, :], total[:], ALU.mult).then_inc(k.summed.sem, 1)

            @block.scalar
            def _(act):
                for h in range(2):
                    act.wait_ge(*k.turned.at(4 * (h + 1)))
                    act.activation(logit[:, h, :], k.bank[3 + h][0:SP, :], ACT.Copy).then_inc(k.turned_used.sem, 1)
                for h in range(2):
                    act.wait_ge(*k.weighted.at(h + 1))
                    act.activation(raised[:, h, :], logit[:, h, :], ACT.Exp).then_inc(k.raised.sem, 1)
                view = k.alpha[:].rearrange("p c (b j l h) -> p c b j l h", b=2, j=2, l=2)
                for h in range(2):
                    for part in range(4):
                        gl, b, n = part // 2, part % 2, 4 * h + part
                        act.wait_ge(*k.turned.at(8 + n + 1))
                        act.activation(view[:, :, b, :, gl, h], k.bank[5 + n % 2][:, 0:SP].rearrange("p (c j) -> p c j", j=2),
                                       ACT.Copy).then_inc(k.turned_used.sem, 1)

            @block.tensor
            def _(pe):
                for h in range(2):
                    for part in range(4):
                        pe.transpose(k.bank[3 + h][0:SP, part * P:(part + 1) * P], k.logits[:, 2 * part + h, :], k.ident[:]
                                     ).then_inc(k.turned.sem, 1)
                for turn, op in enumerate((ALU.max, ALU.max, ALU.add, ALU.add)):
                    pe_line_total(pe, k, op, 2 * turn)
                for h in range(2):
                    pe.wait_ge(*k.summed.at(h + 1))
                    for part in range(4):
                        n = 4 * h + part
                        if n >= 2:
                            pe.wait_ge(*k.turned_used.at(2 + n - 1))
                        pe.transpose(k.bank[5 + n % 2][:, 0:SP], alpha[:, h, part * P:(part + 1) * P],
                                     k.ident[0:SP, 0:SP]).then_inc(k.turned.sem, 1)
    k.line_scanned.close(8)
    k.line_carried.close(8)
    k.turned.close(16)
    k.turned_used.close(10)
    for signal in (k.weighted, k.raised, k.summed):
        signal.close(2)
    k.dve.close()


def layer1_sums(k):
    nc, NC = k.nc, k.NC
    with ExitStack() as ctx:
        sb = allocator(k, ctx, "l1b")
        gap = sb("gap", [P, RING, 2 * Q, F])
        scaled = sb("scaled", [P, RING, 2 * Q, F])
        raised = sb("raised", [P, RING, 2 * Q, F])
        msg = sb("msg", [P, RING, HALVES, 2, GROUPS, F])
        total = sb("total", [P, RING, 2 * Q])
        inv = sb("inv", [P, RING, 2 * Q])
        var = sb("var", [P, RING, Q])
        power = sb("power", [P, Q])
        x2 = sb("x2", [P, RING, Q, F])
        out = sb("out", [P, RING, Q, F])
        s = SumRing(sb)
        t = norm_ring(sb, "ln", Q)
        columns = [k.bank[place][:, 0:SPAN] for place in range(RING)]
        carry = [k.bank[place][:, SPAN:SPAN + 1] for place in range(RING)]
        projected = [k.bank[RING + place][:, 0:SPAN] for place in range(RING)]
        LATEST = 5

        with nc.Block() as block:
            @block.gpsimd
            def _(pool):
                pool.memset(power[:], -0.5).then_inc(k.prepared.sem, 1)
                pool.wait_ge(*k.prepared.at(1))
                for turn in skewed(pool, NC, LATEST):
                    for c in turn.late(5):
                        pool.wait_ge(*k.e_ln.varied.at(c.n + 1))
                        pool.tensor_tensor(t[c.place].inv, var[:, c.place, :], power[:], ALU.pow
                                           ).then_inc(k.e_ln.rooted.sem, 1)
                    for c in turn.late(2):
                        pool.wait_ge(*k.summed.at(c.n + 1))
                        if c.again:
                            pool.wait_ge(*k.columns_ready.at(c.n - 1))
                        for b in range(HALVES):
                            last = pool.tensor_tensor(
                                msg[:, c.place, b, :, :, :].rearrange("p h g f -> p g h f"),
                                raised[:, c.place, b * Q:(b + 1) * Q, :].rearrange("p (g h) f -> p g h f", h=2),
                                inv[:, c.place, b * Q:(b + 1) * Q].rearrange("p (g h) -> p g h", h=2).unsqueeze(3)
                                .to_broadcast([P, GROUPS, 2, F]), ALU.mult)
                        last.then_inc(k.rows_ready.sem, 1)
                    for c in turn.late(0):
                        pool.wait_ge(*k.e_loaded[c.place].at(c.uses + 1))
                        if c.again:
                            pool.wait_ge(*k.raised.at(c.n - 1))
                        pool.tensor_tensor(scaled[:, c.place, :, :], gap[:, c.place, :, :],
                                           spread(flat(k.alpha[:, bass.ds(c.n, 1), :]), 2 * Q, F), ALU.mult
                                           ).then_inc(k.weighted.sem, 1)

            @block.scalar
            def _(act):
                for turn in skewed(act, NC, LATEST):
                    for c in turn.late(4):
                        act.wait_ge(*k.e_ln.centred.at(c.n + 1))
                        act.activation(flat(k.state[:, bass.ds(c.n, 1), :]),
                                       x2[:, c.place, :, :].rearrange("p q f -> p (q f)"), ACT.Copy)
                        ln_square(act, k, k.e_ln, c.n, t[c.place])
                    for c in turn.late(0):
                        act.wait_ge(*k.weighted.at(c.n + 1))
                        if c.again:
                            act.wait_ge(*k.rows_ready.at(c.n - 1))
                        act.activation(raised[:, c.place, :, :], scaled[:, c.place, :, :], ACT.Exp
                                       ).then_inc(k.raised.sem, 1)

            @block.tensor
            def _(pe):
                for turn in skewed(pe, NC, LATEST):
                    for c in turn.late(3):
                        pe.wait_ge(*k.rows_ready.at(c.n + 1))
                        for b in range(HALVES):
                            for h in range(2):
                                last = pe.matmul(columns[c.place][:, b * P:(b + 1) * P],
                                                 msg[:, c.place, b, h, :, :].rearrange("p g f -> p (g f)"),
                                                 k.ident[:], start=(h == 0), stop=(h == 1))
                        last.then_inc(k.columns_ready.sem, 1)
                    for c in turn.late(4):
                        pe.wait_ge(*k.scanned.at(c.n + 1))
                        pe_project(pe, s.sums[:, c.place, :], k.w1, projected[c.place]).then_inc(k.projected.sem, 1)
                    for c in turn.late(3):
                        pe_carry(pe, k, s, c.n, s.last(c.place), carry[c.place])

            @block.vector
            def _(dve):
                order = k.dve
                order.enter(dve)
                order.settle(dve.memset(s.sums[:], 0.0))
                order.close()
                for turn in skewed(dve, NC, LATEST):
                    order.enter_turn(dve, turn, 4)
                    for c in turn.late(1):
                        dve.wait_ge(*k.raised.at(c.n + 1))
                        order.settle(dve.tensor_reduce(total[:, c.place, :], raised[:, c.place, :, :], AX, ALU.add))
                        dve.reciprocal(inv[:, c.place, :], total[:, c.place, :]).then_inc(k.summed.sem, 1)
                    for c in turn.late(3):
                        dve_scan_alone(dve, k, s, c.n, columns[c.place])
                    for c in turn.late(4):
                        dve.wait_ge(*k.projected.at(c.n + 1))
                        order.settle(dve.tensor_tensor(x2[:, c.place, :, :].rearrange("p q f -> p (q f)"),
                                                       flat(k.state[:, bass.ds(c.n, 1), :]), projected[c.place], ALU.add))
                        ln_centre(dve, k, k.e_ln, x2[:, c.place, :, :], Q, t[c.place])
                    for c in turn.late(3):
                        dve_scan(dve, k, c.n, columns[c.place], carry[c.place], s.sums[:, c.place, :])
                    for c in turn.late(5):
                        dve.wait_ge(*k.e_ln.rooted.at(c.n + 1))
                        dve.wait_ge(*k.e_stored[c.place].at(c.uses + 1))
                        dve.scalar_tensor_tensor(out[:, c.place, :, :], t[c.place].centred, 0.0,
                                                 spread(t[c.place].inv, Q, F), ALU.max, ALU.mult).then_inc(k.e_out.sem, 1)
                    for c in turn.late(4):
                        dve.wait_ge(*k.e_ln.squared.at(c.n + 1))
                        order.settle(dve.tensor_reduce(t[c.place].var, t[c.place].squares, AX, ALU.add))
                        dve.tensor_scalar(var[:, c.place, :], t[c.place].var, 1.0 / F, EPS, ALU.mult, ALU.add
                                          ).then_inc(k.e_ln.varied.sem, 1)
                    order.leave_turn(turn, 4)

            @block.sync
            def _(sp):
                def fetch(c, place):
                    sp.dma_start(gap[:, place, :, :].rearrange("p n f -> p (n f)"), edge_rows(k.gap_rows, 0, c)
                                 ).then_inc(k.e_loaded[place].sem, 16)

                for place in range(RING):
                    sp.sem_inc(k.e_stored[place].sem, 16)
                    fetch(place, place)
                for turn in skewed(sp, NC, LATEST):
                    for c in turn.late(0):
                        if c.ahead:
                            sp.wait_ge(*k.weighted.at(c.n + 1))
                            fetch(c.n + RING, c.place)
                    for c in turn.late(5):
                        sp.wait_ge(*k.e_out.at(c.n + 1))
                        sp.dma_start(edge_rows(k.t2, k.NP, c.n), out[:, c.place, :, :].rearrange("p q f -> p (q f)")
                                     ).then_inc(k.e_stored[c.place].sem, 16)
                wait_ring(sp, k.e_stored, NC, 1)
    for signal in (k.weighted, k.summed, k.rows_ready, k.raised, k.projected, k.e_out):
        signal.close(NC)
    k.prepared.close(1)
    close_sums(k)
    ln_close(k.e_ln, NC)
    close_ring(k.e_loaded, NC)
    close_ring(k.e_stored, NC, 1)


def dve_average(dve, k, c, ring, rows):
    dve.wait_ge(*k.gathered[c.slot].at(c.slot_uses + 1))
    dve.tensor_tensor(rows[:].rearrange("p (q f) -> p q f", f=F), ring[:, c.slot, :, :],
                      spread(flat(k.inv_deg[:, bass.ds(c.n, 1), :]), Q, F), ALU.mult).then_inc(k.rows_ready.sem, 1)


def act_next_index(act, k, index, index_ring, c):
    act.wait_ge(*k.gathered[c.slot].at(c.slot_uses + 1))
    if c.gather_ahead:
        act_index(act, k, index, index_ring, c.n + SLOTS, c.slot).then_inc(k.index_set.sem, 1)


def layer2_first(k):
    nc, d, NC = k.nc, k.d, k.NC
    with ExitStack() as ctx:
        sb = allocator(k, ctx, "l2a")
        ring = sb("ring", [P, SLOTS, Q, F])
        index_ring = sb("index_ring", [P, SLOTS, Q], U32)
        rows = sb("rows", [P, SPAN])
        h2 = sb("h2", [P, RING, SPAN])
        kept = sb("kept", [P, RING, SPAN])
        hidden = sb("hidden", [P, RING, 2, SPAN])
        xnew = sb("xnew", [P, Q, F])
        out = sb("out", [P, RING, Q, F])
        s = SumRing(sb)
        n_h2 = sb("n_h2", [P, RING, 4 * P])
        n_x = sb("n_x", [P, RING, NODE_COLS, F])
        n_kept = sb("n_kept", [P, RING, 4 * P])
        n_hidden = sb("n_hidden", [P, RING, 2, 4 * P])
        n_out = sb("n_out", [P, RING, NODE_COLS, F])
        columns, carry = k.bank[0][:, 0:SPAN], k.bank[0][:, SPAN:SPAN + 1]
        turned, e_hidden, e_rows = k.bank[1][:, 0:SPAN], k.bank[2], k.bank[3]
        n_columns, n_hid, n_rows = k.bank[4], (k.bank[5], k.bank[6]), (k.bank[7], k.bank[6])
        LATEST = 2

        with nc.Block() as block:
            @block.gpsimd
            def _(pool):
                for c, slot, i in chunks(pool, NC, ring=SLOTS):
                    pool.wait_ge(*k.index_set.at(c + 1))
                    pool.wait_ge(*k.ring_free[slot].at(i + 1))
                    gather(pool, k, k.t2, ring, index_ring, slot)

            @block.scalar
            def _(act):
                start_ring(act, k, k.table_index, index_ring)
                for turn in skewed(act, NC, LATEST, SLOTS):
                    for c in turn.late(2):
                        act.wait_ge(*k.n_hidden.at(c.n + 1))
                        for j in range(2):
                            last = act.activation(n_hidden[:, c.place, j, :], n_hid[j][:], ACT.Relu, bias=k.b1_col)
                        last.then_inc(k.n_hidden_kept.sem, 1)
                    for c in turn.late(1):
                        act.wait_ge(*k.e_hidden.at(c.n + 1))
                        act.activation(hidden[:, c.place, :, :].rearrange("p j n -> p (j n)"), e_hidden[:], ACT.Relu,
                                       bias=k.b1_col).then_inc(k.e_hidden_kept.sem, 1)
                    for c in turn.late(0):
                        act_next_index(act, k, k.table_index, index_ring, c)
                        act.wait_ge(*k.rows_ready.at(c.n + 1))
                        act.sem_inc(k.ring_free[c.slot].sem, 1)
                    for c in turn.late(2):
                        act.wait_ge(*k.e_state.at(c.n + 1))
                        act.wait_ge(*k.e_stored[c.place].at(c.uses + 1))
                        act.activation(out[:, c.place, :, :], e_rows[:].rearrange("p (n f) -> p n f", f=2 * F)[:, :, 0:F],
                                       ACT.Copy).then_inc(k.e_out.sem, 1)
                        act.wait_ge(*k.n_read.at(c.n + 1))
                        act.wait_ge(*k.n_stored[c.place].at(c.uses + 1))
                        for part in range(2):
                            last = act.activation(n_out[:, c.place, 8 * part:8 * part + 8, :],
                                                  n_rows[part][:].rearrange("p (n f) -> p n f", f=2 * F)[:, :, 0:F], ACT.Copy)
                        last.then_inc(k.n_out2.sem, 1)
                    for c in turn.late(0):
                        act.wait_ge(*k.e_columns.at(c.n + 1))
                        act.activation(kept[:, c.place, :], turned, ACT.Copy).then_inc(k.e_columns_kept.sem, 1)
                        act.wait_ge(*k.n_columns.at(c.n + 1))
                        act.activation(n_kept[:, c.place, :], n_columns[:], ACT.Copy).then_inc(k.n_columns_kept.sem, 1)

            @block.tensor
            def _(pe):
                for turn in skewed(pe, NC, LATEST):
                    for c in turn.late(2):
                        pe.wait_ge(*k.e_hidden_kept.at(c.n + 1))
                        if not c.first:
                            pe.wait_ge(*k.e_out.at(c.n))
                        for h in range(HALVES):
                            for j in range(2):
                                last = pe.matmul(e_rows[:, (2 * h + j) * P:(2 * h + j + 1) * P],
                                                 hidden[:, c.place, j, h * P:(h + 1) * P], k.w2lr[:], start=True, stop=True)
                        last.then_inc(k.e_projected.sem, 1)
                    for c in turn.late(1):
                        pe.wait_ge(*k.e_columns_kept.at(c.n + 1))
                        pe.wait_ge(*k.scanned.at(c.n + 1))
                        for j in range(2):
                            at = slice(j * SPAN, (j + 1) * SPAN)
                            pe.matmul(e_hidden[:, at], k.w1l[:, j * P:(j + 1) * P], s.sums[:, c.place, :], start=True, stop=False)
                            last = pe.matmul(e_hidden[:, at], k.w1r[:, j * P:(j + 1) * P], kept[:, c.place, :],
                                             start=False, stop=True)
                        last.then_inc(k.e_hidden.sem, 1)
                    for c in turn.late(0):
                        pe.wait_ge(*k.rows_ready.at(c.n + 1))
                        pe_turn(pe, k, rows, columns).then_inc(k.columns_ready.sem, 1)
                    for c in turn.late(2):
                        pe.wait_ge(*k.n_hidden_kept.at(c.n + 1))
                        for part in range(4):
                            for j in range(2):
                                last = pe.matmul(n_rows[part // 2][:, (part % 2 * 2 + j) * P:(part % 2 * 2 + j + 1) * P],
                                                 n_hidden[:, c.place, j, part * P:(part + 1) * P], k.w2lr[:],
                                                 start=True, stop=True)
                        last.then_inc(k.n_projected.sem, 1)
                    for c in turn.late(0):
                        pe_carry(pe, k, s, c.n, s.last(c.place), carry)
                        pe.wait_ge(*k.e_loaded[c.place].at(c.uses + 1))
                        pe_turn(pe, k, h2[:, c.place, :], turned).then_inc(k.e_columns.sem, 1)
                        pe.wait_ge(*k.h_loaded[c.place].at(c.uses + 1))
                        if not c.first:
                            pe.wait_ge(*k.n_columns_kept.at(c.n))
                        for part in range(4):
                            last = pe.transpose(n_columns[:, part * P:(part + 1) * P],
                                                n_h2[:, c.place, part * P:(part + 1) * P], k.ident[:])
                        last.then_inc(k.n_columns.sem, 1)
                    for c in turn.late(1):
                        if not c.first:
                            pe.wait_ge(*k.n_out2.at(c.n))
                        pe.wait_ge(*k.n_columns_kept.at(c.n + 1))
                        for j in range(2):
                            last = pe.matmul(n_hid[j][:], k.w1r[:, j * P:(j + 1) * P], n_kept[:, c.place, :],
                                             start=True, stop=True)
                        last.then_inc(k.n_hidden.sem, 1)

            @block.vector
            def _(dve):
                order = k.dve
                order.enter(dve)
                order.settle(dve.memset(s.sums[:], 0.0))
                order.close()
                for turn in skewed(dve, NC, LATEST, SLOTS):
                    order.enter_turn(dve, turn, 1)
                    for c in turn.late(0):
                        dve_average(dve, k, c, ring, rows)
                    for c in turn.late(2):
                        dve.wait_ge(*k.e_projected.at(c.n + 1))
                        order.settle(dve.tensor_tensor(xnew[:], e_rows[:].rearrange("p (n f) -> p n f", f=2 * F)[:, :, F:2 * F],
                                                       k.b2[:].unsqueeze(1).to_broadcast([P, Q, F]), ALU.add))
                        state = flat(k.state[:, bass.ds(c.n, 1), :])
                        dve.tensor_tensor(state, state, xnew[:].rearrange("p q f -> p (q f)"), ALU.add
                                          ).then_inc(k.e_state.sem, 1)
                    for c in turn.late(0):
                        dve_scan_alone(dve, k, s, c.n, columns)
                    for c in turn.late(2):
                        dve.wait_ge(*k.n_loaded[c.place].at(c.uses + 1))
                        dve.wait_ge(*k.n_projected.at(c.n + 1))
                        for part in range(2):
                            at = n_x[:, c.place, 8 * part:8 * part + 8, :]
                            last = dve.tensor_tensor(at, at, n_rows[part][:].rearrange("p (n f) -> p n f", f=2 * F)[:, :, F:2 * F],
                                                     ALU.add)
                        last.then_inc(k.n_read.sem, 1)
                        dve.wait_ge(*k.n_read.at(c.n + 1))
                        dve.tensor_tensor(n_x[:, c.place, :, :], n_x[:, c.place, :, :],
                                          k.b2[:].unsqueeze(1).to_broadcast([P, NODE_COLS, F]), ALU.add).then_inc(k.n_out.sem, 1)
                    for c in turn.late(0):
                        dve_scan(dve, k, c.n, columns, carry, s.sums[:, c.place, :])
                    order.leave_turn(turn, 1)

            @block.sync
            def _(sp):
                def fetch_x(c, place):
                    sp.dma_start(n_x[:, place, :, :].rearrange("p n f -> p (n f)"), node_rows(k.xa, c, k.NP)
                                 ).then_inc(k.n_loaded[place].sem, 16)

                def fetch_h(c, place):
                    sp.dma_start(n_h2[:, place, :], node_rows(k.t2, c, k.NP)).then_inc(k.h_loaded[place].sem, 16)
                    sp.dma_start(h2[:, place, :], edge_rows(k.t2, k.NP, c)).then_inc(k.e_loaded[place].sem, 16)

                for place in range(RING):
                    sp.sem_inc(k.n_stored[place].sem, 16)
                    sp.sem_inc(k.e_stored[place].sem, 16)
                    fetch_h(place, place)
                    fetch_x(place, place)
                for turn in skewed(sp, NC, LATEST):
                    for c in turn.late(2):
                        sp.wait_ge(*k.e_out.at(c.n + 1))
                        sp.dma_start(edge_rows(k.t2b, k.NP, c.n), out[:, c.place, :, :].rearrange("p q f -> p (q f)")
                                     ).then_inc(k.e_stored[c.place].sem, 16)
                        sp.wait_ge(*k.n_out.at(c.n + 1))
                        sp.dma_start(node_rows(k.xb, c.n, k.NP), n_x[:, c.place, :, :].rearrange("p n f -> p (n f)")
                                     ).then_inc(k.x_stored[c.place].sem, 16)
                        sp.wait_ge(*k.n_out2.at(c.n + 1))
                        sp.dma_start(node_rows(k.t2b, c.n, k.NP), n_out[:, c.place, :, :].rearrange("p n f -> p (n f)")
                                     ).then_inc(k.n_stored[c.place].sem, 16)
                    for c in turn.late(0):
                        if c.ahead:
                            sp.wait_ge(*k.n_columns.at(c.n + 1))
                            fetch_h(c.n + RING, c.place)
                    for c in turn.late(2):
                        if c.ahead:
                            sp.wait_ge(*k.x_stored[c.place].at(c.uses + 1))
                            fetch_x(c.n + RING, c.place)
                wait_ring(sp, k.x_stored, NC)
                wait_ring(sp, k.n_stored, NC, 1)
                wait_ring(sp, k.e_stored, NC, 1)
    close_ring(k.gathered, NC)
    close_ring(k.ring_free, NC, 1)
    for signal in (k.index_set, k.rows_ready, k.n_columns, k.n_columns_kept, k.e_columns, k.e_columns_kept, k.n_hidden,
                   k.n_hidden_kept, k.e_hidden, k.e_hidden_kept, k.n_out, k.n_out2, k.n_read, k.e_state, k.e_out, k.n_projected,
                   k.e_projected):
        signal.close(NC)
    close_sums(k)
    close_ring(k.n_loaded, NC)
    close_ring(k.h_loaded, NC)
    close_ring(k.x_stored, NC)
    close_ring(k.n_stored, NC, 1)
    close_ring(k.e_loaded, NC)
    close_ring(k.e_stored, NC, 1)


def layer2_second(k):
    nc, d, NC = k.nc, k.d, k.NC
    with ExitStack() as ctx:
        sb = allocator(k, ctx, "l2b")
        ring = sb("ring", [P, SLOTS, Q, F])
        index_ring = sb("index_ring", [P, SLOTS, Q], U32)
        rows = sb("rows", [P, SPAN])
        x3 = sb("x3", [P, RING, Q, F])
        h3 = sb("h3", [P, RING, Q, F])
        kept = sb("kept", [P, RING, SPAN])
        out = sb("out", [P, RING, SPAN])
        s = SumRing(sb)
        te = norm_ring(sb, "lne", Q)
        n_x = sb("n_x", [P, SLOTS, NODE_COLS * F])
        n_h3 = sb("n_h3", [P, NODE_COLS, F])
        n_kept = sb("n_kept", [P, RING, 4 * P])
        n_out = sb("n_out", [P, RING, NODE_COLS * F])
        n_final = sb("n_final", [P, RING, NODE_COLS * F])
        tn = norm_ring(sb, "lnn", NODE_COLS)
        columns, carry, projected = k.bank[0][:, 0:SPAN], k.bank[0][:, SPAN:SPAN + 1], k.bank[1][:, 0:SPAN]
        turned, e_rows, n_columns, n_rows = k.bank[2][:, 0:SPAN], k.bank[3][:, 0:SPAN], k.bank[4], k.bank[5]
        n_biased = k.bank[6]
        LATEST = 3

        with nc.Block() as block:
            @block.gpsimd
            def _(pool):
                for c, slot, i in chunks(pool, NC, ring=SLOTS):
                    pool.wait_ge(*k.index_set.at(c + 1))
                    pool.wait_ge(*k.ring_free[slot].at(i + 1))
                    gather(pool, k, k.t2b, ring, index_ring, slot)

            @block.scalar
            def _(act):
                start_ring(act, k, k.table_index, index_ring)
                for turn in skewed(act, NC, LATEST, SLOTS):
                    for c in turn.late(2):
                        ln_root(act, k, k.e_ln, c.n, te[c.place])
                    for c in turn.late(1):
                        ln_root(act, k, k.n_ln, c.n, tn[c.place])
                    for c in turn.late(2):
                        act.wait_ge(*k.n_projected.at(c.n + 1))
                        act.wait_ge(*k.n_stored[c.place].at(2 * (c.uses + 1)))
                        act.activation(n_out[:, c.place, :], n_rows[:], ACT.Copy).then_inc(k.n_out.sem, 1)
                    for c in turn.late(0):
                        act_next_index(act, k, k.table_index, index_ring, c)
                        act.wait_ge(*k.rows_ready.at(c.n + 1))
                        act.sem_inc(k.ring_free[c.slot].sem, 1)
                    for c in turn.late(3):
                        act.wait_ge(*k.e_projected.at(c.n + 1))
                        act.wait_ge(*k.e_stored[c.place].at(c.uses + 1))
                        act.activation(out[:, c.place, :], e_rows, ACT.Copy).then_inc(k.e_out.sem, 1)
                    for c in turn.late(1):
                        act.wait_ge(*k.n_columns.at(c.n + 1))
                        act.activation(n_kept[:, c.place, :], n_columns[:], ACT.Copy).then_inc(k.n_columns_kept.sem, 1)
                    for c in turn.late(2):
                        act.wait_ge(*k.e_columns.at(c.n + 1))
                        act.activation(kept[:, c.place, :], turned, ACT.Copy).then_inc(k.e_columns_kept.sem, 1)
                    for c in turn.late(0):
                        ln_square(act, k, k.n_ln, c.n, tn[c.place])
                    for c in turn.late(1):
                        ln_square(act, k, k.e_ln, c.n, te[c.place])
                        act.activation(flat(k.state[:, bass.ds(c.n, 1), :]),
                                       x3[:, c.place, :, :].rearrange("p q f -> p (q f)"), ACT.Copy)

            @block.tensor
            def _(pe):
                for turn in skewed(pe, NC, LATEST):
                    for c in turn.late(2):
                        pe.wait_ge(*k.n_columns_kept.at(c.n + 1))
                        if not c.first:
                            pe.wait_ge(*k.n_out.at(c.n))
                        for part in range(4):
                            at = slice(part * P, (part + 1) * P)
                            last = pe.matmul(n_rows[:, at], n_kept[:, c.place, at], k.w3[:], start=True, stop=True)
                        last.then_inc(k.n_projected.sem, 1)
                        if not c.first:
                            pe.wait_ge(*k.n_out2.at(c.n))
                        for part in range(4):
                            at = slice(part * P, (part + 1) * P)
                            pe.matmul(n_biased[:, at], n_kept[:, c.place, at], k.w3[:], start=True, stop=False)
                            last = pe.matmul(n_biased[:, at], k.ones_row[:], k.b3_row[:], start=False, stop=True)
                        last.then_inc(k.n_hidden.sem, 1)
                    for c in turn.late(1):
                        pe.wait_ge(*k.scanned.at(c.n + 1))
                        pe_project(pe, s.sums[:, c.place, :], k.ident, projected).then_inc(k.projected.sem, 1)
                    for c in turn.late(0):
                        pe.wait_ge(*k.rows_ready.at(c.n + 1))
                        pe_turn(pe, k, rows, columns).then_inc(k.columns_ready.sem, 1)
                    for c in turn.late(3):
                        pe.wait_ge(*k.e_columns_kept.at(c.n + 1))
                        if not c.first:
                            pe.wait_ge(*k.e_out.at(c.n))
                        pe_project(pe, kept[:, c.place, :], k.w3, e_rows).then_inc(k.e_projected.sem, 1)
                    for c in turn.late(1):
                        pe.wait_ge(*k.n_rows.at(c.n + 1))
                        for part in range(4):
                            last = pe.transpose(n_columns[:, part * P:(part + 1) * P],
                                                n_h3[:].rearrange("p n f -> p (n f)")[:, part * P:(part + 1) * P], k.ident[:])
                        last.then_inc(k.n_columns.sem, 1)
                    for c in turn.late(0):
                        pe_carry(pe, k, s, c.n, s.last(c.place), carry)
                    for c in turn.late(2):
                        pe.wait_ge(*k.e_en.at(c.n + 1))
                        pe_turn(pe, k, h3[:, c.place, :, :].rearrange("p q f -> p (q f)"), turned
                                ).then_inc(k.e_columns.sem, 1)

            @block.vector
            def _(dve):
                order = k.dve
                order.enter(dve)
                order.settle(dve.memset(s.sums[:], 0.0))
                order.close()
                for turn in skewed(dve, NC, LATEST, SLOTS):
                    order.enter_turn(dve, turn, 6)
                    for c in turn.late(2):
                        dve.wait_ge(*k.e_ln.rooted.at(c.n + 1))
                        order.settle(dve.reciprocal(te[c.place].inv, te[c.place].dev))
                        order.settle(dve.tensor_tensor(te[c.place].inv, te[c.place].inv,
                                                       flat(k.inv_sqrt_deg[:, bass.ds(c.n, 1), :]), ALU.mult))
                        dve.scalar_tensor_tensor(h3[:, c.place, :, :], te[c.place].centred, 0.0,
                                                 spread(te[c.place].inv, Q, F), ALU.max, ALU.mult).then_inc(k.e_en.sem, 1)
                    for c in turn.late(0):
                        dve_average(dve, k, c, ring, rows)
                    for c in turn.late(2):
                        dve.wait_ge(*k.n_hidden.at(c.n + 1))
                        dve.wait_ge(*k.n_stored[c.place].at(2 * (c.uses + 1)))
                        dve.scalar_tensor_tensor(n_final[:, c.place, :], n_biased[:], 0.0, n_x[:, c.slot, :], ALU.max, ALU.add
                                                 ).then_inc(k.n_out2.sem, 1)
                    for c in turn.late(1):
                        ln_scale(dve, k, k.n_ln, c.n, NODE_COLS, tn[c.place], n_h3[:]).then_inc(k.n_rows.sem, 1)
                    for c in turn.late(0):
                        dve_scan_alone(dve, k, s, c.n, columns)
                        dve.wait_ge(*k.x_loaded[c.slot].at(c.slot_uses + 1))
                        ln_centre(dve, k, k.n_ln, n_x[:, c.slot, :].rearrange("p (n f) -> p n f", f=F), NODE_COLS,
                                  tn[c.place])
                    for c in turn.late(1):
                        dve.wait_ge(*k.projected.at(c.n + 1))
                        order.settle(dve.tensor_tensor(x3[:, c.place, :, :].rearrange("p q f -> p (q f)"),
                                                       flat(k.state[:, bass.ds(c.n, 1), :]), projected, ALU.add))
                        ln_centre(dve, k, k.e_ln, x3[:, c.place, :, :], Q, te[c.place])
                    for c in turn.late(0):
                        dve_scan(dve, k, c.n, columns, carry, s.sums[:, c.place, :])
                        ln_variance(dve, k, k.n_ln, c.n, tn[c.place])
                    for c in turn.late(1):
                        ln_variance(dve, k, k.e_ln, c.n, te[c.place])
                    order.leave_turn(turn, 6)

            @block.sync
            def _(sp):
                def fetch(c, slot):
                    sp.dma_start(n_x[:, slot, :], node_rows(k.xb, c, k.NP)).then_inc(k.x_loaded[slot].sem, 16)

                for place in range(RING):
                    sp.sem_inc(k.n_stored[place].sem, 32)
                    sp.sem_inc(k.e_stored[place].sem, 16)
                for slot in range(SLOTS):
                    fetch(slot, slot)
                for turn in skewed(sp, NC, LATEST, SLOTS):
                    for c in turn.late(2):
                        sp.wait_ge(*k.n_out.at(c.n + 1))
                        sp.dma_start(node_rows(k.t3, c.n, k.NP), n_out[:, c.place, :]).then_inc(k.n_stored[c.place].sem, 16)
                        sp.wait_ge(*k.n_out2.at(c.n + 1))
                        sp.dma_start(node_rows(d["out"], c.n, k.NP), n_final[:, c.place, :]
                                     ).then_inc(k.n_stored[c.place].sem, 16)
                        if c.gather_ahead:
                            fetch(c.n + SLOTS, c.slot)
                    for c in turn.late(3):
                        sp.wait_ge(*k.e_out.at(c.n + 1))
                        sp.dma_start(edge_rows(k.t3, k.NP, c.n), out[:, c.place, :]).then_inc(k.e_stored[c.place].sem, 16)
                wait_twice(sp, k.n_stored, NC, 1)
                wait_ring(sp, k.e_stored, NC, 1)
    close_ring(k.gathered, NC)
    close_ring(k.ring_free, NC, 1)
    for signal in (k.index_set, k.rows_ready, k.n_columns, k.n_columns_kept, k.e_columns, k.e_columns_kept, k.n_rows,
                   k.n_out, k.n_out2, k.n_hidden, k.e_en, k.e_out, k.n_projected, k.e_projected, k.projected):
        signal.close(NC)
    close_sums(k)
    ln_close(k.n_ln, NC)
    ln_close(k.e_ln, NC)
    for _ in range(2):
        close_ring(k.n_stored, NC, 1)
    close_ring(k.x_loaded, NC)
    close_ring(k.e_stored, NC, 1)


def layer3(k):
    nc, d, NC = k.nc, k.d, k.NC
    with ExitStack() as ctx:
        sb = allocator(k, ctx, "l3")
        ring = sb("ring", [P, SLOTS, Q, F])
        index_ring = sb("index_ring", [P, SLOTS, Q], U32)
        store_ring = sb("store_ring", [P, SLOTS, Q], U32)
        own = sb("own", [P, RING, SPAN])
        t = sb("t", [P, Q, F])
        out = sb("out", [P, SLOTS, Q, F])
        s = SumTiles(sb)
        columns, carry, projected = k.bank[0][:, 0:SPAN], k.bank[0][:, SPAN:SPAN + 1], k.bank[1][:, 0:SPAN]

        with nc.Block() as block:
            @block.gpsimd
            def _(pool):
                for turn in skewed(pool, NC, 2, SLOTS):
                    for c in turn.late(0):
                        pool.wait_ge(*k.index_set.at(c.n + 1))
                        pool.wait_ge(*k.ring_free[c.slot].at(c.slot_uses + 1))
                        gather(pool, k, k.t3, ring, index_ring, c.slot)
                    for c in turn.late(2):
                        pool.wait_ge(*k.e_out.at(c.n + 1))
                        pool.sem_inc(k.gather_started.sem, 1)
                        for q in range(Q):
                            pool.indirect_dma_start(
                                out=d["out"], out_offset=bass.IndirectOffsetOnAxis(ap=store_ring[:, c.slot, q:q + 1], axis=0),
                                in_=out[:, c.slot, q, :], in_offset=None, bounds_check=k.NP - 1, oob_is_err=False
                            ).then_inc(k.scattered[c.slot].sem, 16)
                wait_ring(pool, k.scattered, NC)

            @block.scalar
            def _(act):
                start_ring(act, k, k.table_index, index_ring)

                for turn in skewed(act, NC, 0, SLOTS):
                    for c in turn.late(0):
                        act_next_index(act, k, k.table_index, index_ring, c)
                        act.wait_ge(*k.columns_ready.at(c.n + 1))
                        act.sem_inc(k.ring_free[c.slot].sem, 1)
                        if c.slot_again:
                            act.wait_ge(*k.scattered[c.slot].at(c.slot_uses))
                        act.activation(store_ring[:, c.slot, :], flat(k.store_rows[:, bass.ds(c.n, 1), :]), ACT.Copy
                                       ).then_inc(k.e_state.sem, 1)

            @block.tensor
            def _(pe):
                for turn in skewed(pe, NC, 0, SLOTS):
                    for c in turn.late(0):
                        pe.wait_ge(*k.gathered[c.slot].at(c.slot_uses + 1))
                        pe_turn(pe, k, ring[:, c.slot, :, :].rearrange("p q f -> p (q f)"), columns
                                ).then_inc(k.columns_ready.sem, 1)
                        pe_carry(pe, k, s, c.n, s.sums[:, SPAN - 1:SPAN], carry)
                        pe.wait_ge(*k.e_loaded[c.place].at(c.uses + 1))
                        pe.wait_ge(*k.scanned.at(c.n + 1))
                        for h in range(HALVES):
                            at = slice(h * P, (h + 1) * P)
                            pe.matmul(projected[:, at], s.sums[:, at], k.ident[:], start=True, stop=False)
                            last = pe.matmul(projected[:, at], k.ident[:], own[:, c.place, at], start=False, stop=True)
                        last.then_inc(k.projected.sem, 1)

            @block.vector
            def _(dve):
                order = k.dve
                order.enter(dve)
                order.settle(dve.memset(s.sums[:], 0.0))
                order.close()
                for turn in skewed(dve, NC, 0, SLOTS):
                    order.enter_turn(dve, turn, 2)
                    for c in turn.late(0):
                        dve_scan_alone(dve, k, s, c.n, columns)
                        dve_scan(dve, k, c.n, columns, carry, s.sums[:])
                        dve.wait_ge(*k.projected.at(c.n + 1))
                        order.settle(dve.tensor_tensor(t[:], projected.rearrange("p (q f) -> p q f", f=F),
                                                       spread(flat(k.inv_sqrt_deg[:, bass.ds(c.n, 1), :]), Q, F), ALU.mult))
                        order.settle(dve.tensor_tensor(t[:], t[:], k.b3[:].unsqueeze(1).to_broadcast([P, Q, F]), ALU.add))
                        dve.wait_ge(*k.e_state.at(c.n + 1))
                        dve.scalar_tensor_tensor(out[:, c.slot, :, :].rearrange("p q f -> p (q f)"),
                                                 t[:].rearrange("p q f -> p (q f)"), 0.0,
                                                 flat(k.state[:, bass.ds(c.n, 1), :]), ALU.max, ALU.add).then_inc(k.e_out.sem, 1)
                    order.leave_turn(turn, 2)

            @block.sync
            def _(sp):
                def fetch(c, place):
                    sp.dma_start(own[:, place, :], edge_rows(k.t3, k.NP, c)).then_inc(k.e_loaded[place].sem, 16)

                for place in range(RING):
                    fetch(place, place)
                for c, place, i, ahead in chunks_ahead(sp, NC):
                    if ahead:
                        sp.wait_ge(*k.projected.at(c + 1))
                        fetch(c + RING, place)



def layout(inputs):
    x = np.asarray(inputs["x"])
    src, dst = np.asarray(inputs["src"]), np.asarray(inputs["dst"])
    gaps = np.asarray(inputs["edge_attr3_2x32"])
    nodes, edges = x.shape[0], src.shape[0]
    NC = max(-(-edges // CHUNK), -(-(nodes + 1) // (NODE_COLS * P)), 3)
    NP, EP, JN = NC * NODE_COLS * P, NC * CHUNK, NC * NODE_COLS
    a = {}
    a["x"] = np.concatenate([x, np.zeros((NP - nodes, F), x.dtype)])
    a["dst_line"] = np.concatenate([np.full(1, -1, dst.dtype), dst, np.full(EP - edges, nodes, dst.dtype),
                                    np.full(1, -2, dst.dtype)])
    a["src_line"] = np.concatenate([src, np.zeros(EP - edges, src.dtype)])
    gaps = np.concatenate([gaps.reshape(edges, 2 * F), np.zeros((EP - edges, 2 * F), gaps.dtype)])
    a["edge_attr"] = np.ascontiguousarray(
        gaps.reshape(NC, GROUPS, HALVES, P, 2 * F).transpose(0, 3, 2, 1, 4).reshape(EP, 2 * F))
    w = {name: np.asarray(value) for name, value in inputs.items() if name.startswith("L")}

    def blocks(weight, times):
        rows, cols = weight.shape
        out = np.zeros((times * rows, times * cols), weight.dtype)
        for n in range(times):
            out[n * rows:(n + 1) * rows, n * cols:(n + 1) * cols] = weight
        return out

    for name in ("L0_gnn_W", "L1_gnn_W1", "L1_gnn_W2s", "L1_gnn_W2d", "L2_gnn_W1_l", "L2_gnn_W1_r"):
        a[name] = blocks(w[name], GROUPS)
    a["L3_gnn_W_turned"] = blocks(w["L3_gnn_W"].T, GROUPS)
    a["L2_gnn_W2_lr"] = blocks(np.concatenate([w["L2_gnn_W2_l"], w["L2_gnn_W2_r"]], axis=1), 2)
    heads = np.zeros((2 * F, 2), w["L1_gnn_attn"].dtype)
    for h in range(2):
        heads[h * F:(h + 1) * F, h] = w["L1_gnn_attn"][0, h]
    a["L1_gnn_attn"] = blocks(heads, 2)
    a["bias_columns"] = np.stack([np.tile(w["L2_gnn_b1"], 2), np.tile(w["L1_gnn_b2s"], 2), np.tile(w["L1_gnn_b2d"], 2)],
                                 axis=1)
    a["L1_gnn_b1_row"] = np.tile(w["L1_gnn_b1"], GROUPS)[None, :]
    a["L1_gnn_b2s_row"] = np.tile(w["L1_gnn_b2s"], GROUPS)[None, :]
    a["L3_gnn_bias_row"] = np.tile(w["L3_gnn_bias"], GROUPS)[None, :]
    a["L3_gnn_bias"], a["L2_gnn_b2"] = w["L3_gnn_bias"], w["L2_gnn_b2"]
    f, g = np.arange(P) % F, np.arange(P) // F
    same_f = f[:, None] == f[None, :]
    a["identity"] = np.eye(P, dtype=np.float32)
    a["carry_patterns"] = np.stack([same_f & (g[:, None] < g[None, :]), same_f & (g[:, None] == GROUPS - 1),
                                    same_f & (g[:, None] > g[None, :]), same_f & (g[:, None] == 0)],
                                   axis=1).astype(np.float32)
    a["below"] = (np.arange(P)[:, None] < np.arange(P)[None, :]).astype(np.float32)
    a["above"] = (np.arange(P)[:, None] > np.arange(P)[None, :]).astype(np.float32)
    pick = np.zeros((P, GROUPS, P), np.float32)
    for group in range(GROUPS):
        pick[F * group, group, :] = 1.0
    a["pick_group"] = pick
    assert JN <= 2048
    a["count_up"] = np.arange(max(JN, P), dtype=np.float16)
    a["edge_number"] = np.arange(EP, dtype=np.float32)
    a["edge_number_rows"] = np.ascontiguousarray(
        a["edge_number"].reshape(NC, GROUPS, HALVES, P).transpose(3, 0, 2, 1).reshape(P, NC * Q))
    a["node_number"] = np.arange(NP, dtype=np.float32).reshape(P, JN)
    return a, NC, nodes


def kernel(**inputs):
    import concourse.bacc as _bacc
    from concourse.bass_utils import run_bass_kernel_spmd as _run

    arrays, NC, nodes = layout(inputs)
    nc = _bacc.Bacc("TRN2", target_bir_lowering=False, num_devices=1)
    d = {name: nc.dram_tensor(name, a.shape, mybir.dt.from_np(a.dtype), kind="ExternalInput").ap()
         for name, a in arrays.items()}
    d["out"] = nc.dram_tensor("out", (NC * NODE_COLS * P, F), F32, kind="ExternalOutput").ap()
    build(nc, d, NC)
    result = _run(nc, [arrays], core_ids=[0])
    return result.results[0]["out"][:nodes]
```
